# Optimizing a Trainium2 kernel written in Bass

```python
import numpy as np
import jax
import jax.numpy as jnp

def _softmax(x, axis=-1):
    return jax.nn.softmax(x, axis=axis)

def _gelu(x):
    return jax.nn.gelu(x, approximate=True)

def _silu(x):
    return jax.nn.silu(x)

def _sigmoid(x):
    return jax.nn.sigmoid(x)

def _layernorm(x, axis=-1, eps=1e-05):
    m = jnp.mean(x, axis=axis, keepdims=True)
    v = jnp.var(x, axis=axis, keepdims=True)
    return (x - m) / jnp.sqrt(v + eps)

def _scatter_add(tgt, idx, src, axis=0):
    return tgt.at[idx].add(src)

def _segment_sum(src, seg, n):
    return jax.ops.segment_sum(src, seg, n)
kernel_name = 'mk_gnn_ffn_d1_gnn_r8_52ea1b'

def setup_inputs(seed: int=0):
    np.random.seed(seed)
    _w = jnp.asarray

    def _rec_inputs():
        import jax
        import jax.numpy as jnp
        _gk = jax.random.key(seed)
        x = -0.0005207 + 1.001 * jax.random.normal(jax.random.fold_in(_gk, 1), (6250, 256), jnp.float32)
        src = jax.random.randint(jax.random.fold_in(_gk, 2), (100000,), 0, 6250, jnp.int32)
        dst = jnp.minimum((6250 * jax.random.uniform(jax.random.fold_in(_gk, 3), (100000,)) ** 2.0).astype(jnp.int32), 49999)
        _o = jnp.argsort(dst, stable=True)
        src = src[_o]
        dst = dst[_o]
        edge_weight = jax.random.uniform(jax.random.fold_in(_gk, 12), (100000,), jnp.float32, 0.0, 0.999998)
        node_vec = jax.random.uniform(jax.random.fold_in(_gk, 13), (6250,), jnp.float32, 0.0, 0.999833)
        return (x, src, dst, edge_weight, node_vec)
    x, src, dst, edge_weight, node_vec = _rec_inputs()

    def _L0_gnn_setup():
        import jax, jax.numpy as jnp
        import numpy as np
        from jax import lax
        N, E, D = (1024, 32768, 256)
        NH, FOUT = (4, 64)
        D_STATE, D_CONV, DT_RANK = (16, 4, 16)

        def _layer_norm(x, g, b, eps=1e-05):
            mu = jnp.mean(x, -1, keepdims=True)
            var = jnp.var(x, -1, keepdims=True)
            return (x - mu) * lax.rsqrt(var + eps) * g + b

        def _mamba(xs, in_proj_w, conv_w, conv_b, x_proj_w, dt_proj_w, dt_proj_b, A_log, D_param, out_proj_w):
            n = xs.shape[0]
            xz = xs @ in_proj_w.T
            xc, z = jnp.split(xz, 2, axis=-1)
            K = conv_w.shape[1]
            xp = jnp.pad(xc, ((K - 1, 0), (0, 0)))
            xc = sum((xp[k:k + n] * conv_w[:, k] for k in range(K))) + conv_b
            xc = jax.nn.silu(xc)
            dbc = xc @ x_proj_w.T
            dt = jax.nn.softplus(dbc[:, :DT_RANK] @ dt_proj_w.T + dt_proj_b)
            Bm = dbc[:, DT_RANK:DT_RANK + D_STATE]
            Cm = dbc[:, DT_RANK + D_STATE:]
            A = -jnp.exp(A_log)
            dA = jnp.exp(dt[:, :, None] * A)
            dBx = (dt * xc)[:, :, None] * Bm[:, None, :]

            def step(h, t):
                dA_t, dBx_t, C_t = t
                h = dA_t * h + dBx_t
                return (h, h @ C_t)
            _, y = lax.scan(step, jnp.zeros((xc.shape[1], D_STATE), xs.dtype), (dA, dBx, Cm))
            y = y + xc * D_param
            y = y * jax.nn.silu(z)
            return y @ out_proj_w.T

        def _forward(x, edge_index, deg_noise, gat_w, gat_a_src, gat_a_tgt, gat_b, ln_local_g, ln_local_b, ln_global_g, ln_global_b, ln2_g, ln2_b, in_proj_w, conv_w, conv_b, x_proj_w, dt_proj_w, dt_proj_b, A_log, D_param, out_proj_w, wl, wg, ff1_w, ff1_b, ff2_w, ff2_b):
            n = x.shape[0]
            src, tgt = (edge_index[0], edge_index[1])
            proj = (x @ gat_w.T).reshape(n, NH, FOUT)
            s_src = jnp.sum(proj * gat_a_src, -1)
            s_tgt = jnp.sum(proj * gat_a_tgt, -1)
            e = jax.nn.leaky_relu(s_src[src] + s_tgt[tgt], 0.2)
            exp_e = jnp.exp(e - jnp.max(e))
            denom = jax.ops.segment_sum(exp_e, tgt, num_segments=n)
            attn = exp_e / (denom[tgt] + 1e-16)
            agg = jax.ops.segment_sum(proj[src] * attn[:, :, None], tgt, num_segments=n)
            h_local = jax.nn.elu((agg + x.reshape(n, NH, FOUT)).reshape(n, NH * FOUT) + gat_b)
            h_local = _layer_norm(h_local, ln_local_g, ln_local_b)
            deg = jax.ops.segment_sum(jnp.ones((src.shape[0],), x.dtype), src, num_segments=n)
            perm = jnp.argsort(deg + deg_noise, stable=True)
            inv = jnp.argsort(perm)
            y = _mamba(x[perm], in_proj_w, conv_w, conv_b, x_proj_w, dt_proj_w, dt_proj_b, A_log, D_param, out_proj_w)
            h_attn = _layer_norm(x + y[inv], ln_global_g, ln_global_b)
            gate = jax.nn.sigmoid(h_local @ wl.T + h_attn @ wg.T)
            h = gate * h_local + (1.0 - gate) * h_attn
            ff = jax.nn.relu(h @ ff1_w.T + ff1_b) @ ff2_w.T + ff2_b
            return _layer_norm(h + ff, ln2_g, ln2_b)
        key = jax.random.key(seed)
        ks = jax.random.split(key, 24)
        w = lambda i, shape, s=0.05: jax.random.normal(ks[i], shape, dtype=jnp.float32) * s
        return {'x': jax.random.normal(ks[0], (N, D), dtype=jnp.float32), 'edge_index': jax.random.randint(ks[1], (2, E), 0, N, dtype=jnp.int32), 'edge_prob': jax.random.uniform(ks[2], (E,), dtype=jnp.float32), 'deg_noise': jax.random.uniform(ks[3], (N,), dtype=jnp.float32), 'gat_w': w(4, (NH * FOUT, D)), 'gat_a_src': w(5, (NH, FOUT)), 'gat_a_tgt': w(6, (NH, FOUT)), 'gat_b': jnp.zeros((NH * FOUT,), jnp.float32), 'ln_local_g': jnp.ones((D,), jnp.float32), 'ln_local_b': jnp.zeros((D,), jnp.float32), 'ln_global_g': jnp.ones((D,), jnp.float32), 'ln_global_b': jnp.zeros((D,), jnp.float32), 'ln2_g': jnp.ones((D,), jnp.float32), 'ln2_b': jnp.zeros((D,), jnp.float32), 'in_proj_w': w(7, (2 * D, D)), 'conv_w': w(8, (D, D_CONV), 0.2), 'conv_b': jnp.zeros((D,), jnp.float32), 'x_proj_w': w(9, (DT_RANK + 2 * D_STATE, D)), 'dt_proj_w': w(10, (D, DT_RANK)), 'dt_proj_b': w(11, (D,), 0.1) - 4.0, 'A_log': jnp.log(jnp.tile(jnp.arange(1, D_STATE + 1, dtype=jnp.float32), (D, 1))), 'D_param': jnp.ones((D,), jnp.float32), 'out_proj_w': w(12, (D, D)), 'wl': w(13, (D, D)), 'wg': w(14, (D, D)), 'ff1_w': w(15, (2 * D, D)), 'ff1_b': jnp.zeros((2 * D,), jnp.float32), 'ff2_w': w(16, (D, 2 * D)), 'ff2_b': jnp.zeros((D,), jnp.float32)}
    _L0_gnn_all = _L0_gnn_setup()
    _L0_gnn_in = {k: v for k, v in _L0_gnn_all.items() if k in ('gat_w', 'gat_a_src', 'gat_a_tgt', 'gat_b', 'ln_local_g', 'ln_local_b', 'ln_global_g', 'ln_global_b', 'ln2_g', 'ln2_b', 'in_proj_w', 'conv_w', 'conv_b', 'x_proj_w', 'dt_proj_w', 'dt_proj_b', 'A_log', 'D_param', 'out_proj_w', 'wl', 'wg', 'ff1_w', 'ff1_b', 'ff2_w', 'ff2_b')}
    del _L0_gnn_all

    def _L0_ffn_setup():
        import jax, jax.numpy as jnp
        import numpy as np
        B, S, H, F, E, K = (8, 512, 256, 512, 16, 2)
        EPS = 1e-05
        key = jax.random.key(seed)
        ks = jax.random.split(key, 9)
        sc = 0.02
        return {'x': jax.random.normal(ks[0], (B, S, H), dtype=jnp.float32), 'gate_w': jax.random.normal(ks[1], (H, E), dtype=jnp.float32) * sc, 'gate_b': jnp.zeros((E,), dtype=jnp.float32), 'w1': jax.random.normal(ks[2], (E, H, F), dtype=jnp.float32) * sc, 'b1': jnp.zeros((E, F), dtype=jnp.float32), 'w2': jax.random.normal(ks[3], (E, F, H), dtype=jnp.float32) * sc, 'b2': jnp.zeros((E, H), dtype=jnp.float32), 'gamma': jnp.ones((H,), dtype=jnp.float32), 'beta': jnp.zeros((H,), dtype=jnp.float32)}
    _L0_ffn_all = _L0_ffn_setup()
    _L0_ffn_in = {k: v for k, v in _L0_ffn_all.items() if k in ('gate_w', 'gate_b', 'w1', 'b1', 'w2', 'b2', 'gamma', 'beta')}
    del _L0_ffn_all
    return {'x': x, 'src': src, 'dst': dst, 'edge_weight': edge_weight, 'node_vec': node_vec, 'L0_gnn_gat_w': _L0_gnn_in['gat_w'], 'L0_gnn_gat_a_src': _L0_gnn_in['gat_a_src'], 'L0_gnn_gat_a_tgt': _L0_gnn_in['gat_a_tgt'], 'L0_gnn_gat_b': _L0_gnn_in['gat_b'], 'L0_gnn_ln_local_g': _L0_gnn_in['ln_local_g'], 'L0_gnn_ln_local_b': _L0_gnn_in['ln_local_b'], 'L0_gnn_ln_global_g': _L0_gnn_in['ln_global_g'], 'L0_gnn_ln_global_b': _L0_gnn_in['ln_global_b'], 'L0_gnn_ln2_g': _L0_gnn_in['ln2_g'], 'L0_gnn_ln2_b': _L0_gnn_in['ln2_b'], 'L0_gnn_in_proj_w': _L0_gnn_in['in_proj_w'], 'L0_gnn_conv_w': _L0_gnn_in['conv_w'], 'L0_gnn_conv_b': _L0_gnn_in['conv_b'], 'L0_gnn_x_proj_w': _L0_gnn_in['x_proj_w'], 'L0_gnn_dt_proj_w': _L0_gnn_in['dt_proj_w'], 'L0_gnn_dt_proj_b': _L0_gnn_in['dt_proj_b'], 'L0_gnn_A_log': _L0_gnn_in['A_log'], 'L0_gnn_D_param': _L0_gnn_in['D_param'], 'L0_gnn_out_proj_w': _L0_gnn_in['out_proj_w'], 'L0_gnn_wl': _L0_gnn_in['wl'], 'L0_gnn_wg': _L0_gnn_in['wg'], 'L0_gnn_ff1_w': _L0_gnn_in['ff1_w'], 'L0_gnn_ff1_b': _L0_gnn_in['ff1_b'], 'L0_gnn_ff2_w': _L0_gnn_in['ff2_w'], 'L0_gnn_ff2_b': _L0_gnn_in['ff2_b'], 'L0_ffn_gate_w': _L0_ffn_in['gate_w'], 'L0_ffn_gate_b': _L0_ffn_in['gate_b'], 'L0_ffn_w1': _L0_ffn_in['w1'], 'L0_ffn_b1': _L0_ffn_in['b1'], 'L0_ffn_w2': _L0_ffn_in['w2'], 'L0_ffn_b2': _L0_ffn_in['b2'], 'L0_ffn_gamma': _L0_ffn_in['gamma'], 'L0_ffn_beta': _L0_ffn_in['beta']}

def reference(x, src, dst, edge_weight, node_vec, L0_gnn_gat_w, L0_gnn_gat_a_src, L0_gnn_gat_a_tgt, L0_gnn_gat_b, L0_gnn_ln_local_g, L0_gnn_ln_local_b, L0_gnn_ln_global_g, L0_gnn_ln_global_b, L0_gnn_ln2_g, L0_gnn_ln2_b, L0_gnn_in_proj_w, L0_gnn_conv_w, L0_gnn_conv_b, L0_gnn_x_proj_w, L0_gnn_dt_proj_w, L0_gnn_dt_proj_b, L0_gnn_A_log, L0_gnn_D_param, L0_gnn_out_proj_w, L0_gnn_wl, L0_gnn_wg, L0_gnn_ff1_w, L0_gnn_ff1_b, L0_gnn_ff2_w, L0_gnn_ff2_b, L0_ffn_gate_w, L0_ffn_gate_b, L0_ffn_w1, L0_ffn_b1, L0_ffn_w2, L0_ffn_b2, L0_ffn_gamma, L0_ffn_beta):
    import jax
    import jax.numpy as jnp

    def _L0_gnn_ref(x, edge_index, edge_prob, deg_noise, gat_w, gat_a_src, gat_a_tgt, gat_b, ln_local_g, ln_local_b, ln_global_g, ln_global_b, ln2_g, ln2_b, in_proj_w, conv_w, conv_b, x_proj_w, dt_proj_w, dt_proj_b, A_log, D_param, out_proj_w, wl, wg, ff1_w, ff1_b, ff2_w, ff2_b):
        import jax, jax.numpy as jnp
        import numpy as np
        from jax import lax
        N, E, D = (1024, 32768, 256)
        NH, FOUT = (4, 64)
        D_STATE, D_CONV, DT_RANK = (16, 4, 16)

        def _layer_norm(x, g, b, eps=1e-05):
            mu = jnp.mean(x, -1, keepdims=True)
            var = jnp.var(x, -1, keepdims=True)
            return (x - mu) * lax.rsqrt(var + eps) * g + b

        def _mamba(xs, in_proj_w, conv_w, conv_b, x_proj_w, dt_proj_w, dt_proj_b, A_log, D_param, out_proj_w):
            n = xs.shape[0]
            xz = xs @ in_proj_w.T
            xc, z = jnp.split(xz, 2, axis=-1)
            K = conv_w.shape[1]
            xp = jnp.pad(xc, ((K - 1, 0), (0, 0)))
            xc = sum((xp[k:k + n] * conv_w[:, k] for k in range(K))) + conv_b
            xc = jax.nn.silu(xc)
            dbc = xc @ x_proj_w.T
            dt = jax.nn.softplus(dbc[:, :DT_RANK] @ dt_proj_w.T + dt_proj_b)
            Bm = dbc[:, DT_RANK:DT_RANK + D_STATE]
            Cm = dbc[:, DT_RANK + D_STATE:]
            A = -jnp.exp(A_log)
            dA = jnp.exp(dt[:, :, None] * A)
            dBx = (dt * xc)[:, :, None] * Bm[:, None, :]

            def step(h, t):
                dA_t, dBx_t, C_t = t
                h = dA_t * h + dBx_t
                return (h, h @ C_t)
            _, y = lax.scan(step, jnp.zeros((xc.shape[1], D_STATE), xs.dtype), (dA, dBx, Cm))
            y = y + xc * D_param
            y = y * jax.nn.silu(z)
            return y @ out_proj_w.T

        def _forward(x, edge_index, deg_noise, gat_w, gat_a_src, gat_a_tgt, gat_b, ln_local_g, ln_local_b, ln_global_g, ln_global_b, ln2_g, ln2_b, in_proj_w, conv_w, conv_b, x_proj_w, dt_proj_w, dt_proj_b, A_log, D_param, out_proj_w, wl, wg, ff1_w, ff1_b, ff2_w, ff2_b):
            n = x.shape[0]
            src, tgt = (edge_index[0], edge_index[1])
            proj = (x @ gat_w.T).reshape(n, NH, FOUT)
            s_src = jnp.sum(proj * gat_a_src, -1)
            s_tgt = jnp.sum(proj * gat_a_tgt, -1)
            e = jax.nn.leaky_relu(s_src[src] + s_tgt[tgt], 0.2)
            exp_e = jnp.exp(e - jnp.max(e))
            denom = jax.ops.segment_sum(exp_e, tgt, num_segments=n)
            attn = exp_e / (denom[tgt] + 1e-16)
            agg = jax.ops.segment_sum(proj[src] * attn[:, :, None], tgt, num_segments=n)
            h_local = jax.nn.elu((agg + x.reshape(n, NH, FOUT)).reshape(n, NH * FOUT) + gat_b)
            h_local = _layer_norm(h_local, ln_local_g, ln_local_b)
            deg = jax.ops.segment_sum(jnp.ones((src.shape[0],), x.dtype), src, num_segments=n)
            perm = jnp.argsort(deg + deg_noise, stable=True)
            inv = jnp.argsort(perm)
            y = _mamba(x[perm], in_proj_w, conv_w, conv_b, x_proj_w, dt_proj_w, dt_proj_b, A_log, D_param, out_proj_w)
            h_attn = _layer_norm(x + y[inv], ln_global_g, ln_global_b)
            gate = jax.nn.sigmoid(h_local @ wl.T + h_attn @ wg.T)
            h = gate * h_local + (1.0 - gate) * h_attn
            ff = jax.nn.relu(h @ ff1_w.T + ff1_b) @ ff2_w.T + ff2_b
            return _layer_norm(h + ff, ln2_g, ln2_b)
        return _forward(x, edge_index, deg_noise, gat_w, gat_a_src, gat_a_tgt, gat_b, ln_local_g, ln_local_b, ln_global_g, ln_global_b, ln2_g, ln2_b, in_proj_w, conv_w, conv_b, x_proj_w, dt_proj_w, dt_proj_b, A_log, D_param, out_proj_w, wl, wg, ff1_w, ff1_b, ff2_w, ff2_b)

    def _L0_ffn_ref(x, gate_w, gate_b, w1, b1, w2, b2, gamma, beta):
        import jax, jax.numpy as jnp
        import numpy as np
        B, S, H, F, E, K = (8, 512, 256, 512, 16, 2)
        EPS = 1e-05
        gate_logits = x @ gate_w + gate_b
        topk_vals, topk_idx = jax.lax.top_k(gate_logits, K)
        topk_w = jax.nn.softmax(topk_vals, axis=-1)
        h = jax.nn.relu(jnp.einsum('bsh,ehf->bsef', x, w1) + b1)
        expert_out = jnp.einsum('bsef,efh->bseh', h, w2) + b2
        sel = jnp.take_along_axis(expert_out, topk_idx[:, :, :, None], axis=2)
        moe = jnp.sum(topk_w[..., None] * sel, axis=2)
        y = x + moe
        mu = jnp.mean(y, axis=-1, keepdims=True)
        var = jnp.var(y, axis=-1, keepdims=True)
        return (y - mu) / jnp.sqrt(var + EPS) * gamma + beta
    edge_index = jnp.stack([src, dst])
    x = x + _L0_gnn_ref(_layernorm(x, axis=-1), edge_index, edge_weight, node_vec, L0_gnn_gat_w, L0_gnn_gat_a_src, L0_gnn_gat_a_tgt, L0_gnn_gat_b, L0_gnn_ln_local_g, L0_gnn_ln_local_b, L0_gnn_ln_global_g, L0_gnn_ln_global_b, L0_gnn_ln2_g, L0_gnn_ln2_b, L0_gnn_in_proj_w, L0_gnn_conv_w, L0_gnn_conv_b, L0_gnn_x_proj_w, L0_gnn_dt_proj_w, L0_gnn_dt_proj_b, L0_gnn_A_log, L0_gnn_D_param, L0_gnn_out_proj_w, L0_gnn_wl, L0_gnn_wg, L0_gnn_ff1_w, L0_gnn_ff1_b, L0_gnn_ff2_w, L0_gnn_ff2_b)
    x = x + _L0_ffn_ref(_layernorm(x, axis=-1)[None], L0_ffn_gate_w, L0_ffn_gate_b, L0_ffn_w1, L0_ffn_b1, L0_ffn_w2, L0_ffn_b2, L0_ffn_gamma, L0_ffn_beta)[0]
    return x

_drawn_inputs = setup_inputs


def setup_inputs(seed=0):
    import zlib

    import numpy as np

    out = dict(_drawn_inputs(seed))
    spreads = {'L0_gnn_gat_b': (0.0, 0.1),
     'L0_gnn_ln_local_g': (1.0, 0.2),
     'L0_gnn_ln_local_b': (0.0, 0.1),
     'L0_gnn_ln_global_g': (1.0, 0.2),
     'L0_gnn_ln_global_b': (0.0, 0.1),
     'L0_gnn_ln2_g': (1.0, 0.2),
     'L0_gnn_ln2_b': (0.0, 0.1),
     'L0_gnn_conv_b': (0.0, 0.8),
     'L0_gnn_D_param': (1.0, 0.6),
     'L0_gnn_ff1_b': (0.0, 0.1),
     'L0_gnn_ff2_b': (0.0, 0.1),
     'L0_ffn_gate_b': (0.0, 0.34),
     'L0_ffn_b1': (0.0, 0.8),
     'L0_ffn_b2': (0.0, 0.317),
     'L0_ffn_gamma': (1.0, 0.2),
     'L0_ffn_beta': (0.0, 0.1)}
    factors = {'node_vec': 3.455,
     'L0_gnn_gat_a_src': 2.979,
     'L0_gnn_gat_a_tgt': 8.0,
     'L0_gnn_in_proj_w': 2.841,
     'L0_gnn_conv_w': 3.088,
     'L0_gnn_x_proj_w': 8.0,
     'L0_gnn_dt_proj_w': 8.0,
     'L0_gnn_dt_proj_b': 8.0,
     'L0_gnn_A_log': 8.0,
     'L0_gnn_out_proj_w': 2.846}
    for name, (base, spread) in spreads.items():
        noise = np.random.default_rng([zlib.crc32(name.encode()), seed]).standard_normal(out[name].shape)
        drawn = base * np.exp(spread * noise) if base else spread * noise
        out[name] = jnp.asarray(drawn.astype(out[name].dtype))
    for name, factor in factors.items():
        out[name] = (out[name] * factor).astype(out[name].dtype)
    return out
```

```python
from contextlib import ExitStack

import concourse.bass as bass
from concourse import mybir

P = 128
F32 = mybir.dt.float32
BF16 = mybir.dt.bfloat16
I32 = mybir.dt.int32
ALU = mybir.AluOpType
ACT = mybir.ActivationFunctionType
AX = mybir.AxisListType

N, E, D = 6250, 100000, 256
NT = -(-N // P)
NP = NT * P
NLAST = N - (NT - 1) * P
GRP = 7
NG = NT // GRP
ET = 784
EP = ET * P
HEADS, FOUT = 4, 64
ROW = D + HEADS
NS, NR = 16, 16
TC = 448
NCH = NP // TC
TB = 112
NB = TC // TB
EX, FF = 16, 512
MT = (2 * NP + EX * (P - 1)) // P
MT += MT % 2
LN_EPS = 1e-5
DEN_EPS = 1e-16
FAR = 1.0e6
HUGE = 3.0e38
assert NT % GRP == 0 and NP % TC == 0 and ET >= -(-E // P) and ET % (NCH * 8) == 0


class Chain:

    def __init__(self, eng, sem):
        self.eng, self.sem, self.n = eng, sem, 0

    def mark(self, ins):
        ins.then_inc(self.sem, 1)
        self.n += 1

    def wait(self):
        self.eng.wait_ge(self.sem, self.n)

    def step(self, ins):
        self.mark(ins)
        self.wait()

    def restart(self):
        if self.n:
            self.eng.wait_ge(self.sem, self.n)
            self.eng.sem_inc(self.sem, -self.n)
        self.n = 0


class Phase:

    used = []

    def __init__(self, nc, tag, ctx):
        self.nc, self.tag, self.ctx = nc, tag, ctx

    def sb(self, name, shape, dt=F32):
        return self.ctx.enter_context(self.nc.sbuf_tensor(f"{self.tag}_{name}", shape, dt))

    def ps(self, name, shape, dt=F32):
        return self.ctx.enter_context(self.nc.psum_tensor(f"{self.tag}_{name}", shape, dt))

    def sem(self, name):
        s = self.nc.alloc_semaphore(name=f"{self.tag}_{name}")
        self.used.append(s)
        return s

    def sems(self, names):
        return [self.sem(n) for n in names.split()]

    def block(self):
        return self.ctx.enter_context(self.nc.Block())


def clear_semaphores(nc):
    nc.clear_and_free_semaphores(Phase.used)
    Phase.used = []
    nc.all_engine_barrier()


def rows(ap, p=P):
    return ap.rearrange("(t p) d -> p t d", p=p)


def spread(ap, n, parts=P):
    return bass.AP(ap.tensor, ap.offset, [[0, parts], [1, n]])


def inverse_deviation(pool, ch, K, rstd, var):
    ch.step(pool.tensor_scalar(rstd, var, LN_EPS, None, ALU.add))
    ch.step(pool.tensor_tensor(rstd, rstd, K.nhalf[:, 0:rstd.shape[1]], ALU.pow))


def constants(nc, A, K):
    with ExitStack() as ctx:
        ph = Phase(nc, "cst", ctx)
        made, = ph.sems("made")
        block = ph.block()

        @block.gpsimd
        def _(pool):
            ch = Chain(pool, made)
            ch.mark(pool.memset(K.ident[:, :], 0.0))
            ch.mark(pool.memset(K.upper[:, :], 1.0))
            ch.mark(pool.memset(K.ones[:, :], 1.0))
            ch.mark(pool.memset(K.nhalf[:, :], -0.5))
            ch.wait()
            ch.mark(pool.affine_select(out=K.ident[:, :], in_=K.ident[:, :], compare_op=ALU.not_equal, fill=1.0,
                                  base=0, pattern=[[-1, P]], channel_multiplier=1))
            ch.mark(pool.affine_select(out=K.upper[:, :], in_=K.upper[:, :], compare_op=ALU.is_gt, fill=0.0,
                                  base=0, pattern=[[1, P]], channel_multiplier=-1))
            ch.mark(pool.iota(K.iota_i[:, :], pattern=[[1, P]], base=0, channel_multiplier=0))
            ch.mark(pool.iota(K.node_i[:, :], pattern=[[P, NT]], base=0, channel_multiplier=1))
            ch.wait()
            ch.mark(pool.tensor_copy(K.iota[:, :], K.iota_i[:, :]))
            ch.mark(pool.tensor_copy(K.node[:, :], K.node_i[:, :]))
            ch.restart()


def project(nc, A, K):
    with ExitStack() as ctx:
        ph = Phase(nc, "prj", ctx)
        xin = ph.sb("xin", [P, GRP, D])
        xn = ph.sb("xn", [P, GRP, D])
        st = ph.sb("st", [P, GRP, 6])
        mv = ph.sb("mv", [P, GRP, 2])
        rstd = ph.sb("rstd", [P, GRP])
        xT = ph.sb("xT", [P, 2, 2, P])
        pj = ph.sb("pj", [P, GRP, D + 8])
        gat = ph.sb("gat", [P, 2, D])
        w = ph.sb("w", [P, 2, D + 8])
        adiag = ph.sb("adiag", [P, 2, 8])
        tp = [ph.ps(f"tp{i}", [P, 2, P]) for i in range(2)]
        pp = [ph.ps(f"pp{i}", [P, 512]) for i in range(2)]
        wl, wz, wf, wr = ph.sems("wl wz wf wr")
        xl, xfree, st_r, rs_r, xn_pe, xn_sp = ph.sems("xl xfree st_r rs_r xn_pe xn_sp")
        tp_r, xT_r, pp_r, pp_free, pj_r, xn_w, pj_w, pad, padded, stgt = ph.sems("tp_r xT_r pp_r pp_free pj_r xn_w pj_w pad padded stgt")
        dch, ach, pch = ph.sems("dch ach pch")
        block = ph.block()

        @block.sync
        def _(sp):
            sp.dma_start(gat[:, :, :], A["gat_w"].rearrange("(c p) d -> p c d", p=P)).then_inc(wl, 16)
            sp.dma_start(w[:, :, 0:D], A["gat_wT"].rearrange("(c p) f -> p c f", p=P)).then_inc(wl, 16)
            sp.wait_ge(wz, 1)
            for a, off in ((A["a_src"], 0), (A["a_tgt"], HEADS)):
                for h in range(HEADS):
                    q = (h % 2) * FOUT
                    sp.dma_start(adiag[q:q + FOUT, h // 2, off + h:off + h + 1],
                                 a[h:h + 1, :].rearrange("a f -> f a")).then_inc(wl, 16)
            with sp.Fori(0, NG) as i:
                sp.wait_ge(xfree, 1)
                sp.sem_inc(xfree, -1)
                sp.dma_start(xin[:, :, :], rows(A["x"])[:, bass.ds(i * GRP, GRP), :]).then_inc(xl, 16)
                sp.wait_ge(xn_sp, 1)
                sp.sem_inc(xn_sp, -1)
                sp.dma_start(rows(A["xn_d"])[:, bass.ds(i * GRP, GRP), :], xn[:, :, :]).then_inc(xn_w, 16)
                sp.wait_ge(pj_r, GRP)
                sp.sem_inc(pj_r, -GRP)
                sp.dma_start(rows(A["table"])[:, bass.ds(i * GRP, GRP), :], pj[:, :, 0:ROW]).then_inc(pj_w, 16)
            sp.wait_ge(padded, 1)
            sp.dma_start(rows(A["stgt_d"]), K.s_all[:, :, HEADS:2 * HEADS]).then_inc(stgt, 16)
            sp.wait_ge(stgt, 16)
            sp.wait_ge(xn_w, 16)
            sp.wait_ge(pj_w, 16)

        @block.vector
        def _(dve):
            ch = Chain(dve, dch)
            dve.memset(adiag[:, :, :], 0.0).then_inc(wz, 1)
            dve.sem_inc(xfree, 1)
            dve.sem_inc(xn_w, 16)
            with dve.Fori(0, NG) as i:
                dve.wait_ge(xl, 16)
                dve.sem_inc(xl, -16)
                for k in range(GRP):
                    ch.mark(dve.bn_stats(st[:, k, :], xin[:, k, :]))
                ch.wait()
                for k in range(GRP):
                    ch.mark(dve.bn_aggr(mv[:, k, :], st[:, k, :]))
                ch.wait()
                dve.sem_inc(st_r, 1)
                dve.wait_ge(rs_r, 1)
                dve.sem_inc(rs_r, -1)
                dve.wait_ge(xn_w, 16)
                dve.sem_inc(xn_w, -16)
                for k in range(GRP):
                    ch.step(dve.tensor_scalar(xn[:, k, :], xin[:, k, :], mv[:, k, 0:1], rstd[:, k:k + 1],
                                              ALU.subtract, ALU.mult))
                    dve.sem_inc(xn_pe, 1)
                dve.sem_inc(xn_sp, 1)
                dve.sem_inc(xfree, 1)
                ch.restart()

        @block.gpsimd
        def _(pool):
            ch = Chain(pool, pch)
            with pool.Fori(0, NG) as i:
                pool.wait_ge(st_r, 1)
                pool.sem_inc(st_r, -1)
                inverse_deviation(pool, ch, K, rstd[:, :], mv[:, :, 1])
                pool.sem_inc(rs_r, 1)
                ch.restart()
            pool.wait_ge(pad, 1)
            ch.step(pool.affine_select(out=K.s_all[:, NT - 1, HEADS:2 * HEADS], in_=K.s_all[:, NT - 1, HEADS:2 * HEADS],
                                       compare_op=ALU.is_ge, fill=-1.0e30, base=NLAST - 1,
                                       pattern=[[0, HEADS]], channel_multiplier=-1))
            pool.sem_inc(padded, 1)
            ch.restart()

        @block.tensor
        def _(pe):
            pe.wait_ge(wl, 16 * (2 + 2 * HEADS))
            for m in range(2):
                for c in range(2):
                    mm = pe.matmul(pp[0][:, m * 8:m * 8 + 8], gat[:, c, m * P:(m + 1) * P], adiag[:, c, :],
                                   start=(c == 0), stop=(c == 1))
            mm.then_inc(wf, 1)
            pe.wait_ge(wr, 1)
            pe.sem_inc(pp_free, 2)
            with pe.Fori(0, NG) as i:
                def turn(k):
                    pe.wait_ge(xn_pe, k + 1)
                    for c in range(2):
                        t = pe.transpose(tp[k % 2][:, c, :], xn[:, k, c * P:(c + 1) * P], K.ident[:, :])
                    t.then_inc(tp_r, 1)

                turn(0)
                for k in range(GRP):
                    if k + 1 < GRP:
                        turn(k + 1)
                    pe.wait_ge(xT_r, k + 1)
                    pe.wait_ge(pp_free, 1)
                    pe.sem_inc(pp_free, -1)
                    for c in range(2):
                        mm = pe.matmul(pp[k % 2][:, 0:D + 8], xT[:, k % 2, c, :], w[:, c, :], start=(c == 0), stop=(c == 1))
                    mm.then_inc(pp_r, 1)
                pe.sem_inc(xn_pe, -GRP)
                pe.sem_inc(xT_r, -GRP)

        @block.scalar
        def _(act):
            ch = Chain(act, ach)
            act.wait_ge(wf, 1)
            act.activation(w[:, :, D:D + 8], pp[0][:, 0:16].rearrange("p (m e) -> p m e", m=2), ACT.Copy).then_inc(wr, 1)
            act.sem_inc(pj_w, 16)
            with act.Fori(0, NG) as i:
                act.wait_ge(pj_w, 16)
                act.sem_inc(pj_w, -16)

                def copy(k):
                    act.wait_ge(tp_r, k + 1)
                    act.activation(xT[:, k % 2, :, :], tp[k % 2][:, :, :], ACT.Copy).then_inc(xT_r, 1)

                copy(0)
                for k in range(GRP):
                    act.wait_ge(pp_r, k + 1)
                    ch.mark(act.activation(K.s_all[:, bass.ds(i * GRP + k, 1), :],
                                      pp[k % 2][:, D:D + 8].rearrange("p (a e) -> p a e", a=1), ACT.Copy))
                    ch.step(act.activation(pj[:, k, :], pp[k % 2][:, 0:D + 8], ACT.Copy))
                    act.sem_inc(pj_r, 1)
                    act.sem_inc(pp_free, 1)
                    if k + 1 < GRP:
                        copy(k + 1)
                act.sem_inc(tp_r, -GRP)
                act.sem_inc(pp_r, -GRP)
                ch.restart()
            act.sem_inc(pad, 1)


def locate(nc, A, K):
    with ExitStack() as ctx:
        ph = Phase(nc, "loc", ctx)
        fr_i = ph.sb("fr_i", [P, ET], I32)
        fr = ph.sb("fr", [P, ET])
        junk = ph.sb("junk", [P, ET])
        below = ph.sb("below", [P, NT])
        same = ph.sb("same", [P, NT])
        at = ph.sb("at", [P, NT])
        at_i = ph.sb("at_i", [P, NT], I32)
        b2 = ph.sb("b2", [P, NT])
        s2 = ph.sb("s2", [P, NT])
        rw_i = ph.sb("rw_i", [P, NT, P], I32)
        rw = ph.sb("rw", [P, NT, P])
        cm = ph.sb("cm", [P, NT, P])
        zero = ph.sb("zero", [P, ET * HEADS])
        far = ph.sb("far", [P, NT])
        far_i = ph.sb("far_i", [P, NT], I32)
        fw, fl, at_r, got, dch, zr, vz, far_r, vs = ph.sems("fw fl at_r got dch zr vz far_r vs")
        block = ph.block()

        @block.sync
        def _(sp):
            sp.dma_start(A["first_d"], bass.AP(A["dst"].tensor, 0, [[P, ET]]),
                         allow_slow_non_contiguous=True).then_inc(fw, 16)
            sp.wait_ge(fw, 16)
            sp.dma_start(fr_i[:, :], spread(A["first_d"], ET)).then_inc(fl, 16)
            sp.wait_ge(zr, 1)
            sp.dma_start(A["v_d"].rearrange("(p c) h -> p (c h)", p=P), zero[:, :]).then_inc(vz, 16)
            sp.wait_ge(vz, 16)

        @block.vector
        def _(dve):
            ch = Chain(dve, dch)
            dve.memset(zero[:, :], 0.0).then_inc(zr, 1)
            dve.wait_ge(fl, 16)
            ch.step(dve.tensor_copy(fr[:, :], fr_i[:, :]))
            with dve.Fori(0, NG) as i:
                for k in range(GRP):
                    b = bass.ds(i * GRP + k, 1)
                    dve.tensor_scalar(junk[:, :], fr[:, :], K.node[:, b], None, ALU.is_lt, ALU.add,
                                      accum_out=below[:, b]).then_inc(at_r, 1)
                    dve.wait_ge(at_r, 2 * k + 1)
                    dve.tensor_scalar(junk[:, :], fr[:, :], K.node[:, b], None, ALU.is_equal, ALU.add,
                                      accum_out=same[:, b]).then_inc(at_r, 1)
                    dve.wait_ge(at_r, 2 * k + 2)
                dve.sem_inc(at_r, -2 * GRP)
            ch.step(dve.tensor_scalar(at[:, :], below[:, :], -1.0, 0.0, ALU.add, ALU.max))
            ch.step(dve.tensor_copy(at_i[:, :], at[:, :]))
            dve.sem_inc(far_r, 1)
            dve.wait_ge(got, 16 * NT)
            ch.step(dve.tensor_copy(rw[:, :, :], rw_i[:, :, :]))
            nb = K.node[:, :].unsqueeze(2).to_broadcast([P, NT, P])
            ch.step(dve.tensor_tensor(cm[:, :, :], rw[:, :, :], nb, ALU.is_lt))
            ch.step(dve.tensor_reduce(b2[:, :], cm[:, :, :], AX.X, ALU.add))
            ch.step(dve.tensor_tensor(cm[:, :, :], rw[:, :, :], nb, ALU.is_equal))
            ch.step(dve.tensor_reduce(s2[:, :], cm[:, :, :], AX.X, ALU.add))
            ch.step(dve.scalar_tensor_tensor(out=b2[:, :], in0=at[:, :], scalar=float(P), in1=b2[:, :],
                                             op0=ALU.mult, op1=ALU.add))
            ch.step(dve.tensor_tensor(s2[:, :], s2[:, :], same[:, :], ALU.add))
            ch.step(dve.tensor_scalar(K.some[:, :], s2[:, :], 0.0, None, ALU.is_gt))
            ch.step(dve.tensor_scalar(far[:, :], K.some[:, :], -FAR, FAR, ALU.mult, ALU.add))
            ch.step(dve.tensor_tensor(far[:, :], far[:, :], b2[:, :], ALU.add))
            ch.step(dve.tensor_copy(far_i[:, :], far[:, :]))
            ch.step(dve.tensor_scalar(b2[:, :], b2[:, :], float(EP - 1), None, ALU.min))
            ch.step(dve.tensor_copy(K.start[:, :], b2[:, :]))
            dve.sem_inc(far_r, 1)
            ch.restart()

        @block.gpsimd
        def _(pool):
            pool.wait_ge(far_r, 1)
            for b in range(NT):
                pool.indirect_dma_start(rw_i[:, b, :], None, A["dst"].rearrange("(t q) -> t q", q=P),
                                        bass.IndirectOffsetOnAxis(at_i[:, b:b + 1], 0)).then_inc(got, 16)
            pool.wait_ge(far_r, 2)
            pool.wait_ge(vz, 16)
            for b in range(NT):
                pool.indirect_dma_start(A["v_d"], bass.IndirectOffsetOnAxis(far_i[:, b:b + 1], 0),
                                        K.s_all[:, b, HEADS:2 * HEADS], None,
                                        bounds_check=EP - 1, oob_is_err=False).then_inc(vs, 16)
            pool.wait_ge(vs, 16 * NT)


def order(nc, A, K):
    G = 8
    with ExitStack() as ctx:
        ph = Phase(nc, "ord", ctx)
        src_i = ph.sb("src_i", [P, ET], I32)
        part = ph.sb("part", [P, ET], I32)
        lo = ph.sb("lo", [P, ET])
        hi = ph.sb("hi", [P, ET])
        iota_b = ph.sb("iota_b", [P, P], BF16)
        ones_b = ph.sb("ones_b", [P, P], BF16)
        zero_b = ph.sb("zero_b", [P, P], BF16)
        ohl = ph.sb("ohl", [P, 2, G, P], BF16)
        ohh = ph.sb("ohh", [P, 2, G, NT], BF16)
        noise = ph.sb("noise", [P, NT])
        key = ph.sb("key", [P, 2, NT])
        sgn = ph.sb("sgn", [P, NT])
        sgn_i = ph.sb("sgn_i", [P, NT], I32)
        keyT = ph.sb("keyT", [NT, 2, P])
        low = ph.sb("low", [P, P])
        krow = ph.sb("krow", [P, NP])
        rrow = ph.sb("rrow", [P, NP])
        more = ph.sb("more", [P, 2, NP], BF16)
        tie = ph.sb("tie", [P, P], BF16)
        rk = ph.sb("rk", [P, 4, TC], I32)
        xn = ph.sb("xn", [P, NT, D])
        deg = ph.ps("deg", [P, 512])
        kt = ph.ps("kt", [P, 512])
        rp = ph.ps("rp", [P, 4, 512])
        ld, nl, xl, dch, ach = ph.sems("ld nl xl dch ach")
        oh_r, oh_f, deg_r, key_r, pad_r, kp_r, kt_r, kts, kw, kl = ph.sems("oh_r oh_f deg_r key_r pad_r kp_r kt_r kts kw kl")
        m_r, m_f, rp_r, rk_r, rw, rl, sc = ph.sems("m_r m_f rp_r rk_r rw rl sc")
        block = ph.block()

        @block.sync
        def _(sp):
            sp.dma_start(src_i[:, :], A["src"].rearrange("(p c) -> p c", p=P)).then_inc(ld, 16)
            sp.dma_start(noise[:, :], A["noise"]).then_inc(nl, 16)
            sp.dma_start(xn[:, :, :], rows(A["xn_d"])).then_inc(xl, 16)
            sp.wait_ge(kts, 1)
            sp.dma_start(A["keys_d"].rearrange("r (b f) -> b r f", f=P), keyT[:, :, :]).then_inc(kw, 16)
            sp.wait_ge(kw, 16)
            sp.dma_start(krow[:, :], spread(A["keys_d"], NP)).then_inc(kl, 16)
            sp.dma_start(rrow[:, :], bass.AP(A["keys_d"].tensor, NP, [[0, P], [1, NP]])).then_inc(kl, 16)
            sp.wait_ge(rk_r, 1)
            for q in range(4):
                n = min(4, NCH - 4 * q)
                sp.dma_start(A["rank_d"][4 * q * TC:(4 * q + n) * TC].rearrange("(a b f) -> a b f", a=1, f=TC),
                             rk[32 * q:32 * q + 1, 0:n, :]).then_inc(rw, 16)
            sp.wait_ge(rw, 64)
            sp.dma_start(K.rank[:, :], A["rank_d"].rearrange("(b p) -> p b", p=P),
                         allow_slow_non_contiguous=True).then_inc(rl, 16)

        @block.vector
        def _(dve):
            ch = Chain(dve, dch)
            ch.mark(dve.tensor_copy(iota_b[:, :], K.iota[:, :]))
            ch.mark(dve.memset(ones_b[:, :], 1.0))
            ch.mark(dve.memset(zero_b[:, :], 0.0))
            ch.mark(dve.tensor_scalar(low[:, :], K.upper[:, :], -1.0, 1.0, ALU.mult, ALU.add))
            dve.wait_ge(ld, 16)
            ch.mark(dve.tensor_scalar(part[:, :], src_i[:, :], P - 1, None, ALU.bitwise_and))
            ch.wait()
            ch.step(dve.tensor_copy(lo[:, :], part[:, :]))
            ch.step(dve.tensor_scalar(part[:, :], src_i[:, :], 7, None, ALU.logical_shift_right))
            ch.step(dve.tensor_copy(hi[:, :], part[:, :]))
            ch.restart()
            dve.sem_inc(oh_f, 2)
            with dve.Fori(0, ET // (2 * G)) as i:
                for s in range(2):
                    dve.wait_ge(oh_f, 1)
                    dve.sem_inc(oh_f, -1)
                    cols = bass.ds(i * 2 * G + s * G, G)
                    ch.mark(dve.tensor_tensor(ohh[:, s, :, :], iota_b[:, 0:NT].unsqueeze(1).to_broadcast([P, G, NT]),
                                         hi[:, cols].unsqueeze(2).to_broadcast([P, G, NT]), ALU.is_equal))
                    for g in range(G):
                        ch.mark(dve.tensor_scalar(ohl[:, s, g, :], iota_b[:, :], lo[:, bass.ds(i * 2 * G + s * G + g, 1)],
                                             None, ALU.is_equal))
                    ch.wait()
                    dve.sem_inc(oh_r, 1)
                ch.restart()
            dve.wait_ge(deg_r, 1)
            dve.wait_ge(nl, 16)
            ch.step(dve.tensor_tensor(key[:, 0, :], deg[:, 0:NT], noise[:, :], ALU.add))
            dve.sem_inc(key_r, 1)
            dve.wait_ge(pad_r, 1)
            ch.step(dve.tensor_scalar(sgn[:, :], key[:, 0, :], 0.0, 2.0, ALU.is_ge, ALU.mult))
            ch.step(dve.tensor_scalar(sgn_i[:, :], sgn[:, :], -1.0, None, ALU.add))
            ch.step(dve.tensor_tensor(key[:, 1, :].bitcast(I32), key[:, 0, :].bitcast(I32), sgn_i[:, :], ALU.add))
            ch.step(dve.tensor_scalar(sgn[:, :], key[:, 0, :], 0.0, 2.0 ** -126, ALU.is_equal, ALU.mult))
            ch.step(dve.tensor_tensor(key[:, 1, :], key[:, 1, :], sgn[:, :], ALU.add))
            dve.sem_inc(kp_r, 1)
            dve.wait_ge(kt_r, 1)
            ch.step(dve.tensor_copy(keyT[:, :, :], kt[0:NT, 0:2 * P].rearrange("b (r f) -> b r f", r=2)))
            dve.sem_inc(kts, 1)
            ch.restart()
            dve.wait_ge(kl, 32)
            dve.sem_inc(m_f, 2)

            def compare(j, s):
                blk = bass.ds(j * P, P)
                kj = key[:, 0, bass.ds(j, 1)]
                dve.wait_ge(m_f, 1)
                dve.sem_inc(m_f, -1)
                ch.mark(dve.tensor_scalar(more[:, s, :], rrow[:, :], kj, None, ALU.is_gt))
                ch.mark(dve.scalar_tensor_tensor(out=tie[:, :], in0=krow[:, blk], scalar=kj, in1=low[:, :],
                                            op0=ALU.is_equal, op1=ALU.mult))
                ch.wait()
                ch.mark(dve.tensor_tensor(more[:, s, blk], more[:, s, blk], tie[:, :], ALU.subtract))
                ch.mark(dve.tensor_copy(rrow[:, blk], krow[:, blk]))
                ch.wait()
                dve.sem_inc(m_r, 1)

            compare(0, 0)
            ch.restart()
            with dve.Fori(0, (NT - 1) // 2) as i:
                compare(i * 2 + 1, 1)
                compare(i * 2 + 2, 0)
                ch.restart()

        @block.gpsimd
        def _(pool):
            pool.wait_ge(key_r, 1)
            pool.affine_select(out=key[:, 0, NT - 1:NT], in_=key[:, 0, NT - 1:NT], compare_op=ALU.is_ge, fill=HUGE,
                               base=NLAST - 1, pattern=[[0, 1]], channel_multiplier=-1).then_inc(pad_r, 1)
            pool.wait_ge(rl, 16)
            pool.wait_ge(xl, 16)
            for b in range(NT):
                pool.indirect_dma_start(A["xs_d"], bass.IndirectOffsetOnAxis(K.rank[:, b:b + 1], 0),
                                        xn[:, b, :], None).then_inc(sc, 16)
            pool.wait_ge(sc, 16 * NT)

        @block.tensor
        def _(pe):
            pe.wait_ge(oh_r, 1)
            pe.matmul(deg[:, 0:NT], zero_b[:, :], zero_b[:, 0:NT], start=True, stop=False, skip_group_check=True)
            with pe.Fori(0, ET // (2 * G)) as i:
                for s in range(2):
                    pe.wait_ge(oh_r, 1)
                    pe.sem_inc(oh_r, -1)
                    for g in range(G):
                        mm = pe.matmul(deg[:, 0:NT], ohl[:, s, g, :], ohh[:, s, g, :], start=False, stop=False,
                                       skip_group_check=True)
                    mm.then_inc(oh_f, 1)
            pe.matmul(deg[:, 0:NT], zero_b[:, :], zero_b[:, 0:NT], start=False, stop=True,
                      skip_group_check=True).then_inc(deg_r, 1)
            pe.wait_ge(kp_r, 1)
            for r in range(2):
                mm = pe.transpose(kt[0:NT, r * P:(r + 1) * P], key[:, r, :], K.ident[:, :])
            mm.then_inc(kt_r, 1)

            def count(s, first=False, last=False):
                pe.wait_ge(m_r, 1)
                pe.sem_inc(m_r, -1)
                for c in range(NCH):
                    q = c // 4
                    mm = pe.matmul(rp[32 * q:32 * q + 1, c % 4, 0:TC], ones_b[:, 0:1],
                                   more[:, s, c * TC:(c + 1) * TC], start=first, stop=last, skip_group_check=True)
                mm.then_inc(m_f, 1)

            count(0, first=True)
            with pe.Fori(0, (NT - 1) // 2) as i:
                count(1)
                count(0)
            pe.drain().then_inc(rp_r, 1)

        @block.scalar
        def _(act):
            ch = Chain(act, ach)
            act.wait_ge(rp_r, 1)
            for q in range(4):
                n = min(4, NCH - 4 * q)
                ch.mark(act.activation(rk[32 * q:32 * q + 1, 0:n, :], rp[32 * q:32 * q + 1, 0:n, 0:TC], ACT.Copy))
            ch.wait()
            act.sem_inc(rk_r, 1)
            ch.restart()


def spread_scores(nc, A, K):
    with ExitStack() as ctx:
        ph = Phase(nc, "spr", ctx)
        dst = ph.sb("dst", [P, ET], I32)
        prev = ph.sb("prev", [P, ET], I32)
        keep = ph.sb("keep", [P, ET])
        v = ph.sb("v", [P, ET, HEADS])
        tc = ph.sb("tc", [P, ET, 2 * HEADS])
        tmp = ph.sb("tmp", [P, ET])
        mx = ph.sb("mx", [P, HEADS])
        dl, vl, hd, mx_r, top_r, tc_r, tw, dch = ph.sems("dl vl hd mx_r top_r tc_r tw dch")
        block = ph.block()

        @block.sync
        def _(sp):
            sp.dma_start(dst[:, :], A["dst"].rearrange("(p c) -> p c", p=P)).then_inc(dl, 16)
            sp.dma_start(prev[:, :], A["dprev"].rearrange("(p c) -> p c", p=P)).then_inc(dl, 16)
            sp.dma_start(v[:, :, :], A["v_d"].rearrange("(p c) h -> p c h", p=P)).then_inc(vl, 16)
            sp.wait_ge(tc_r, 1)
            sp.dma_start(A["tc_d"].rearrange("(p c) h -> p c h", p=P), tc[:, :, :]).then_inc(tw, 16)
            sp.wait_ge(tw, 16)

        @block.gpsimd
        def _(pool):
            pool.wait_ge(mx_r, 1)
            pool.partition_all_reduce(K.top_src[:, :], mx[:, :], P, bass.bass_isa.ReduceOp.max).then_inc(top_r, 1)
            pool.wait_ge(dl, 32)
            pool.wait_ge(vl, 16)
            pool.indirect_dma_start(v[:, 0, :], None, A["stgt_d"],
                                    bass.IndirectOffsetOnAxis(dst[:, 0:1], 0)).then_inc(hd, 16)

        @block.vector
        def _(dve):
            ch = Chain(dve, dch)
            ch.step(dve.tensor_reduce(mx[:, :], K.s_all[:, :, 0:HEADS].rearrange("p t h -> p h t"), AX.X, ALU.max))
            dve.sem_inc(mx_r, 1)
            dve.wait_ge(dl, 32)
            ch.step(dve.tensor_tensor(keep[:, :], dst[:, :], prev[:, :], ALU.is_equal))
            ch.step(dve.memset(keep[:, 0:1], 0.0))
            dve.wait_ge(hd, 16)
            for h in range(HEADS):
                ch.mark(dve.tensor_tensor_scan(tc[:, :, h], keep[:, :], v[:, :, h], 0.0, ALU.mult, ALU.add))
            ch.wait()
            dve.wait_ge(top_r, 1)
            for h in range(HEADS):
                ch.step(dve.tensor_scalar(tmp[:, :], tc[:, :, h], K.top_src[:, h:h + 1], None, ALU.add))
                ch.step(dve.scalar_tensor_tensor(out=tc[:, :, HEADS + h], in0=tmp[:, :], scalar=0.2, in1=tmp[:, :],
                                                 op0=ALU.mult, op1=ALU.max))
            dve.sem_inc(tc_r, 1)
            ch.restart()


def halves(ap):
    return ap.rearrange("(h p) -> p h", p=P)


def mamba_in(nc, A, K):
    with ExitStack() as ctx:
        ph = Phase(nc, "min", ctx)
        inw = ph.sb("inw", [P, 2, 2 * D])
        xpw = ph.sb("xpw", [P, 2, 48])
        dtw = ph.sb("dtw", [NR, D])
        cw = ph.sb("cw", [P, 2, 4])
        vec = ph.sb("vec", [P, 3, 2, 1])
        xs = ph.sb("xs", [TB, NB, D])
        xsT = ph.sb("xsT", [P, 2, TC])
        xcb = ph.sb("xcb", [P, 2, 3 + TC])
        cv = ph.sb("cv", [P, 2, TC])
        xcs = ph.sb("xcs", [P, 2, TC])
        dbc = ph.sb("dbc", [48, TC])
        ab = ph.sb("ab", [P, 2, TC])
        ex = ph.sb("ex", [P, 2, TC])
        lg = ph.sb("lg", [P, 2, TC])
        pl = ph.sb("pl", [P, 2, TC])
        rl = ph.sb("rl", [P, 2, TC])
        small = ph.sb("small", [P, 2, TC], I32)
        dtu = ph.sb("dtu", [P, 4, TC])
        szq = ph.sb("szq", [P, 4, TC])
        xt = ph.ps("xt", [P, 2, 512])
        ip = ph.ps("ip", [P, 2, 512])
        dp = ph.ps("dp", [P, 2, 512])
        db = ph.ps("db", [P, 512])
        wl, xl, xs_f, xt_r, xT_r, ip_r, ip_f, xcb_f, xc_r, sz_r = ph.sems("wl xl xs_f xt_r xT_r ip_r ip_f xcb_f xc_r sz_r")
        cv_r, xcs_pe, xcs_v, db_r, dbs_pe, dbs_sp, dt_r, dp_f = ph.sems("cv_r xcs_pe xcs_v db_r dbs_pe dbs_sp dt_r dp_f")
        ex_r, ln_r, pl_r, dtu_r, szq_r, dbc_w, dtu_w, szq_w = ph.sems("ex_r ln_r pl_r dtu_r szq_r dbc_w dtu_w szq_w")
        dch, ach, pch = ph.sems("dch ach pch")
        block = ph.block()

        def take(eng, sem, n=1):
            eng.wait_ge(sem, n)
            eng.sem_inc(sem, -n)

        @block.sync
        def _(sp):
            sp.dma_start(inw[:, :, :], A["in_wT"].rearrange("(c p) f -> p c f", p=P)).then_inc(wl, 16)
            sp.dma_start(xpw[:, :, :], A["xp_wT"].rearrange("(c p) f -> p c f", p=P)).then_inc(wl, 16)
            sp.dma_start(dtw[:, :], A["dt_wT"]).then_inc(wl, 16)
            sp.dma_start(cw[:, :, :], A["conv_w"].rearrange("(h p) k -> p h k", p=P)).then_inc(wl, 16)
            for j, v in enumerate((A["conv_b"], A["dt_b"], A["Dp"])):
                sp.dma_start(vec[:, j, :, 0], halves(v), allow_slow_non_contiguous=True).then_inc(wl, 16)
            with sp.Fori(0, NCH) as i:
                take(sp, xs_f)
                sp.dma_start(xs[:, :, :], rows(A["xs_d"], TB)[:, bass.ds(i * NB, NB), :]).then_inc(xl, 16)
                take(sp, dbs_sp)
                sp.dma_start(A["dbc_d"][:, bass.ds(i * TC, TC)], dbc[:, :]).then_inc(dbc_w, 16)
                take(sp, dtu_r)
                sp.dma_start(A["dtu_d"][:, bass.ds(i, 1), :, :].rearrange("p a b t -> p (a b) t"), dtu[:, :, :])\
                    .then_inc(dtu_w, 16)
                sp.dma_start(A["szq_d"][:, bass.ds(i, 1), :, :].rearrange("p a b t -> p (a b) t"), szq[:, :, :])\
                    .then_inc(szq_w, 16)
            for s in (dbc_w, dtu_w, szq_w):
                sp.wait_ge(s, 16)

        @block.tensor
        def _(pe):
            pe.wait_ge(wl, 16 * 7)
            pe.sem_inc(ip_f, 1)
            pe.sem_inc(dp_f, 1)
            with pe.Fori(0, NCH) as i:
                take(pe, xl, 16)
                for c in range(2):
                    for j in range(NB):
                        t = pe.transpose(xt[:, c, j * TB:(j + 1) * TB], xs[:, j, c * P:(c + 1) * P], K.ident[0:TB, 0:TB])
                t.then_inc(xt_r, 1)
                take(pe, xT_r)
                for z in range(2):
                    take(pe, ip_f)
                    for h in range(2):
                        for c in range(2):
                            mm = pe.matmul(ip[:, h, 0:TC], inw[:, c, (2 * z + h) * P:(2 * z + h + 1) * P], xsT[:, c, :],
                                           start=(c == 0), stop=(c == 1))
                    mm.then_inc(ip_r, 1)
                take(pe, xcs_pe)
                for c in range(2):
                    mm = pe.matmul(db[0:48, 0:TC], xpw[:, c, :], xcs[:, c, :], start=(c == 0), stop=(c == 1))
                mm.then_inc(db_r, 1)
                take(pe, dbs_pe)
                take(pe, dp_f)
                for h in range(2):
                    mm = pe.matmul(dp[:, h, 0:TC], dtw[:, h * P:(h + 1) * P], dbc[0:NR, :], start=True, stop=True)
                mm.then_inc(dt_r, 1)

        @block.scalar
        def _(act):
            ch = Chain(act, ach)
            act.wait_ge(wl, 16 * 7)
            act.sem_inc(xs_f, 1)
            act.sem_inc(dbc_w, 16)
            act.sem_inc(szq_w, 16)
            with act.Fori(0, NCH) as i:
                take(act, xt_r)
                ch.step(act.activation(xsT[:, :, :], xt[:, :, 0:TC], ACT.Copy))
                act.sem_inc(xT_r, 1)
                act.sem_inc(xs_f, 1)
                take(act, ip_r)
                take(act, xcb_f)
                ch.step(act.activation(xcb[:, :, 3:3 + TC], ip[:, :, 0:TC], ACT.Copy))
                act.sem_inc(xc_r, 1)
                act.sem_inc(ip_f, 1)
                take(act, ip_r)
                take(act, szq_w, 16)
                ch.step(act.activation(szq[:, 0:2, :], ip[:, :, 0:TC], ACT.Silu))
                act.sem_inc(sz_r, 1)
                act.sem_inc(ip_f, 1)
                take(act, cv_r)
                ch.step(act.activation(xcs[:, :, :], cv[:, :, :], ACT.Silu))
                act.sem_inc(xcs_pe, 1)
                act.sem_inc(xcs_v, 1)
                take(act, db_r)
                take(act, dbc_w, 16)
                ch.step(act.activation(dbc[:, :], db[0:48, 0:TC], ACT.Copy))
                act.sem_inc(dbs_pe, 1)
                act.sem_inc(dbs_sp, 1)
                take(act, dt_r)
                for h in range(2):
                    ch.mark(act.activation(ab[:, h, :], dp[:, h, 0:TC], ACT.Abs, bias=vec[:, 1, h, :]))
                ch.wait()
                ch.step(act.activation(ex[:, :, :], ab[:, :, :], ACT.Exp, scale=-1.0))
                act.sem_inc(ex_r, 1)
                ch.step(act.activation(lg[:, :, :], ex[:, :, :], ACT.Ln, bias=1.0))
                act.sem_inc(ln_r, 1)
                ch.restart()

        @block.gpsimd
        def _(pool):
            ch = Chain(pool, pch)
            with pool.Fori(0, NCH) as i:
                take(pool, ex_r)
                ch.step(pool.tensor_scalar(pl[:, :, :], ex[:, :, :], 1.0 / 3.0, -0.5, ALU.mult, ALU.add))
                ch.step(pool.tensor_tensor(pl[:, :, :], pl[:, :, :], ex[:, :, :], ALU.mult))
                pool.sem_inc(pl_r, 1)
                ch.restart()

        @block.vector
        def _(dve):
            ch = Chain(dve, dch)
            dve.wait_ge(wl, 16 * 7)
            ch.step(dve.memset(xcb[:, :, 0:3], 0.0))
            ch.restart()
            dve.sem_inc(xcb_f, 1)
            dve.sem_inc(dtu_w, 16)
            with dve.Fori(0, NCH) as i:
                take(dve, xc_r)
                for h in range(2):
                    ch.mark(dve.tensor_scalar(cv[:, h, :], xcb[:, h, 0:TC], cw[:, h, 0:1], vec[:, 0, h, :], ALU.mult, ALU.add))
                ch.wait()
                for k in range(1, 4):
                    for h in range(2):
                        ch.mark(dve.scalar_tensor_tensor(out=cv[:, h, :], in0=xcb[:, h, k:k + TC], scalar=cw[:, h, k:k + 1],
                                                    in1=cv[:, h, :], op0=ALU.mult, op1=ALU.add))
                    ch.wait()
                dve.sem_inc(cv_r, 1)
                ch.step(dve.tensor_copy(xcb[:, :, 0:3], xcb[:, :, TC:TC + 3]))
                dve.sem_inc(xcb_f, 1)
                take(dve, ln_r)
                for h in range(2):
                    ch.mark(dve.tensor_scalar(rl[:, h, :], dp[:, h, 0:TC], vec[:, 1, h, :], 0.0, ALU.add, ALU.max))
                ch.wait()
                dve.sem_inc(dp_f, 1)
                take(dve, pl_r)
                ch.mark(dve.tensor_scalar(small[:, :, :], ex[:, :, :], 2.0 ** -6, None, ALU.is_lt))
                ch.mark(dve.scalar_tensor_tensor(out=pl[:, :, :], in0=pl[:, :, :], scalar=1.0, in1=ex[:, :, :],
                                            op0=ALU.add, op1=ALU.mult))
                ch.wait()
                ch.step(dve.copy_predicated(lg[:, :, :], small[:, :, :], pl[:, :, :]))
                take(dve, dtu_w, 16)
                ch.step(dve.tensor_tensor(dtu[:, 0:2, :], rl[:, :, :], lg[:, :, :], ALU.add))
                take(dve, xcs_v)
                ch.mark(dve.tensor_tensor(dtu[:, 2:4, :], dtu[:, 0:2, :], xcs[:, :, :], ALU.mult))
                take(dve, sz_r)
                for h in range(2):
                    ch.mark(dve.scalar_tensor_tensor(out=szq[:, 2 + h, :], in0=xcs[:, h, :], scalar=vec[:, 2, h, :],
                                                in1=szq[:, h, :], op0=ALU.mult, op1=ALU.mult))
                ch.wait()
                dve.sem_inc(dtu_r, 1)
                ch.restart()


class Counted:

    def __init__(self, eng):
        self.eng, self.seen = eng, {}

    def wait(self, sem, n=1):
        self.seen[sem.name] = (sem, self.seen.get(sem.name, (sem, 0))[1] + n)
        self.eng.wait_ge(sem, self.seen[sem.name][1])

    def turn(self):
        for sem, n in self.seen.values():
            self.eng.sem_inc(sem, -n)
        self.seen = {}


def edges_and_scan(nc, A, K):
    GPC = 8
    RING = 4
    assert ET == NCH * GPC * GRP and NS == 2 * GPC
    first_tiles = 4
    with ExitStack() as ctx:
        ph = Phase(nc, "run", ctx)
        idx = ph.sb("idx", [P, ET], I32)
        tgt_i = ph.sb("tgt_i", [P, ET], I32)
        tgt = ph.sb("tgt", [P, ET])
        ids = ph.sb("ids", [P, GPC, GRP], I32)
        pay = ph.sb("pay", [P, RING, GRP, ROW])
        tc = ph.sb("tc", [P, 2, GRP, 2 * HEADS])
        trow = ph.sb("trow", [P, 2, GRP * P], I32)
        z = ph.sb("z", [P, GRP, HEADS])
        emax = ph.sb("emax", [P, GRP, HEADS])
        em1 = ph.sb("em1", [P, 1])
        wexp = ph.sb("wexp", [P, 2, GRP, HEADS])
        mask = ph.sb("mask", [P, 2, GRP, P])
        ob = ph.sb("ob", [P, 2, GRP, ROW])
        a_log = ph.sb("a_log", [P, 2, NS])
        a_pos = ph.sb("a_pos", [P, 2, NS])
        a_neg = ph.sb("a_neg", [P, 2, NS])
        wo = ph.sb("wo", [P, 2, D])
        dt = ph.sb("dt", [P, 2, TC])
        u = ph.sb("u", [P, 2, TC])
        dbc = ph.sb("dbc", [48, TC])
        szq = ph.sb("szq", [P, 4, TC])
        da = ph.sb("da", [P, 4, TC])
        dbx = ph.sb("dbx", [P, 2, TC])
        hh = ph.sb("hh", [P, 2, TC])
        hc = ph.sb("hc", [P, 4, TC])
        state = ph.sb("state", [P, 2 * NS])
        yT = ph.sb("yT", [P, 2, TC])
        yo = ph.sb("yo", [TB, NB, D])
        bc = ph.ps("bc", [P, 4, 512])
        ys = ph.ps("ys", [P, 2, 512])
        ep = ph.ps("ep", [P, 2, 512])
        ix_l, al_l, wo_l, a_r, dt_l, u_l, b_l, szq_l = ph.sems("ix_l al_l wo_l a_r dt_l u_l b_l szq_l")
        dt_f, u_f, b_f, szq_f = ph.sems("dt_f u_f b_f szq_f")
        el = ph.sems("el0 el1")
        gat = ph.sems("gat0 gat1 gat2 gat3")
        el_f, pay_f, d_r, w_r, pm_r, ep_r, ep_f, ob_r = ph.sems("el_f pay_f d_r w_r pm_r ep_r ep_f ob_r")
        ob_w = ph.sems("ob_w0 ob_w1")
        bc_r, bc_f, da_r, da_f, hc_r, ys_r, yT_r, yp_r, yo_r, yo_w = ph.sems("bc_r bc_f da_r da_f hc_r ys_r yT_r yp_r yo_r yo_w")
        em_r, dch, ach, pch = ph.sems("em_r dch ach pch")
        block = ph.block()

        @block.sync
        def _(sp):
            c = Counted(sp)
            sp.dma_start(idx[:, :], A["srcT"]).then_inc(ix_l, 16)
            sp.dma_start(tgt_i[:, :], A["dstT"]).then_inc(ix_l, 16)
            sp.dma_start(a_log[:, :, :], A["A_log"].rearrange("(h p) n -> p h n", p=P)).then_inc(al_l, 16)
            sp.dma_start(wo[:, :, :], A["out_wT"].rearrange("(c p) f -> p c f", p=P)).then_inc(wo_l, 16)
            with sp.Fori(0, NCH) as i:
                def load_edges(g):
                    s = g % 2
                    c.wait(el_f)
                    t0 = i * (GPC * GRP) + g * GRP
                    sp.dma_start(tc[:, s, :, :], rows(A["tc_d"])[:, bass.ds(t0, GRP), :]).then_inc(el[s], 16)
                    sp.dma_start(trow[:, s, :], bass.AP(A["dst"].tensor, 0, [[0, P], [1, EP]])[:, bass.ds(t0 * P, GRP * P)])\
                        .then_inc(el[s], 16)

                def store_sums(g):
                    c.wait(ob_r)
                    t0 = i * (GPC * GRP) + g * GRP
                    sp.dma_start(rows(A["agg_d"])[:, bass.ds(t0, GRP), :], ob[:, g % 2, :, :]).then_inc(ob_w[g % 2], 16)

                load_edges(0)
                c.wait(dt_f)
                sp.dma_start(dt[:, :, :], A["dtu_d"][:, bass.ds(i, 1), 0:2, :].rearrange("p a b t -> p (a b) t")).then_inc(dt_l, 16)
                c.wait(b_f)
                sp.dma_start(dbc[:, :], A["dbc_d"][:, bass.ds(i * TC, TC)]).then_inc(b_l, 16)
                c.wait(u_f)
                sp.dma_start(u[:, :, :], A["dtu_d"][:, bass.ds(i, 1), 2:4, :].rearrange("p a b t -> p (a b) t")).then_inc(u_l, 16)
                c.wait(szq_f)
                sp.dma_start(szq[:, :, :], A["szq_d"][:, bass.ds(i, 1), :, :].rearrange("p a b t -> p (a b) t")).then_inc(szq_l, 16)
                for g in range(GPC):
                    if g + 1 < GPC:
                        load_edges(g + 1)
                    if g:
                        store_sums(g - 1)
                store_sums(GPC - 1)
                c.wait(yo_r)
                sp.dma_start(rows(A["ym_d"], TB)[:, bass.ds(i * NB, NB), :], yo[:, :, :]).then_inc(yo_w, 16)
                c.turn()

        @block.gpsimd
        def _(pool):
            c = Counted(pool)
            ch = Chain(pool, pch)
            pool.wait_ge(ix_l, 32)
            pool.sem_inc(pay_f, RING)
            with pool.Fori(0, NCH) as i:
                for g in range(GPC):
                    c.wait(pay_f)
                    ch.step(pool.tensor_copy(ids[:, g, :], idx[:, bass.ds(i * (GPC * GRP) + g * GRP, GRP)]))
                    for k in range(GRP):
                        pool.indirect_dma_start(pay[:, g % RING, k, :], None, A["table"],
                                                bass.IndirectOffsetOnAxis(ids[:, g, k:k + 1], 0)).then_inc(gat[g % RING], 16)
                ch.restart()
                c.turn()
            pool.wait_ge(em_r, 1)
            ch.step(pool.partition_all_reduce(K.top_e[:, :], em1[:, :], P, bass.bass_isa.ReduceOp.max))
            ch.restart()

        @block.tensor
        def _(pe):
            c = Counted(pe)
            pe.wait_ge(wo_l, 16)
            pe.sem_inc(bc_f, 1)
            pe.sem_inc(ep_f, 2)
            with pe.Fori(0, NCH) as i:
                def broadcast(n):
                    if n == 0:
                        c.wait(b_l, 16)
                        c.wait(bc_f)
                    for j in range(2):
                        r = NR + j * NS + n
                        mm = pe.matmul(bc[:, (n % 2) * 2 + j, 0:TC], K.ident[0:48, r:r + 1].to_broadcast([48, P]), dbc[:, :],
                                       start=True, stop=True)
                    mm.then_inc(bc_r, 1)

                def add_states(n):
                    for h in range(2):
                        c.wait(hc_r)
                        mm = pe.matmul(ys[:, h, 0:TC], K.ident[:, :], hc[:, (n % 2) * 2 + h, :], start=(n == 0), stop=(n == NS - 1))
                    if n == NS - 1:
                        mm.then_inc(ys_r, 1)

                def sum_tiles(g, tiles):
                    if 0 in tiles:
                        c.wait(pm_r)
                    for k in tiles:
                        c.wait(ep_f)
                        pe.matmul(ep[:, (g * GRP + k) % 2, 0:ROW], mask[:, g % 2, k, :], pay[:, g % RING, k, :],
                                  start=True, stop=True).then_inc(ep_r, 1)

                for n in range(NS):
                    g = n // 2
                    broadcast(n)
                    if n:
                        add_states(n - 1)
                    if n % 2:
                        sum_tiles(g, range(first_tiles))
                    elif g:
                        sum_tiles(g - 1, range(first_tiles, GRP))
                add_states(NS - 1)
                sum_tiles(GPC - 1, range(first_tiles, GRP))
                c.wait(yT_r)
                for j in range(NB):
                    for h in range(2):
                        mm = pe.matmul(bc[0:TB, j, 0:D], yT[:, h, j * TB:(j + 1) * TB], wo[:, h, :], start=(h == 0), stop=(h == 1))
                mm.then_inc(yp_r, 1)
                pe.sem_inc(b_f, 1)
                c.turn()

        @block.scalar
        def _(act):
            c = Counted(act)
            ch = Chain(act, ach)
            act.wait_ge(al_l, 16)
            act.activation(a_pos[:, :, :], a_log[:, :, :], ACT.Exp).then_inc(a_r, 1)
            act.wait_ge(a_r, 2)
            act.sem_inc(da_f, 4)
            act.sem_inc(dt_f, 1)
            act.sem_inc(b_f, 1)
            act.sem_inc(yo_w, 16)
            act.sem_inc(ob_w[0], 16)
            act.sem_inc(ob_w[1], 16)
            with act.Fori(0, NCH) as i:
                def decay(n):
                    if n == 0:
                        c.wait(dt_l, 16)
                    for h in range(2):
                        c.wait(da_f)
                        act.activation(da[:, (n % 2) * 2 + h, :], dt[:, h, :], ACT.Exp, scale=a_neg[:, h, n:n + 1])\
                            .then_inc(da_r, 1)

                def weights(g):
                    c.wait(d_r)
                    act.activation(wexp[:, g % 2, :, :], wexp[:, g % 2, :, :], ACT.Exp).then_inc(w_r, 1)

                def leave(g, tiles):
                    if 0 in tiles:
                        c.wait(ob_w[g % 2], 16)
                    for k in tiles:
                        c.wait(ep_r)
                        ch.step(act.activation(ob[:, g % 2, k, :], ep[:, (g * GRP + k) % 2, 0:ROW], ACT.Copy))
                        act.sem_inc(ep_f, 1)
                    if GRP - 1 in tiles:
                        act.sem_inc(ob_r, 1)
                        act.sem_inc(pay_f, 1)

                decay(0)
                for n in range(NS):
                    g = n // 2
                    if n % 2 == 0:
                        weights(g)
                    if n + 1 < NS:
                        decay(n + 1)
                    if n % 2:
                        leave(g, range(first_tiles))
                    elif g:
                        leave(g - 1, range(first_tiles, GRP))
                leave(GPC - 1, range(first_tiles, GRP))
                c.wait(yp_r)
                c.wait(yo_w, 16)
                ch.step(act.activation(yo[:, :, :], bc[0:TB, :, 0:D], ACT.Copy))
                act.sem_inc(yo_r, 1)
                act.sem_inc(bc_f, 1)
                act.sem_inc(dt_f, 1)
                ch.restart()
                c.turn()
            act.wait_ge(yo_w, 16)
            for s in range(2):
                act.wait_ge(ob_w[s], 16)

        @block.vector
        def _(dve):
            c = Counted(dve)
            ch = Chain(dve, dch)
            dve.wait_ge(a_r, 1)
            dve.tensor_scalar(a_neg[:, :, :], a_pos[:, :, :], -1.0, None, ALU.mult).then_inc(a_r, 1)
            ch.mark(dve.memset(state[:, :], 0.0))
            ch.mark(dve.memset(emax[:, :, :], -HUGE))
            dve.wait_ge(ix_l, 32)
            ch.mark(dve.tensor_copy(tgt[:, :], tgt_i[:, :]))
            ch.restart()
            dve.sem_inc(el_f, 2)
            dve.sem_inc(u_f, 1)
            dve.sem_inc(szq_f, 1)
            with dve.Fori(0, NCH) as i:
                def exponents(g):
                    s = g % 2
                    dve.wait_ge(gat[g % RING], i * (2 * GRP * 16) + (g // RING + 1) * GRP * 16)
                    c.wait(el[s], 32)
                    ch.step(dve.tensor_tensor(z[:, :, :], pay[:, g % RING, :, D:ROW], tc[:, s, :, 0:HEADS], ALU.add))
                    ch.step(dve.scalar_tensor_tensor(out=z[:, :, :], in0=z[:, :, :], scalar=0.2, in1=z[:, :, :],
                                                     op0=ALU.mult, op1=ALU.max))
                    ch.mark(dve.tensor_tensor(emax[:, :, :], emax[:, :, :], z[:, :, :], ALU.max))
                    dve.tensor_tensor(wexp[:, s, :, :], z[:, :, :], tc[:, s, :, HEADS:2 * HEADS], ALU.subtract).then_inc(d_r, 1)

                def weigh(g):
                    s = g % 2
                    c.wait(w_r)
                    heads = pay[:, g % RING, :, 0:D].rearrange("p t (h f) -> p t h f", h=HEADS)
                    ch.mark(dve.tensor_tensor(heads, heads, wexp[:, s, :, :].unsqueeze(3).to_broadcast([P, GRP, HEADS, FOUT]), ALU.mult))
                    ch.mark(dve.tensor_copy(pay[:, g % RING, :, D:ROW], wexp[:, s, :, :]))
                    cols = tgt[:, bass.ds(i * (GPC * GRP) + g * GRP, GRP)]
                    ch.mark(dve.tensor_tensor(mask[:, s, :, :], trow[:, s, :].rearrange("p (t q) -> p t q", q=P),
                                         cols.unsqueeze(2).to_broadcast([P, GRP, P]), ALU.is_equal))
                    ch.wait()
                    dve.sem_inc(pm_r, 1)
                    dve.sem_inc(el_f, 1)

                def scan(n, h):
                    q = (n % 2) * 2
                    if h == 0:
                        if n == 0:
                            c.wait(u_l, 16)
                        c.wait(bc_r)
                    ch.step(dve.tensor_tensor(dbx[:, h, :], u[:, h, :], bc[:, q, 0:TC], ALU.mult))
                    c.wait(da_r)
                    ch.step(dve.tensor_tensor_scan(hh[:, h, :], da[:, q + h, :], dbx[:, h, :],
                                                   state[:, 2 * n + h:2 * n + h + 1], ALU.mult, ALU.add))
                    dve.sem_inc(da_f, 1)
                    ch.mark(dve.tensor_copy(state[:, 2 * n + h:2 * n + h + 1], hh[:, h, TC - 1:TC]))
                    dve.tensor_tensor(hc[:, q + h, :], hh[:, h, :], bc[:, q + 1, 0:TC], ALU.mult).then_inc(hc_r, 1)

                for n in range(NS):
                    g = n // 2
                    if n % 2 == 0:
                        exponents(g)
                        scan(n, 0)
                        weigh(g)
                        scan(n, 1)
                    else:
                        scan(n, 0)
                        scan(n, 1)
                dve.sem_inc(u_f, 1)
                c.wait(ys_r)
                c.wait(szq_l, 16)
                ch.step(dve.tensor_tensor(yT[:, :, :], ys[:, :, 0:TC], szq[:, 0:2, :], ALU.mult))
                ch.step(dve.tensor_tensor(yT[:, :, :], yT[:, :, :], szq[:, 2:4, :], ALU.add))
                dve.sem_inc(yT_r, 1)
                dve.sem_inc(szq_f, 1)
                ch.restart()
                c.turn()
            ch.step(dve.tensor_reduce(em1[:, :], emax[:, :, :], AX.XY, ALU.max))
            dve.sem_inc(em_r, 1)
            ch.restart()


def combine_nodes(nc, A, K):
    TOK = GRP * P
    HT = TOK // 2
    SPILL = ET // NCH * 2
    with ExitStack() as ctx:
        ph = Phase(nc, "com", ctx)
        fi = ph.sb("fi", [SPILL, GRP, 2], I32)
        ff = ph.sb("ff", [SPILL, GRP])
        cont = ph.sb("cont", [SPILL, GRP])
        frow = ph.sb("frow", [SPILL, GRP, ROW])
        here = ph.sb("here", [SPILL, P])
        pick = ph.sb("pick", [SPILL, 2, GRP, P])
        cb = ph.sb("cb", [P, NT, HEADS])
        eps = ph.sb("eps", [P, NT, HEADS])
        vec = ph.sb("vec", [P, 8, D])
        gb = ph.sb("gb", [P, EX])
        f1b = ph.sb("f1b", [P, 4])
        wl = ph.sb("wl", [P, 2, D])
        wg = ph.sb("wg", [P, 2, D])
        w1 = ph.sb("w1", [P, 2, 2 * D])
        w2 = ph.sb("w2", [P, 4, D])
        gw = ph.sb("gw", [P, 2, EX])
        ids = ph.sb("ids", [P, 2, GRP], I32)
        agg = ph.sb("agg", [P, GRP, ROW])
        yg = ph.sb("yg", [P, GRP, D])
        xn = ph.sb("xn", [P, GRP, D])
        x = ph.sb("x", [P, GRP, D])
        tmp = ph.sb("tmp", [P, GRP, D])
        hl = ph.sb("hl", [P, GRP, D])
        ha = ph.sb("ha", [P, GRP, D])
        gt = ph.sb("gt", [P, GRP, D])
        h = ph.sb("h", [P, GRP, D])
        fo = ph.sb("fo", [P, GRP, D])
        hT = ph.sb("hT", [P, 2, 4, P])
        tT = ph.sb("tT", [P, 2, TOK])
        fT = ph.sb("fT", [P, 4, TOK])
        rec = ph.sb("rec", [P, GRP, HEADS])
        st = ph.sb("st", [P, GRP, 6])
        mva = ph.sb("mva", [P, GRP, 2])
        mvl = ph.sb("mvl", [P, GRP, 2])
        mvb = ph.sb("mvb", [P, GRP, 2])
        rsa = ph.sb("rsa", [P, GRP])
        rsl = ph.sb("rsl", [P, GRP])
        rsb = ph.sb("rsb", [P, GRP])
        lg = ph.sb("lg", [P, GRP, EX])
        m8 = ph.sb("m8", [P, GRP, 8])
        i8 = ph.sb("i8", [P, GRP, 8], mybir.dt.uint32)
        i2 = ph.sb("i2", [P, GRP, 2])
        spp = ph.ps("spp", [P, 2, 512])
        tr = ph.ps("tr", [P, 2, 4, P])
        gp = ph.ps("gp", [P, 2, 512])
        fp = ph.ps("fp", [P, 2, 512])
        cl, vl, wld, ep1, ep2 = ph.sems("cl vl wld ep1 ep2")
        ag, ygs = ph.sems("ag ygs")
        xn_l, xn_f, x_l, x_f, g_f, sta, rsa_r, na_r, ga_r, stl, rsl_r, nl_r, gl_pe, gl_v, stb, rsb_r = ph.sems(
            "xn_l xn_f x_l x_f g_f sta rsa_r na_r ga_r stl rsl_r nl_r gl_pe gl_v stb rsb_r")
        pk_r, sp_r, mn_r, el_r, tr_r, tr_f, hT_r, gp_r, gp_f, gt_r, h_r, tT_r, fp_r, fp_f, fT_r, fo_r, xm_pe, x1_sp, xm_sp, lg_r = ph.sems(
            "pk_r sp_r mn_r el_r tr_r tr_f hT_r gp_r gp_f gt_r h_r tT_r fp_r fp_f fT_r fo_r xm_pe x1_sp xm_sp lg_r")
        x1_w, xm_w, dch, ach, pch = ph.sems("x1_w xm_w dch ach pch")
        block = ph.block()
        tiles = range(GRP)

        def passes(eng, first, mid, mix, rest, turn):
            first(0)
            mid(0)
            turn()
            with eng.Fori(0, NG - 1) as g:
                mix(g)
                first(g + 1)
                mid(g + 1)
                rest(g)
                turn()
            mix(NG - 1)
            rest(NG - 1)
            turn()

        def nothing(g):
            pass

        def group(g):
            return bass.ds(g * GRP, GRP)

        @block.sync
        def _(sp):
            c = Counted(sp)
            sp.dma_start(fi[:, :, 0], bass.AP(A["dst"].tensor, 0, [[P, SPILL], [P * SPILL, GRP]]), allow_slow_non_contiguous=True).then_inc(cl, 16)
            sp.dma_start(fi[:, :, 1], bass.AP(A["dprev"].tensor, 0, [[P, SPILL], [P * SPILL, GRP]]), allow_slow_non_contiguous=True).then_inc(cl, 16)
            sp.dma_start(frow[:, :, :], bass.AP(A["agg_d"].tensor, 0, [[P * ROW, SPILL], [P * SPILL * ROW, GRP], [1, ROW]])).then_inc(cl, 16)
            for j, v in enumerate((A["gat_b"], A["lnl_g"], A["lnl_b"], A["lng_g"], A["lng_b"], A["ff2_b"], A["ln2_g"], A["ln2_b"])):
                sp.dma_start(vec[:, j, :], spread(v, D)).then_inc(vl, 16)
            sp.dma_start(gb[:, :], spread(A["gate_b"], EX)).then_inc(vl, 16)
            sp.dma_start(f1b[:, :], A["ff1_b"].rearrange("(m p) -> p m", p=P), allow_slow_non_contiguous=True).then_inc(wld, 16)
            for t, w in ((wl, A["wlT"]), (wg, A["wgT"]), (w1, A["ff1_wT"]), (w2, A["ff2_wT"]), (gw, A["gate_w"])):
                sp.dma_start(t[:, :, :], w.rearrange("(c p) f -> p c f", p=P)).then_inc(wld, 16)

            def load_xn(g):
                c.wait(xn_f)
                sp.dma_start(xn[:, :, :], rows(A["xn_d"])[:, group(g), :]).then_inc(xn_l, 16)

            def load_x(g):
                c.wait(x_f)
                sp.dma_start(x[:, :, :], rows(A["x"])[:, group(g), :]).then_inc(x_l, 16)

            def store(g):
                c.wait(x1_sp)
                sp.dma_start(rows(A["x1_d"])[:, group(g), :], x[:, :, :]).then_inc(x1_w, 16)
                c.wait(xm_sp)
                sp.dma_start(rows(A["xm_d"])[:, group(g), :], fo[:, :, :]).then_inc(xm_w, 16)

            passes(sp, load_xn, nothing, load_x, store, c.turn)

        @block.gpsimd
        def _(pool):
            c = Counted(pool)
            ch = Chain(pool, pch)
            pool.wait_ge(vl, 16 * 9)

            def scaled(t, gain, bias):
                for j, op in ((gain, ALU.mult), (bias, ALU.add)):
                    ch.step(pool.tensor_tensor(t[:, :, :], t[:, :, :], vec[:, j, :].unsqueeze(1).to_broadcast([P, GRP, D]), op))

            def first(g):
                c.wait(g_f)
                ch.mark(pool.tensor_copy(ids[:, 0, :], K.start[:, group(g)]))
                ch.mark(pool.tensor_copy(ids[:, 1, :], K.rank[:, group(g)]))
                ch.wait()
                for k in tiles:
                    pool.indirect_dma_start(yg[:, k, :], None, A["ym_d"], bass.IndirectOffsetOnAxis(ids[:, 1, k:k + 1], 0)).then_inc(ygs, 16)
                for k in tiles:
                    pool.indirect_dma_start(agg[:, k, :], None, A["agg_d"], bass.IndirectOffsetOnAxis(ids[:, 0, k:k + 1], 0)).then_inc(ag, 16)
                c.wait(sta)
                inverse_deviation(pool, ch, K, rsa[:, :], mva[:, :, 1])
                pool.sem_inc(rsa_r, 1)
                c.wait(na_r)
                scaled(ha, 3, 4)
                c.wait(stl)
                inverse_deviation(pool, ch, K, rsl[:, :], mvl[:, :, 1])
                pool.sem_inc(rsl_r, 1)
                c.wait(nl_r)
                scaled(hl, 1, 2)
                pool.sem_inc(gl_pe, 1)
                pool.sem_inc(gl_v, 1)

            def rest(g):
                for _ in range(2):
                    c.wait(stb)
                    inverse_deviation(pool, ch, K, rsb[:, :], mvb[:, :, 1])
                    pool.sem_inc(rsb_r, 1)

            def turn():
                ch.restart()
                c.turn()

            passes(pool, first, nothing, nothing, rest, turn)

        @block.tensor
        def _(pe):
            c = Counted(pe)
            pe.wait_ge(wld, 16 * 6)
            pe.sem_inc(tr_f, 2)
            pe.sem_inc(gp_f, 2)
            pe.sem_inc(fp_f, 2)

            def spill(g):
                for k in tiles:
                    c.wait(pk_r)
                    for j in range(GRP):
                        mm = pe.matmul(spp[:, k % 2, 0:ROW], pick[:, k % 2, j, :], frow[:, j, :], start=(j == 0), stop=(j == GRP - 1))
                    mm.then_inc(sp_r, 1)

            def turned(parts, s):
                c.wait(tr_f)
                for j, part in enumerate(parts):
                    t = pe.transpose(tr[:, s, j, :], part, K.ident[:, :])
                t.then_inc(tr_r, 1)

            def both(k):
                turned([t[:, k, j * P:(j + 1) * P] for t in (hl, ha) for j in range(2)], k % 2)

            def gate(g):
                c.wait(gl_pe)
                both(0)
                for k in tiles:
                    if k + 1 < GRP:
                        both(k + 1)
                    c.wait(hT_r)
                    c.wait(gp_f)
                    for j in range(4):
                        mm = pe.matmul(gp[:, k % 2, 0:D], hT[:, k % 2, j, :], (wl if j < 2 else wg)[:, j % 2, :], start=(j == 0), stop=(j == 3))
                    mm.then_inc(gp_r, 1)

            def forward(g):
                c.wait(h_r)
                for k in tiles:
                    turned([h[:, k, j * P:(j + 1) * P] for j in range(2)], k % 2)
                c.wait(tT_r, GRP)
                for m in range(4):
                    for s in range(2):
                        c.wait(fp_f)
                        for j in range(2):
                            mm = pe.matmul(fp[:, s, 0:HT], w1[:, j, m * P:(m + 1) * P], tT[:, j, s * HT:(s + 1) * HT], start=(j == 0), stop=(j == 1))
                        mm.then_inc(fp_r, 1)
                c.wait(fT_r, 8)
                for k in tiles:
                    c.wait(gp_f)
                    for m in range(4):
                        mm = pe.matmul(gp[:, k % 2, 0:D], fT[:, m, k * P:(k + 1) * P], w2[:, m, :], start=(m == 0), stop=(m == 3))
                    mm.then_inc(gp_r, 1)

            def logits(g):
                c.wait(xm_pe)
                for k in tiles:
                    turned([fo[:, k, j * P:(j + 1) * P] for j in range(2)], k % 2)
                c.wait(tT_r, GRP)
                for k in tiles:
                    for j in range(2):
                        mm = pe.matmul(fp[:, 0, k * EX:(k + 1) * EX], tT[:, j, k * P:(k + 1) * P], gw[:, j, :], start=(j == 0), stop=(j == 1))
                mm.then_inc(lg_r, 1)

            passes(pe, spill, gate, forward, logits, c.turn)

        @block.scalar
        def _(act):
            c = Counted(act)
            ch = Chain(act, ach)
            act.wait_ge(wld, 16 * 6)
            act.wait_ge(ep1, 1)
            ch.step(act.activation(eps[:, :, :], cb[:, :, :], ACT.Exp))
            act.sem_inc(ep2, 1)

            def elu(g):
                c.wait(mn_r)
                act.activation(tmp[:, :, :], tmp[:, :, :], ACT.Exp).then_inc(el_r, 1)

            def gate(g):
                def leave(k):
                    c.wait(tr_r)
                    ch.step(act.activation(hT[:, k % 2, :, :], tr[:, k % 2, :, :], ACT.Copy))
                    act.sem_inc(tr_f, 1)
                    act.sem_inc(hT_r, 1)

                leave(0)
                for k in tiles:
                    if k + 1 < GRP:
                        leave(k + 1)
                    c.wait(gp_r)
                    ch.step(act.activation(gt[:, k, :], gp[:, k % 2, 0:D], ACT.Sigmoid))
                    act.sem_inc(gp_f, 1)
                act.sem_inc(gt_r, 1)

            def leave_pairs():
                for k in tiles:
                    c.wait(tr_r)
                    ch.step(act.activation(tT[:, :, k * P:(k + 1) * P], tr[:, k % 2, 0:2, :], ACT.Copy))
                    act.sem_inc(tr_f, 1)
                    act.sem_inc(tT_r, 1)

            def forward(g):
                leave_pairs()
                for m in range(4):
                    for s in range(2):
                        c.wait(fp_r)
                        ch.step(act.activation(fT[:, m, s * HT:(s + 1) * HT], fp[:, s, 0:HT], ACT.Relu, bias=f1b[:, m:m + 1]))
                        act.sem_inc(fp_f, 1)
                        act.sem_inc(fT_r, 1)
                for k in tiles:
                    c.wait(gp_r)
                    if k == 0:
                        c.wait(xm_w, 16)
                    ch.step(act.activation(fo[:, k, :], gp[:, k % 2, 0:D], ACT.Copy))
                    act.sem_inc(gp_f, 1)
                act.sem_inc(fo_r, 1)

            def logits(g):
                leave_pairs()

            def turn():
                ch.restart()
                c.turn()

            act.sem_inc(xm_w, 16)
            passes(act, elu, gate, forward, logits, turn)
            act.wait_ge(xm_w, 16)

        @block.vector
        def _(dve):
            c = Counted(dve)
            ch = Chain(dve, dch)
            dve.wait_ge(cl, 48)
            ch.step(dve.tensor_tensor(cont[:, :], fi[:, :, 0], fi[:, :, 1], ALU.is_equal))
            ch.step(dve.tensor_copy(ff[:, :], fi[:, :, 0]))
            ch.step(dve.scalar_tensor_tensor(out=ff[:, :], in0=ff[:, :], scalar=1.0, in1=cont[:, :], op0=ALU.add, op1=ALU.mult))
            ch.mark(dve.tensor_scalar(ff[:, :], ff[:, :], -1.0, None, ALU.add))
            ch.mark(dve.tensor_copy(here[:, :], K.iota[0:SPILL, :]))
            for q in range(HEADS):
                ch.mark(dve.tensor_scalar(cb[:, :, q], K.s_all[:, :, HEADS + q], K.top_src[:, q:q + 1], None, ALU.add))
            ch.wait()
            ch.step(dve.scalar_tensor_tensor(out=cb[:, :, :], in0=cb[:, :, :], scalar=0.2, in1=cb[:, :, :], op0=ALU.mult, op1=ALU.max))
            ch.step(dve.tensor_scalar(cb[:, :, :], cb[:, :, :], -1.0, K.top_e[:, 0:1], ALU.mult, ALU.add))
            ch.step(dve.tensor_scalar(cb[:, :, :], cb[:, :, :], 80.0, None, ALU.min))
            dve.sem_inc(ep1, 1)
            dve.wait_ge(ep2, 1)
            ch.step(dve.tensor_scalar(eps[:, :, :], eps[:, :, :], DEN_EPS, 1e-37, ALU.mult, ALU.max))
            ch.restart()
            dve.wait_ge(vl, 16 * 9)
            dve.sem_inc(xn_f, 1)
            dve.sem_inc(x_f, 1)
            dve.sem_inc(g_f, 1)
            dve.sem_inc(x1_w, 16)

            def row(j):
                return vec[:, j, :].unsqueeze(1).to_broadcast([P, GRP, D])

            def stats(t, mv, sem):
                for k in tiles:
                    ch.mark(dve.bn_stats(st[:, k, :], t[:, k, :]))
                ch.wait()
                for k in tiles:
                    ch.mark(dve.bn_aggr(mv[:, k, :], st[:, k, :]))
                ch.wait()
                dve.sem_inc(sem, 1)

            def normed(out, t, mv, rs):
                for k in tiles:
                    ch.mark(dve.tensor_scalar(out[:, k, :], t[:, k, :], mv[:, k, 0:1], rs[:, k:k + 1], ALU.subtract, ALU.mult))
                ch.wait()

            def first(g):
                c.wait(xn_l, 16)
                dve.wait_ge(ygs, g * (16 * GRP) + 16 * GRP)
                ch.step(dve.tensor_tensor(ha[:, :, :], yg[:, :, :], xn[:, :, :], ALU.add))
                stats(ha, mva, sta)
                c.wait(rsa_r)
                normed(ha, ha, mva, rsa)
                dve.sem_inc(na_r, 1)
                dve.wait_ge(ag, g * (16 * GRP) + 16 * GRP)

                def choose(k):
                    ch.step(dve.tensor_tensor(pick[:, k % 2, :, :], here[:, :].unsqueeze(1).to_broadcast([SPILL, GRP, P]),
                                              ff[:, :].unsqueeze(2).to_broadcast([SPILL, GRP, P]), ALU.is_equal))
                    dve.sem_inc(pk_r, 1)
                    ch.step(dve.tensor_scalar(here[:, :], here[:, :], float(P), None, ALU.add))

                choose(0)
                for k in tiles:
                    if k + 1 < GRP:
                        choose(k + 1)
                    c.wait(sp_r)
                    ch.mark(dve.scalar_tensor_tensor(out=agg[:, k, :], in0=agg[:, k, :], scalar=K.some[:, bass.ds(g * GRP + k, 1)],
                                                in1=spp[:, k % 2, 0:ROW], op0=ALU.mult, op1=ALU.add))
                ch.wait()
                ch.step(dve.tensor_tensor(rec[:, :, :], agg[:, :, D:ROW], eps[:, group(g), :], ALU.add))
                ch.step(dve.reciprocal(rec[:, :, :], rec[:, :, :]))
                ch.step(dve.tensor_tensor(hl[:, :, :].rearrange("p t (q f) -> p t q f", q=HEADS),
                                          agg[:, :, 0:D].rearrange("p t (q f) -> p t q f", q=HEADS),
                                          rec[:, :, :].unsqueeze(3).to_broadcast([P, GRP, HEADS, FOUT]), ALU.mult))
                dve.sem_inc(g_f, 1)
                ch.step(dve.tensor_tensor(hl[:, :, :], hl[:, :, :], xn[:, :, :], ALU.add))
                dve.sem_inc(xn_f, 1)
                ch.step(dve.tensor_tensor(hl[:, :, :], hl[:, :, :], row(0), ALU.add))
                ch.step(dve.tensor_scalar(tmp[:, :, :], hl[:, :, :], 0.0, None, ALU.min))
                dve.sem_inc(mn_r, 1)
                ch.step(dve.tensor_scalar(hl[:, :, :], hl[:, :, :], 0.0, -1.0, ALU.max, ALU.add))
                c.wait(el_r)
                ch.step(dve.tensor_tensor(hl[:, :, :], hl[:, :, :], tmp[:, :, :], ALU.add))
                stats(hl, mvl, stl)
                c.wait(rsl_r)
                normed(hl, hl, mvl, rsl)
                dve.sem_inc(nl_r, 1)

            def mix(g):
                c.wait(gl_v)
                c.wait(gt_r)
                ch.step(dve.tensor_tensor(h[:, :, :], hl[:, :, :], ha[:, :, :], ALU.subtract))
                ch.step(dve.tensor_tensor(h[:, :, :], h[:, :, :], gt[:, :, :], ALU.mult))
                ch.step(dve.tensor_tensor(h[:, :, :], h[:, :, :], ha[:, :, :], ALU.add))
                dve.sem_inc(h_r, 1)

            def rest(g):
                c.wait(fo_r)
                ch.step(dve.tensor_tensor(h[:, :, :], h[:, :, :], fo[:, :, :], ALU.add))
                ch.step(dve.tensor_tensor(h[:, :, :], h[:, :, :], row(5), ALU.add))
                stats(h, mvb, stb)
                c.wait(rsb_r)
                normed(h, h, mvb, rsb)
                ch.step(dve.tensor_tensor(h[:, :, :], h[:, :, :], row(6), ALU.mult))
                ch.step(dve.tensor_tensor(h[:, :, :], h[:, :, :], row(7), ALU.add))
                c.wait(x_l, 16)
                ch.step(dve.tensor_tensor(x[:, :, :], x[:, :, :], h[:, :, :], ALU.add))
                dve.sem_inc(x1_sp, 1)
                stats(x, mvb, stb)
                c.wait(rsb_r)
                normed(fo, x, mvb, rsb)
                dve.sem_inc(xm_pe, 1)
                dve.sem_inc(xm_sp, 1)
                c.wait(lg_r)
                ch.step(dve.tensor_tensor(lg[:, :, :], fp[:, 0, 0:GRP * EX].rearrange("p (t e) -> p t e", e=EX),
                                          gb[:, :].unsqueeze(1).to_broadcast([P, GRP, EX]), ALU.add))
                for k in tiles:
                    ch.mark(dve.max(m8[:, k, :], lg[:, k, :]))
                ch.wait()
                for k in tiles:
                    ch.mark(dve.max_index(i8[:, k, :], m8[:, k, :], lg[:, k, :]))
                ch.wait()
                ch.mark(dve.tensor_tensor(K.gap[:, group(g)], m8[:, :, 1], m8[:, :, 0], ALU.subtract))
                ch.step(dve.tensor_copy(i2[:, :, :], i8[:, :, 0:2]))
                ch.step(dve.tensor_tensor(K.hot[:, group(g), :, :], K.iota[:, 0:EX].unsqueeze(1).unsqueeze(1).to_broadcast([P, GRP, 2, EX]),
                                          i2[:, :, :].unsqueeze(3).to_broadcast([P, GRP, 2, EX]), ALU.is_equal))
                c.wait(x1_w, 16)
                dve.sem_inc(x_f, 1)

            def turn():
                ch.restart()
                c.turn()

            dve.sem_inc(x1_w, -16)
            passes(dve, first, nothing, mix, rest, turn)


def dispatch(nc, A, K):
    with ExitStack() as ctx:
        ph = Phase(nc, "dis", ctx)
        xm = ph.sb("xm", [P, NT, D])
        zero = ph.sb("zero", [P, 2048])
        osum = ph.sb("osum", [P, NT, EX])
        tot = ph.sb("tot", [P, NT, EX])
        pos = ph.sb("pos", [P, NT, EX])
        sel = ph.sb("sel", [P, NT, EX])
        two = ph.sb("two", [P, 2, NT])
        inc = ph.sb("inc", [P, EX])
        pad = ph.sb("pad", [P, EX])
        pad_i = ph.sb("pad_i", [P, EX], I32)
        offi = ph.sb("offi", [P, EX])
        one = ph.sb("one", [P, P])
        tj_i = ph.sb("tj_i", [P, MT], I32)
        tj = ph.sb("tj", [P, MT])
        te = ph.sb("te", [P, MT, EX])
        ti = ph.sb("ti", [P, MT])
        e1 = ph.sb("e1", [P, NT])
        wi = ph.ps("wi", [P, 2, 512])
        to = ph.ps("to", [P, 2, 512])
        xl, zr, zw, tj_r, os_r, mm_r, ps_r, ex_r, sc, dch, ach, pch = ph.sems("xl zr zw tj_r os_r mm_r ps_r ex_r sc dch ach pch")
        block = ph.block()
        halves_ = [(0, 25), (25, NT)]
        whole = MT * P * D // (P * 2048)

        @block.sync
        def _(sp):
            sp.dma_start(xm[:, :, :], rows(A["xm_d"])).then_inc(xl, 16)
            sp.wait_ge(zr, 1)
            flat = A["disp_d"].rearrange("r d -> (r d)")
            for j in range(whole):
                sp.dma_start(flat[j * P * 2048:(j + 1) * P * 2048].rearrange("(p f) -> p f", p=P), zero[:, :]).then_inc(zw, 16)
            left = (MT * P * D - whole * P * 2048) // P
            if left:
                sp.dma_start(flat[whole * P * 2048:].rearrange("(p f) -> p f", p=P), zero[:, 0:left]).then_inc(zw, 16)

        stores = whole + (1 if (MT * P * D) % (P * 2048) else 0)

        @block.gpsimd
        def _(pool):
            pool.iota(tj_i[:, :], pattern=[[P, MT]], base=0, channel_multiplier=0).then_inc(tj_r, 1)
            pool.wait_ge(ps_r, 1)
            pool.wait_ge(xl, 16)
            pool.wait_ge(zw, 16 * stores)
            for b in range(NT):
                for q in range(2):
                    pool.indirect_dma_start(A["disp_d"], bass.IndirectOffsetOnAxis(K.pos[:, q, b:b + 1], 0), xm[:, b, :], None).then_inc(sc, 16)
            pool.wait_ge(sc, 16 * 2 * NT)

        @block.tensor
        def _(pe):
            pe.wait_ge(os_r, 1)
            for j, (a, b) in enumerate(halves_):
                pe.matmul(wi[:, j, 0:(b - a) * EX], K.upper[:, :], osum[:, a:b, :].rearrange("p t e -> p (t e)"), start=True, stop=True)
                mm = pe.matmul(to[:, j, 0:(b - a) * EX], K.ones[:, :], osum[:, a:b, :].rearrange("p t e -> p (t e)"), start=True, stop=True)
            mm.then_inc(mm_r, 1)

        @block.scalar
        def _(act):
            act.activation(e1[:, :], K.gap[:, :], ACT.Exp).then_inc(ex_r, 1)

        @block.vector
        def _(dve):
            ch = Chain(dve, dch)
            dve.memset(zero[:, :], 0.0).then_inc(zr, 1)
            ch.mark(dve.memset(one[:, :], 1.0))
            ch.step(dve.tensor_tensor(osum[:, :, :], K.hot[:, :, 0, :], K.hot[:, :, 1, :], ALU.add))
            dve.sem_inc(os_r, 1)
            dve.wait_ge(ex_r, 1)
            ch.step(dve.tensor_scalar(K.wts[:, 1, :], e1[:, :], 1.0, None, ALU.add))
            ch.step(dve.reciprocal(K.wts[:, 0, :], K.wts[:, 1, :]))
            ch.step(dve.tensor_tensor(K.wts[:, 1, :], e1[:, :], K.wts[:, 0, :], ALU.mult))
            dve.wait_ge(mm_r, 1)
            for j, (a, b) in enumerate(halves_):
                ch.mark(dve.tensor_copy(tot[:, a:b, :].rearrange("p t e -> p (t e)"), to[:, j, 0:(b - a) * EX]))
            ch.wait()
            for e in range(EX):
                ch.mark(dve.tensor_tensor_scan(pos[:, :, e], one[:, 0:NT], tot[:, :, e], 0.0, ALU.mult, ALU.add))
            ch.wait()
            ch.step(dve.tensor_copy(inc[:, :], pos[:, NT - 1, :]))
            ch.step(dve.tensor_tensor(pos[:, :, :], pos[:, :, :], tot[:, :, :], ALU.subtract))
            for j, (a, b) in enumerate(halves_):
                ch.mark(dve.tensor_tensor(pos[:, a:b, :].rearrange("p t e -> p (t e)"), pos[:, a:b, :].rearrange("p t e -> p (t e)"),
                                     wi[:, j, 0:(b - a) * EX], ALU.add))
            ch.wait()
            ch.step(dve.tensor_scalar(pad[:, :], inc[:, :], float(P - 1), None, ALU.add))
            ch.step(dve.tensor_copy(pad_i[:, :], pad[:, :]))
            ch.step(dve.tensor_scalar(pad_i[:, :], pad_i[:, :], 7, 7, ALU.logical_shift_right, ALU.logical_shift_left))
            ch.step(dve.tensor_copy(pad[:, :], pad_i[:, :]))
            ch.step(dve.tensor_tensor_scan(offi[:, :], one[:, 0:EX], pad[:, :], 0.0, ALU.mult, ALU.add))
            ch.step(dve.tensor_tensor(pad[:, :], offi[:, :], pad[:, :], ALU.subtract))
            ch.step(dve.tensor_tensor(pos[:, :, :], pos[:, :, :], pad[:, :].unsqueeze(1).to_broadcast([P, NT, EX]), ALU.add))
            for q in range(2):
                ch.step(dve.tensor_tensor(sel[:, :, :], pos[:, :, :], K.hot[:, :, q, :], ALU.mult))
                ch.step(dve.tensor_reduce(two[:, q, :], sel[:, :, :], AX.X, ALU.add))
            ch.step(dve.tensor_copy(K.pos[:, :, :], two[:, :, :]))
            dve.sem_inc(ps_r, 1)
            dve.wait_ge(tj_r, 1)
            ch.step(dve.tensor_copy(tj[:, :], tj_i[:, :]))
            ch.step(dve.tensor_tensor(te[:, :, :], tj[:, :].unsqueeze(2).to_broadcast([P, MT, EX]),
                                      offi[:, :].unsqueeze(1).to_broadcast([P, MT, EX]), ALU.is_ge))
            ch.step(dve.tensor_reduce(ti[:, :], te[:, :, :], AX.X, ALU.add))
            ch.step(dve.tensor_scalar(ti[:, :], ti[:, :], float(EX - 1), float(P), ALU.min, ALU.mult))
            ch.step(dve.tensor_scalar(ti[:, :], ti[:, :], K.node[:, 0:1], None, ALU.add))
            ch.step(dve.tensor_copy(K.wrow[:, :], ti[:, :]))
            ch.restart()


def experts(nc, A, K):
    KC, FC = D // P, FF // P
    with ExitStack() as ctx:
        ph = Phase(nc, "exp", ctx)
        ids = ph.sb("ids", [P, 2], I32)
        xt = ph.sb("xt", [P, 2, D])
        w1 = ph.sb("w1", [P, 2, KC * FF])
        w2 = ph.sb("w2", [P, 2, FC * D])
        b1 = ph.sb("b1", [P, 2, FC])
        xT = ph.sb("xT", [P, 2, KC, P])
        hT = ph.sb("hT", [P, 2, FC, P])
        yo = ph.sb("yo", [P, 2, D])
        tr = ph.ps("tr", [P, 2, 512])
        hp = ph.ps("hp", [P, 2, 512])
        op = ph.ps("op", [P, 2, 512])
        xl, wg_, yw = ph.sems("xl0 xl1"), ph.sems("wg0 wg1"), ph.sems("yw0 yw1")
        x_f, w_f, tr_r, xT_r, hp_r, hT_r, op_r, yo_r, ach, dch, pch = ph.sems("x_f w_f tr_r xT_r hp_r hT_r op_r yo_r ach dch pch")
        block = ph.block()
        w1_rows = A["w1"].rearrange("e (p k) f -> (e p) (k f)", k=KC)
        w2_rows = A["w2"].rearrange("e (p k) d -> (e p) (k d)", k=FC)
        b1_rows = A["b1"].rearrange("e (p k) -> (e p) k", k=FC)

        @block.sync
        def _(sp):
            c = Counted(sp)
            with sp.Fori(0, MT // 2) as i:
                for s in range(2):
                    c.wait(x_f)
                    sp.dma_start(xt[:, s, :], rows(A["disp_d"])[:, bass.ds(i * 2 + s, 1), :].rearrange("p a d -> p (a d)")).then_inc(xl[s], 16)
                for s in range(2):
                    c.wait(yo_r)
                    sp.dma_start(rows(A["eout_d"])[:, bass.ds(i * 2 + s, 1), :].rearrange("p a d -> p (a d)"), yo[:, s, :]).then_inc(yw[s], 16)
                c.turn()

        @block.gpsimd
        def _(pool):
            c = Counted(pool)
            ch = Chain(pool, pch)
            pool.sem_inc(w_f, 2)
            with pool.Fori(0, MT // 2) as i:
                for s in range(2):
                    c.wait(w_f)
                    ch.step(pool.tensor_copy(ids[:, s:s + 1], K.wrow[:, bass.ds(i * 2 + s, 1)]))
                    for t, w in ((w1, w1_rows), (w2, w2_rows), (b1, b1_rows)):
                        pool.indirect_dma_start(t[:, s, :], None, w, bass.IndirectOffsetOnAxis(ids[:, s:s + 1], 0)).then_inc(wg_[s], 16)
                ch.restart()
                c.turn()

        @block.tensor
        def _(pe):
            c = Counted(pe)
            pe.sem_inc(x_f, 2)
            with pe.Fori(0, MT // 2) as i:
                def turned(s):
                    c.wait(xl[s], 16)
                    for k in range(KC):
                        t = pe.transpose(tr[:, s, k * P:(k + 1) * P], xt[:, s, :].rearrange("p (q k) -> p k q", k=KC)[:, k, :], K.ident[:, :])
                    t.then_inc(tr_r, 1)

                def up(s):
                    pe.wait_ge(wg_[s], i * 48 + 48)
                    c.wait(xT_r)
                    w = w1[:, s, :].rearrange("p (k q m) -> p k m q", k=KC, m=FC)
                    for m in range(FC):
                        for k in range(KC):
                            mm = pe.matmul(hp[:, s, m * P:(m + 1) * P], w[:, k, m, :], xT[:, s, k, :], start=(k == 0), stop=(k == KC - 1))
                    mm.then_inc(hp_r, 1)

                def down(s):
                    c.wait(hT_r)
                    for m in range(FC):
                        mm = pe.matmul(op[:, s, 0:D], hT[:, s, m, :], w2[:, s, m * D:(m + 1) * D], start=(m == 0), stop=(m == FC - 1))
                    mm.then_inc(op_r, 1)

                turned(0)
                turned(1)
                up(0)
                up(1)
                down(0)
                down(1)
                c.turn()

        @block.scalar
        def _(act):
            c = Counted(act)
            ch = Chain(act, ach)
            with act.Fori(0, MT // 2) as i:
                for s in range(2):
                    c.wait(tr_r)
                    ch.step(act.activation(xT[:, s, :, :], tr[:, s, 0:KC * P].rearrange("p (k q) -> p k q", k=KC), ACT.Copy))
                    act.sem_inc(xT_r, 1)
                    act.sem_inc(x_f, 1)
                for s in range(2):
                    c.wait(hp_r)
                    for m in range(FC):
                        ch.mark(act.activation(hT[:, s, m, :], hp[:, s, m * P:(m + 1) * P], ACT.Relu, bias=b1[:, s, m:m + 1]))
                    ch.wait()
                    act.sem_inc(hT_r, 1)
                ch.restart()
                c.turn()

        @block.vector
        def _(dve):
            c = Counted(dve)
            ch = Chain(dve, dch)
            for s in range(2):
                dve.sem_inc(yw[s], 16)
            with dve.Fori(0, MT // 2) as i:
                for s in range(2):
                    c.wait(op_r)
                    c.wait(yw[s], 16)
                    ch.step(dve.tensor_copy(yo[:, s, :], op[:, s, 0:D]))
                    dve.sem_inc(yo_r, 1)
                    dve.sem_inc(w_f, 1)
                ch.restart()
                c.turn()
            for s in range(2):
                dve.wait_ge(yw[s], 16)


def finish(nc, A, K):
    with ExitStack() as ctx:
        ph = Phase(nc, "fin", ctx)
        ids = ph.sb("ids", [P, 2, GRP], I32)
        e = ph.sb("e", [P, 2, GRP, D])
        xm = ph.sb("xm", [P, GRP, D])
        x1 = ph.sb("x1", [P, GRP, D])
        g = ph.sb("g", [P, NT, EX])
        g1 = ph.sb("g1", [P, NT, EX])
        gs = ph.sb("gs", [P, GRP, EX])
        gT = ph.sb("gT", [EX, 2, P])
        b2 = ph.sb("b2", [EX, D])
        vec = ph.sb("vec", [P, 2, D])
        y = ph.sb("y", [P, GRP, D])
        st = ph.sb("st", [P, GRP, 6])
        mv = ph.sb("mv", [P, GRP, 2])
        rs = ph.sb("rs", [P, GRP])
        tp = ph.ps("tp", [EX, 2, 512])
        bp = ph.ps("bp", [P, 2, 512])
        cl, eg, xm_l, x1_l, in_f, e_f, y_w = ph.sems("cl eg xm_l x1_l in_f e_f y_w")
        g_r, gs_r, tp_r, gT_r, bp_r, bp_f, st_r, rs_r, y_r, dch, pch, ach = ph.sems("g_r gs_r tp_r gT_r bp_r bp_f st_r rs_r y_r dch pch ach")
        block = ph.block()
        tiles = range(GRP)

        @block.sync
        def _(sp):
            c = Counted(sp)
            sp.dma_start(b2[:, :], A["b2"]).then_inc(cl, 16)
            for j, v in enumerate((A["gamma"], A["beta"])):
                sp.dma_start(vec[:, j, :], spread(v, D)).then_inc(cl, 16)

            def load(i):
                c.wait(in_f)
                sp.dma_start(xm[:, :, :], rows(A["xm_d"])[:, bass.ds(i * GRP, GRP), :]).then_inc(xm_l, 16)
                sp.dma_start(x1[:, :, :], rows(A["x1_d"])[:, bass.ds(i * GRP, GRP), :]).then_inc(x1_l, 16)

            with sp.Fori(0, NG - 1) as i:
                load(i)
                c.wait(y_r)
                sp.dma_start(rows(A["out"][0:(NT - 1) * P, :])[:, bass.ds(i * GRP, GRP), :], y[:, :, :]).then_inc(y_w, 16)
                c.turn()
            load(NG - 1)
            c.wait(y_r)
            t0 = (NG - 1) * GRP
            c.turn()
            sp.dma_start(rows(A["out"][t0 * P:(NT - 1) * P, :]), y[:, 0:GRP - 1, :]).then_inc(y_w, 16)
            sp.dma_start(A["out"][(NT - 1) * P:N, :], y[0:NLAST, GRP - 1, :]).then_inc(y_w, 16)

        @block.gpsimd
        def _(pool):
            c = Counted(pool)
            ch = Chain(pool, pch)
            with pool.Fori(0, NG) as i:
                c.wait(e_f)
                ch.step(pool.tensor_copy(ids[:, :, :], K.pos[:, :, bass.ds(i * GRP, GRP)]))
                for q in range(2):
                    for k in tiles:
                        pool.indirect_dma_start(e[:, q, k, :], None, A["eout_d"],
                                                bass.IndirectOffsetOnAxis(ids[:, q, k:k + 1], 0)).then_inc(eg, 16)
                c.wait(st_r)
                inverse_deviation(pool, ch, K, rs[:, :], mv[:, :, 1])
                pool.sem_inc(rs_r, 1)
                ch.restart()
                c.turn()

        @block.tensor
        def _(pe):
            c = Counted(pe)
            pe.wait_ge(cl, 48)
            pe.sem_inc(bp_f, 2)
            with pe.Fori(0, NG):
                c.wait(gs_r)
                for k in tiles:
                    pe.transpose(tp[:, k % 2, 0:P], gs[:, k, :], K.ident[:, :]).then_inc(tp_r, 1)
                    c.wait(gT_r)
                    if k != 1:
                        c.wait(bp_f, 2 if k == 0 else 1)
                    pe.matmul(bp[:, k % 2, 0:D], gT[:, k % 2, :], b2[:, :], start=True, stop=True).then_inc(bp_r, 1)
                c.turn()

        @block.scalar
        def _(act):
            c = Counted(act)
            act.wait_ge(g_r, 1)
            with act.Fori(0, NG) as i:
                act.activation(gs[:, :, :], g[:, bass.ds(i * GRP, GRP), :], ACT.Copy).then_inc(gs_r, 1)
                for k in tiles:
                    c.wait(tp_r)
                    act.activation(gT[:, k % 2, :], tp[:, k % 2, 0:P], ACT.Copy).then_inc(gT_r, 1)
                c.turn()

        @block.vector
        def _(dve):
            c = Counted(dve)
            ch = Chain(dve, dch)
            for q, t in ((0, g), (1, g1)):
                ch.mark(dve.tensor_tensor(t[:, :, :], K.hot[:, :, q, :], K.wts[:, q, :].unsqueeze(2).to_broadcast([P, NT, EX]), ALU.mult))
            ch.wait()
            ch.step(dve.tensor_tensor(g[:, :, :], g[:, :, :], g1[:, :, :], ALU.add))
            dve.sem_inc(g_r, 1)
            ch.restart()
            dve.wait_ge(cl, 48)
            dve.sem_inc(in_f, 1)
            dve.sem_inc(e_f, 1)
            dve.sem_inc(y_w, 16)

            def group(i):
                c.wait(y_w, 16)
                c.wait(xm_l, 16)
                for k in tiles:
                    c.wait(bp_r)
                    ch.step(dve.tensor_tensor(y[:, k, :], bp[:, k % 2, 0:D], xm[:, k, :], ALU.add))
                    dve.sem_inc(bp_f, 1)
                dve.wait_ge(eg, i * (16 * 2 * GRP) + 16 * 2 * GRP)
                for q in range(2):
                    for k in tiles:
                        ch.mark(dve.scalar_tensor_tensor(out=y[:, k, :], in0=e[:, q, k, :], scalar=K.wts[:, q, bass.ds(i * GRP + k, 1)],
                                                    in1=y[:, k, :], op0=ALU.mult, op1=ALU.add))
                    ch.wait()
                dve.sem_inc(e_f, 1)
                for k in tiles:
                    ch.mark(dve.bn_stats(st[:, k, :], y[:, k, :]))
                ch.wait()
                for k in tiles:
                    ch.mark(dve.bn_aggr(mv[:, k, :], st[:, k, :]))
                ch.wait()
                dve.sem_inc(st_r, 1)
                c.wait(rs_r)
                for k in tiles:
                    ch.mark(dve.tensor_scalar(y[:, k, :], y[:, k, :], mv[:, k, 0:1], rs[:, k:k + 1], ALU.subtract, ALU.mult))
                ch.wait()
                for j, op in ((0, ALU.mult), (1, ALU.add)):
                    ch.step(dve.tensor_tensor(y[:, :, :], y[:, :, :], vec[:, j, :].unsqueeze(1).to_broadcast([P, GRP, D]), op))
                c.wait(x1_l, 16)
                ch.step(dve.tensor_tensor(y[:, :, :], y[:, :, :], x1[:, :, :], ALU.add))
                dve.sem_inc(y_r, 1)
                dve.sem_inc(in_f, 1)
                ch.restart()
                c.turn()

            with dve.Fori(0, NG) as i:
                group(i)
            dve.wait_ge(y_w, 32)


_INS = {
    "x": ((NP, D), F32), "src": ((EP,), I32), "dst": ((EP,), I32), "dprev": ((EP,), I32), "srcT": ((P, ET), I32), "dstT": ((P, ET), I32), "noise": ((P, NT), F32),
    "gat_w": ((D, D), F32), "gat_wT": ((D, D), F32), "a_src": ((HEADS, FOUT), F32), "a_tgt": ((HEADS, FOUT), F32),
    "gat_b": ((D,), F32), "lnl_g": ((D,), F32), "lnl_b": ((D,), F32), "lng_g": ((D,), F32), "lng_b": ((D,), F32),
    "ln2_g": ((D,), F32), "ln2_b": ((D,), F32), "in_wT": ((D, 2 * D), F32), "conv_w": ((D, 4), F32),
    "conv_b": ((D,), F32), "xp_wT": ((D, 48), F32), "dt_wT": ((NR, D), F32), "dt_b": ((D,), F32),
    "A_log": ((D, NS), F32), "Dp": ((D,), F32), "out_wT": ((D, D), F32), "wlT": ((D, D), F32), "wgT": ((D, D), F32),
    "ff1_wT": ((D, 2 * D), F32), "ff1_b": ((2 * D,), F32), "ff2_wT": ((2 * D, D), F32), "ff2_b": ((D,), F32),
    "gate_w": ((D, EX), F32), "gate_b": ((EX,), F32), "w1": ((EX, D, FF), F32), "b1": ((EX, FF), F32),
    "w2": ((EX, FF, D), F32), "b2": ((EX, D), F32), "gamma": ((D,), F32), "beta": ((D,), F32),
}

_SCRATCH = {
    "xn_d": ((NP, D), F32), "table": ((NP, ROW), F32), "stgt_d": ((NP, HEADS), F32),
    "keys_d": ((2, NP), F32), "rank_d": ((NP,), I32), "first_d": ((ET,), I32), "v_d": ((EP, HEADS), F32),
    "tc_d": ((EP, 2 * HEADS), F32), "xs_d": ((NP, D), F32), "dbc_d": ((48, NP), F32),
    "dtu_d": ((P, NCH, 4, TC), F32), "szq_d": ((P, NCH, 4, TC), F32), "agg_d": ((EP, ROW), F32),
    "ym_d": ((NP, D), F32), "x1_d": ((NP, D), F32), "xm_d": ((NP, D), F32),
    "disp_d": ((MT * P, D), F32), "eout_d": ((MT * P, D), F32), "mx_d": ((P,), F32),
}


class Shared:
    pass


def gnn_ffn_kernel(nc, ins, out, debug=(), upto=99):
    Phase.used = []
    scratch = {}
    for name, (shape, dt) in _SCRATCH.items():
        kind = "ExternalOutput" if name in debug else "Internal"
        scratch[name] = nc.dram_tensor(name, shape, dt, kind=kind).ap()
    A = dict(ins, out=out, **scratch)
    with ExitStack() as ctx:
        def keep(name, shape, dt=F32):
            return ctx.enter_context(nc.sbuf_tensor("k_" + name, shape, dt))

        K = Shared()
        K.ident = keep("ident", [P, P])
        K.upper = keep("upper", [P, P])
        K.ones = keep("ones", [P, P])
        K.iota = keep("iota", [P, P])
        K.nhalf = keep("nhalf", [P, 16])
        K.iota_i = keep("iota_i", [P, P], I32)
        K.node = keep("node", [P, NT])
        K.node_i = keep("node_i", [P, NT], I32)
        K.s_all = keep("s_all", [P, NT, 2 * HEADS])
        K.rank = keep("rank", [P, NT], I32)
        K.start = keep("start", [P, NT], I32)
        K.some = keep("some", [P, NT])
        K.top_src = keep("top_src", [P, HEADS])
        K.top_e = keep("top_e", [P, 1])
        K.gap = keep("gap", [P, NT])
        K.hot = keep("hot", [P, NT, 2, EX])
        K.wts = keep("wts", [P, 2, NT])
        K.pos = keep("pos", [P, 2, NT], I32)
        K.wrow = keep("wrow", [P, MT], I32)
        phases = [constants, project, locate, order, spread_scores, mamba_in, edges_and_scan,
                  combine_nodes, dispatch, experts, finish]
        for n, phase in enumerate(phases):
            if n <= upto:
                phase(nc, A, K)
                if phase in (order, edges_and_scan):
                    clear_semaphores(nc)


def kernel(**inputs):
    import numpy as np
    import concourse.bacc as _bacc
    from concourse.bass_utils import run_bass_kernel_spmd as _run

    nc = _bacc.Bacc("TRN2", target_bir_lowering=False, num_devices=1)
    arrays = layout(inputs)
    ins = {n: nc.dram_tensor("in_" + n, s, t, kind="ExternalInput").ap() for n, (s, t) in _INS.items()}
    out = nc.dram_tensor("out", (N, D), F32, kind="ExternalOutput").ap()
    gnn_ffn_kernel(nc, ins, out)
    r = _run(nc, [arrays], core_ids=[0])
    return np.asarray(r.results[0]["out"])


def layout(inputs):
    import numpy as np

    v = {k.replace("L0_gnn_", "").replace("L0_ffn_", ""): np.asarray(a) for k, a in inputs.items()}
    tail = np.full(EP - E, NP - 1, np.int32)
    noise = np.concatenate([v["node_vec"], np.zeros(NP - N, np.float32)])
    dst = np.concatenate([v["dst"], tail])
    a = {
        "srcT": np.concatenate([v["src"], tail]).reshape(ET, P).T, "dstT": dst.reshape(ET, P).T,
        "x": np.concatenate([v["x"], np.zeros((NP - N, D), np.float32)]),
        "src": np.concatenate([v["src"], tail]),
        "dst": dst, "dprev": np.concatenate([np.full(1, -1, np.int32), v["dst"], tail])[:EP],
        "noise": noise.reshape(NT, P).T, "gat_w": v["gat_w"], "gat_wT": v["gat_w"].T,
        "a_src": v["gat_a_src"], "a_tgt": v["gat_a_tgt"], "gat_b": v["gat_b"],
        "lnl_g": v["ln_local_g"], "lnl_b": v["ln_local_b"], "lng_g": v["ln_global_g"], "lng_b": v["ln_global_b"],
        "ln2_g": v["ln2_g"], "ln2_b": v["ln2_b"], "in_wT": v["in_proj_w"].T, "conv_w": v["conv_w"],
        "conv_b": v["conv_b"], "xp_wT": v["x_proj_w"].T, "dt_wT": v["dt_proj_w"].T, "dt_b": v["dt_proj_b"],
        "A_log": v["A_log"], "Dp": v["D_param"], "out_wT": v["out_proj_w"].T, "wlT": v["wl"].T, "wgT": v["wg"].T,
        "ff1_wT": v["ff1_w"].T, "ff1_b": v["ff1_b"], "ff2_wT": v["ff2_w"].T, "ff2_b": v["ff2_b"],
        "gate_w": v["gate_w"], "gate_b": v["gate_b"], "w1": v["w1"], "b1": v["b1"], "w2": v["w2"], "b2": v["b2"],
        "gamma": v["gamma"], "beta": v["beta"],
    }
    return {"in_" + n: np.ascontiguousarray(x) for n, x in a.items()}
```

```python
from contextlib import ExitStack

import concourse.bass as bass
from concourse import mybir

P = 128
F32 = mybir.dt.float32
BF16 = mybir.dt.bfloat16
I32 = mybir.dt.int32
ALU = mybir.AluOpType
ACT = mybir.ActivationFunctionType
AX = mybir.AxisListType

N, E, D = 6250, 100000, 256
NT = -(-N // P)
NP = NT * P
NLAST = N - (NT - 1) * P
GRP = 7
NG = NT // GRP
ET = 784
EP = ET * P
HEADS, FOUT = 4, 64
ROW = D + HEADS
NS, NR = 16, 16
TC = 448
NCH = NP // TC
TB = 112
NB = TC // TB
EX, FF = 16, 512
MT = (2 * NP + EX * (P - 1)) // P
MT += MT % 2
LN_EPS = 1e-5
DEN_EPS = 1e-16
FAR = 1.0e6
HUGE = 3.0e38
assert NT % GRP == 0 and NP % TC == 0 and ET >= -(-E // P) and ET % (NCH * 8) == 0


class Chain:

    def __init__(self, eng, sem):
        self.eng, self.sem, self.n = eng, sem, 0

    def mark(self, ins):
        ins.then_inc(self.sem, 1)
        self.n += 1

    def wait(self):
        self.eng.wait_ge(self.sem, self.n)

    def after(self, n):
        self.eng.wait_ge(self.sem, n)

    def step(self, ins):
        self.mark(ins)
        self.wait()

    def restart(self):
        if self.n:
            self.eng.wait_ge(self.sem, self.n)
            self.eng.sem_inc(self.sem, -self.n)
        self.n = 0


class Counted:

    def __init__(self, eng):
        self.eng, self.seen = eng, {}

    def wait(self, sem, n=1):
        self.seen[sem.name] = (sem, self.seen.get(sem.name, (sem, 0))[1] + n)
        self.eng.wait_ge(sem, self.seen[sem.name][1])

    def turn(self):
        for sem, n in self.seen.values():
            self.eng.sem_inc(sem, -n)
        self.seen = {}


class Phase:

    used = []

    def __init__(self, nc, tag, ctx):
        self.nc, self.tag, self.ctx = nc, tag, ctx

    def sb(self, name, shape, dt=F32):
        return self.ctx.enter_context(self.nc.sbuf_tensor(f"{self.tag}_{name}", shape, dt))

    def ps(self, name, shape, dt=F32):
        return self.ctx.enter_context(self.nc.psum_tensor(f"{self.tag}_{name}", shape, dt))

    def sem(self, name):
        s = self.nc.alloc_semaphore(name=f"{self.tag}_{name}")
        self.used.append(s)
        return s

    def sems(self, names):
        return [self.sem(n) for n in names.split()]

    def block(self):
        return self.ctx.enter_context(self.nc.Block())


def clear_semaphores(nc):
    nc.clear_and_free_semaphores(Phase.used)
    Phase.used = []
    nc.all_engine_barrier()


def rows(ap, p=P):
    return ap.rearrange("(t p) d -> p t d", p=p)


def spread(ap, n, parts=P):
    return bass.AP(ap.tensor, ap.offset, [[0, parts], [1, n]])


def inverse_deviation(pool, ch, K, rstd, var):
    ch.step(pool.tensor_scalar(rstd, var, LN_EPS, None, ALU.add))
    ch.step(pool.tensor_tensor(rstd, rstd, K.nhalf[:, 0:rstd.shape[1]], ALU.pow))


def constants(nc, A, K):
    with ExitStack() as ctx:
        ph = Phase(nc, "cst", ctx)
        made, = ph.sems("made")
        block = ph.block()

        @block.gpsimd
        def _(pool):
            ch = Chain(pool, made)
            ch.mark(pool.memset(K.ident[:, :], 0.0))
            ch.mark(pool.memset(K.upper[:, :], 1.0))
            ch.mark(pool.memset(K.ones[:, :], 1.0))
            ch.mark(pool.memset(K.nhalf[:, :], -0.5))
            ch.wait()
            ch.mark(pool.affine_select(out=K.ident[:, :], in_=K.ident[:, :], compare_op=ALU.not_equal, fill=1.0,
                                  base=0, pattern=[[-1, P]], channel_multiplier=1))
            ch.mark(pool.affine_select(out=K.upper[:, :], in_=K.upper[:, :], compare_op=ALU.is_gt, fill=0.0,
                                  base=0, pattern=[[1, P]], channel_multiplier=-1))
            ch.mark(pool.iota(K.iota_i[:, :], pattern=[[1, P]], base=0, channel_multiplier=0))
            ch.mark(pool.iota(K.node_i[:, :], pattern=[[P, NT]], base=0, channel_multiplier=1))
            ch.wait()
            ch.mark(pool.tensor_copy(K.iota[:, :], K.iota_i[:, :]))
            ch.mark(pool.tensor_copy(K.node[:, :], K.node_i[:, :]))
            ch.restart()


def project(nc, A, K):
    with ExitStack() as ctx:
        ph = Phase(nc, "prj", ctx)
        xin = ph.sb("xin", [P, GRP, D])
        xn = ph.sb("xn", [P, GRP, D])
        st = ph.sb("st", [P, GRP, 6])
        mv = ph.sb("mv", [P, GRP, 2])
        rstd = ph.sb("rstd", [P, GRP])
        xT = ph.sb("xT", [P, 2, 2, P])
        pj = ph.sb("pj", [P, GRP, D + 8])
        gat = ph.sb("gat", [P, 2, D])
        w = ph.sb("w", [P, 2, D + 8])
        adiag = ph.sb("adiag", [P, 2, 8])
        tp = [ph.ps(f"tp{i}", [P, 2, P]) for i in range(2)]
        pp = [ph.ps(f"pp{i}", [P, 512]) for i in range(2)]
        wl, wz, wf, wr = ph.sems("wl wz wf wr")
        xl, xfree, st_r, rs_r, xn_pe, xn_sp = ph.sems("xl xfree st_r rs_r xn_pe xn_sp")
        tp_r, xT_r, pp_r, pp_free, pj_r, xn_w, pj_w, pad, padded, stgt = ph.sems("tp_r xT_r pp_r pp_free pj_r xn_w pj_w pad padded stgt")
        dch, ach, pch = ph.sems("dch ach pch")
        block = ph.block()

        @block.sync
        def _(sp):
            sp.dma_start(gat[:, :, :], A["gat_w"].rearrange("(c p) d -> p c d", p=P)).then_inc(wl, 16)
            sp.dma_start(w[:, :, 0:D], A["gat_wT"].rearrange("(c p) f -> p c f", p=P)).then_inc(wl, 16)
            sp.wait_ge(wz, 1)
            for a, off in ((A["a_src"], 0), (A["a_tgt"], HEADS)):
                for h in range(HEADS):
                    q = (h % 2) * FOUT
                    sp.dma_start(adiag[q:q + FOUT, h // 2, off + h:off + h + 1],
                                 a[h:h + 1, :].rearrange("a f -> f a")).then_inc(wl, 16)
            with sp.Fori(0, NG) as i:
                sp.wait_ge(xfree, 1)
                sp.sem_inc(xfree, -1)
                sp.dma_start(xin[:, :, :], rows(A["x"])[:, bass.ds(i * GRP, GRP), :]).then_inc(xl, 16)
                sp.wait_ge(xn_sp, 1)
                sp.sem_inc(xn_sp, -1)
                sp.dma_start(rows(A["xn_d"])[:, bass.ds(i * GRP, GRP), :], xn[:, :, :]).then_inc(xn_w, 16)
                sp.wait_ge(pj_r, GRP)
                sp.sem_inc(pj_r, -GRP)
                sp.dma_start(rows(A["table"])[:, bass.ds(i * GRP, GRP), :], pj[:, :, 0:ROW]).then_inc(pj_w, 16)
            sp.wait_ge(padded, 1)
            sp.dma_start(rows(A["stgt_d"]), K.s_all[:, :, HEADS:2 * HEADS]).then_inc(stgt, 16)
            sp.wait_ge(stgt, 16)
            sp.wait_ge(xn_w, 16)
            sp.wait_ge(pj_w, 16)

        @block.vector
        def _(dve):
            ch = Chain(dve, dch)
            dve.memset(adiag[:, :, :], 0.0).then_inc(wz, 1)
            dve.sem_inc(xfree, 1)
            dve.sem_inc(xn_w, 16)
            with dve.Fori(0, NG) as i:
                dve.wait_ge(xl, 16)
                dve.sem_inc(xl, -16)
                for k in range(GRP):
                    ch.mark(dve.bn_stats(st[:, k, :], xin[:, k, :]))
                ch.wait()
                for k in range(GRP):
                    ch.mark(dve.bn_aggr(mv[:, k, :], st[:, k, :]))
                ch.wait()
                dve.sem_inc(st_r, 1)
                dve.wait_ge(rs_r, 1)
                dve.sem_inc(rs_r, -1)
                dve.wait_ge(xn_w, 16)
                dve.sem_inc(xn_w, -16)
                for k in range(GRP):
                    ch.step(dve.tensor_scalar(xn[:, k, :], xin[:, k, :], mv[:, k, 0:1], rstd[:, k:k + 1],
                                              ALU.subtract, ALU.mult))
                    dve.sem_inc(xn_pe, 1)
                dve.sem_inc(xn_sp, 1)
                dve.sem_inc(xfree, 1)
                ch.restart()

        @block.gpsimd
        def _(pool):
            ch = Chain(pool, pch)
            with pool.Fori(0, NG) as i:
                pool.wait_ge(st_r, 1)
                pool.sem_inc(st_r, -1)
                inverse_deviation(pool, ch, K, rstd[:, :], mv[:, :, 1])
                pool.sem_inc(rs_r, 1)
                ch.restart()
            pool.wait_ge(pad, 1)
            ch.step(pool.affine_select(out=K.s_all[:, NT - 1, HEADS:2 * HEADS], in_=K.s_all[:, NT - 1, HEADS:2 * HEADS],
                                       compare_op=ALU.is_ge, fill=-1.0e30, base=NLAST - 1,
                                       pattern=[[0, HEADS]], channel_multiplier=-1))
            pool.sem_inc(padded, 1)
            ch.restart()

        @block.tensor
        def _(pe):
            pe.wait_ge(wl, 16 * (2 + 2 * HEADS))
            for m in range(2):
                for c in range(2):
                    mm = pe.matmul(pp[0][:, m * 8:m * 8 + 8], gat[:, c, m * P:(m + 1) * P], adiag[:, c, :],
                                   start=(c == 0), stop=(c == 1))
            mm.then_inc(wf, 1)
            pe.wait_ge(wr, 1)
            pe.sem_inc(pp_free, 2)
            with pe.Fori(0, NG) as i:
                def turn(k):
                    pe.wait_ge(xn_pe, k + 1)
                    for c in range(2):
                        t = pe.transpose(tp[k % 2][:, c, :], xn[:, k, c * P:(c + 1) * P], K.ident[:, :])
                    t.then_inc(tp_r, 1)

                turn(0)
                for k in range(GRP):
                    if k + 1 < GRP:
                        turn(k + 1)
                    pe.wait_ge(xT_r, k + 1)
                    pe.wait_ge(pp_free, 1)
                    pe.sem_inc(pp_free, -1)
                    for c in range(2):
                        mm = pe.matmul(pp[k % 2][:, 0:D + 8], xT[:, k % 2, c, :], w[:, c, :], start=(c == 0), stop=(c == 1))
                    mm.then_inc(pp_r, 1)
                pe.sem_inc(xn_pe, -GRP)
                pe.sem_inc(xT_r, -GRP)

        @block.scalar
        def _(act):
            ch = Chain(act, ach)
            act.wait_ge(wf, 1)
            act.activation(w[:, :, D:D + 8], pp[0][:, 0:16].rearrange("p (m e) -> p m e", m=2), ACT.Copy).then_inc(wr, 1)
            act.sem_inc(pj_w, 16)
            with act.Fori(0, NG) as i:
                act.wait_ge(pj_w, 16)
                act.sem_inc(pj_w, -16)

                def copy(k):
                    act.wait_ge(tp_r, k + 1)
                    act.activation(xT[:, k % 2, :, :], tp[k % 2][:, :, :], ACT.Copy).then_inc(xT_r, 1)

                copy(0)
                for k in range(GRP):
                    act.wait_ge(pp_r, k + 1)
                    ch.mark(act.activation(K.s_all[:, bass.ds(i * GRP + k, 1), :],
                                      pp[k % 2][:, D:D + 8].rearrange("p (a e) -> p a e", a=1), ACT.Copy))
                    ch.step(act.activation(pj[:, k, :], pp[k % 2][:, 0:D + 8], ACT.Copy))
                    act.sem_inc(pj_r, 1)
                    act.sem_inc(pp_free, 1)
                    if k + 1 < GRP:
                        copy(k + 1)
                act.sem_inc(tp_r, -GRP)
                act.sem_inc(pp_r, -GRP)
                ch.restart()
            act.sem_inc(pad, 1)


def locate(nc, A, K):
    with ExitStack() as ctx:
        ph = Phase(nc, "loc", ctx)
        fr_i = ph.sb("fr_i", [P, ET], I32)
        fr = ph.sb("fr", [P, ET])
        junk = ph.sb("junk", [P, ET])
        below = ph.sb("below", [P, NT])
        same = ph.sb("same", [P, NT])
        at = ph.sb("at", [P, NT])
        at_i = ph.sb("at_i", [P, NT], I32)
        b2 = ph.sb("b2", [P, NT])
        s2 = ph.sb("s2", [P, NT])
        full = ph.sb("full", [P, NT])
        none = ph.sb("none", [P, NT])
        over = ph.sb("over", [P, NT])
        rw_i = ph.sb("rw_i", [P, NT, P], I32)
        rw = ph.sb("rw", [P, NT, P])
        cm = ph.sb("cm", [P, NT, P])
        zero = ph.sb("zero", [P, ET * HEADS])
        far = ph.sb("far", [P, NT])
        far_i = ph.sb("far_i", [P, NT], I32)
        fw, fl, at_r, got, dch, zr, vz, far_r, vs = ph.sems("fw fl at_r got dch zr vz far_r vs")
        block = ph.block()

        @block.sync
        def _(sp):
            sp.dma_start(A["first_d"], bass.AP(A["dst"].tensor, 0, [[P, ET]]),
                         allow_slow_non_contiguous=True).then_inc(fw, 16)
            sp.wait_ge(fw, 16)
            sp.dma_start(fr_i[:, :], spread(A["first_d"], ET)).then_inc(fl, 16)
            sp.wait_ge(zr, 1)
            sp.dma_start(A["v_d"].rearrange("(p c) h -> p (c h)", p=P), zero[:, :]).then_inc(vz, 16)
            sp.wait_ge(vz, 16)

        @block.vector
        def _(dve):
            ch = Chain(dve, dch)
            dve.memset(zero[:, :], 0.0).then_inc(zr, 1)
            dve.wait_ge(fl, 16)
            ch.step(dve.tensor_copy(fr[:, :], fr_i[:, :]))
            with dve.Fori(0, NG) as i:
                for k in range(GRP):
                    b = bass.ds(i * GRP + k, 1)
                    dve.tensor_scalar(junk[:, :], fr[:, :], K.node[:, b], None, ALU.is_lt, ALU.add,
                                      accum_out=below[:, b]).then_inc(at_r, 1)
                    dve.wait_ge(at_r, 2 * k + 1)
                    dve.tensor_scalar(junk[:, :], fr[:, :], K.node[:, b], None, ALU.is_equal, ALU.add,
                                      accum_out=same[:, b]).then_inc(at_r, 1)
                    dve.wait_ge(at_r, 2 * k + 2)
                dve.sem_inc(at_r, -2 * GRP)
            ch.step(dve.tensor_scalar(at[:, :], below[:, :], -1.0, 0.0, ALU.add, ALU.max))
            ch.step(dve.tensor_copy(at_i[:, :], at[:, :]))
            dve.sem_inc(far_r, 1)
            dve.wait_ge(got, 16 * NT)
            ch.step(dve.tensor_copy(rw[:, :, :], rw_i[:, :, :]))
            nb = K.node[:, :].unsqueeze(2).to_broadcast([P, NT, P])
            ch.step(dve.tensor_tensor(cm[:, :, :], rw[:, :, :], nb, ALU.is_lt))
            ch.step(dve.tensor_reduce(b2[:, :], cm[:, :, :], AX.X, ALU.add))
            ch.step(dve.tensor_tensor(cm[:, :, :], rw[:, :, :], nb, ALU.is_equal))
            ch.step(dve.tensor_reduce(s2[:, :], cm[:, :, :], AX.X, ALU.add))
            ch.mark(dve.tensor_scalar(full[:, :], b2[:, :], float(P), None, ALU.is_ge))
            ch.mark(dve.tensor_scalar(none[:, :], b2[:, :], 0.0, None, ALU.is_le))
            ch.wait()
            ch.mark(dve.tensor_tensor(none[:, :], none[:, :], full[:, :], ALU.add))
            ch.mark(dve.tensor_tensor(full[:, :], full[:, :], at[:, :], ALU.add))
            ch.wait()
            ch.step(dve.tensor_tensor(over[:, :], same[:, :], none[:, :], ALU.is_gt))
            ch.step(dve.scalar_tensor_tensor(out=over[:, :], in0=full[:, :], scalar=float(1 - ET), in1=over[:, :],
                                             op0=ALU.add, op1=ALU.mult))
            ch.step(dve.tensor_scalar(K.spill[:, :], over[:, :], float(ET), None, ALU.add))
            ch.step(dve.scalar_tensor_tensor(out=b2[:, :], in0=at[:, :], scalar=float(P), in1=b2[:, :],
                                             op0=ALU.mult, op1=ALU.add))
            ch.step(dve.tensor_tensor(s2[:, :], s2[:, :], same[:, :], ALU.add))
            ch.step(dve.tensor_scalar(K.some[:, :], s2[:, :], 0.0, None, ALU.is_gt))
            ch.step(dve.tensor_scalar(far[:, :], K.some[:, :], -FAR, FAR, ALU.mult, ALU.add))
            ch.step(dve.tensor_tensor(far[:, :], far[:, :], b2[:, :], ALU.add))
            ch.step(dve.tensor_copy(far_i[:, :], far[:, :]))
            ch.step(dve.tensor_scalar(b2[:, :], b2[:, :], float(EP - 1), None, ALU.min))
            ch.step(dve.tensor_copy(K.start[:, :], b2[:, :]))
            dve.sem_inc(far_r, 1)
            ch.restart()

        @block.gpsimd
        def _(pool):
            pool.wait_ge(far_r, 1)
            for b in range(NT):
                pool.indirect_dma_start(rw_i[:, b, :], None, A["dst"].rearrange("(t q) -> t q", q=P),
                                        bass.IndirectOffsetOnAxis(at_i[:, b:b + 1], 0)).then_inc(got, 16)
            pool.wait_ge(far_r, 2)
            pool.wait_ge(vz, 16)
            for b in range(NT):
                pool.indirect_dma_start(A["v_d"], bass.IndirectOffsetOnAxis(far_i[:, b:b + 1], 0),
                                        K.s_all[:, b, HEADS:2 * HEADS], None,
                                        bounds_check=EP - 1, oob_is_err=False).then_inc(vs, 16)
            pool.wait_ge(vs, 16 * NT)


def order(nc, A, K):
    G = 8
    with ExitStack() as ctx:
        ph = Phase(nc, "ord", ctx)
        src_i = ph.sb("src_i", [P, ET], I32)
        part = ph.sb("part", [P, ET], I32)
        lo = ph.sb("lo", [P, ET])
        hi = ph.sb("hi", [P, ET])
        iota_b = ph.sb("iota_b", [P, P], BF16)
        ones_b = ph.sb("ones_b", [P, P], BF16)
        zero_b = ph.sb("zero_b", [P, P], BF16)
        ohl = ph.sb("ohl", [P, 2, G, P], BF16)
        ohh = ph.sb("ohh", [P, 2, G, NT], BF16)
        noise = ph.sb("noise", [P, NT])
        key = ph.sb("key", [P, 2, NT])
        sgn = ph.sb("sgn", [P, NT])
        sgn_i = ph.sb("sgn_i", [P, NT], I32)
        keyT = ph.sb("keyT", [NT, 2, P])
        low = ph.sb("low", [P, P])
        krow = ph.sb("krow", [P, NP])
        rrow = ph.sb("rrow", [P, NP])
        more = ph.sb("more", [P, 2, NP], BF16)
        tie = ph.sb("tie", [P, P], BF16)
        rk = ph.sb("rk", [P, 4, TC], I32)
        xn = ph.sb("xn", [P, NT, D])
        deg = ph.ps("deg", [P, 512])
        kt = ph.ps("kt", [P, 512])
        rp = ph.ps("rp", [P, 4, 512])
        ld, nl, xl, dch, ach = ph.sems("ld nl xl dch ach")
        oh_r, oh_f, deg_r, key_r, pad_r, kp_r, kt_r, kts, kw, kl = ph.sems("oh_r oh_f deg_r key_r pad_r kp_r kt_r kts kw kl")
        m_r, m_f, rp_r, rk_r, rw, rl, sc = ph.sems("m_r m_f rp_r rk_r rw rl sc")
        block = ph.block()

        @block.sync
        def _(sp):
            sp.dma_start(src_i[:, :], A["src"].rearrange("(p c) -> p c", p=P)).then_inc(ld, 16)
            sp.dma_start(noise[:, :], A["noise"]).then_inc(nl, 16)
            sp.dma_start(xn[:, :, :], rows(A["xn_d"])).then_inc(xl, 16)
            sp.wait_ge(kts, 1)
            sp.dma_start(A["keys_d"].rearrange("r (b f) -> b r f", f=P), keyT[:, :, :]).then_inc(kw, 16)
            sp.wait_ge(kw, 16)
            sp.dma_start(krow[:, :], spread(A["keys_d"], NP)).then_inc(kl, 16)
            sp.dma_start(rrow[:, :], bass.AP(A["keys_d"].tensor, NP, [[0, P], [1, NP]])).then_inc(kl, 16)
            sp.wait_ge(rk_r, 1)
            for q in range(4):
                n = min(4, NCH - 4 * q)
                sp.dma_start(A["rank_d"][4 * q * TC:(4 * q + n) * TC].rearrange("(a b f) -> a b f", a=1, f=TC),
                             rk[32 * q:32 * q + 1, 0:n, :]).then_inc(rw, 16)
            sp.wait_ge(rw, 64)
            sp.dma_start(K.rank[:, :], A["rank_d"].rearrange("(b p) -> p b", p=P),
                         allow_slow_non_contiguous=True).then_inc(rl, 16)

        @block.vector
        def _(dve):
            ch = Chain(dve, dch)
            ch.mark(dve.tensor_copy(iota_b[:, :], K.iota[:, :]))
            ch.mark(dve.memset(ones_b[:, :], 1.0))
            ch.mark(dve.memset(zero_b[:, :], 0.0))
            ch.mark(dve.tensor_scalar(low[:, :], K.upper[:, :], -1.0, 1.0, ALU.mult, ALU.add))
            dve.wait_ge(ld, 16)
            ch.mark(dve.tensor_scalar(part[:, :], src_i[:, :], P - 1, None, ALU.bitwise_and))
            ch.wait()
            ch.step(dve.tensor_copy(lo[:, :], part[:, :]))
            ch.step(dve.tensor_scalar(part[:, :], src_i[:, :], 7, None, ALU.logical_shift_right))
            ch.step(dve.tensor_copy(hi[:, :], part[:, :]))
            ch.restart()
            dve.sem_inc(oh_f, 2)
            with dve.Fori(0, ET // (2 * G)) as i:
                for s in range(2):
                    dve.wait_ge(oh_f, 1)
                    dve.sem_inc(oh_f, -1)
                    cols = bass.ds(i * 2 * G + s * G, G)
                    ch.mark(dve.tensor_tensor(ohh[:, s, :, :], iota_b[:, 0:NT].unsqueeze(1).to_broadcast([P, G, NT]),
                                         hi[:, cols].unsqueeze(2).to_broadcast([P, G, NT]), ALU.is_equal))
                    for g in range(G):
                        ch.mark(dve.tensor_scalar(ohl[:, s, g, :], iota_b[:, :], lo[:, bass.ds(i * 2 * G + s * G + g, 1)],
                                             None, ALU.is_equal))
                    ch.wait()
                    dve.sem_inc(oh_r, 1)
                ch.restart()
            dve.wait_ge(deg_r, 1)
            dve.wait_ge(nl, 16)
            ch.step(dve.tensor_tensor(key[:, 0, :], deg[:, 0:NT], noise[:, :], ALU.add))
            dve.sem_inc(key_r, 1)
            dve.wait_ge(pad_r, 1)
            ch.step(dve.tensor_scalar(sgn[:, :], key[:, 0, :], 0.0, 2.0, ALU.is_ge, ALU.mult))
            ch.step(dve.tensor_scalar(sgn_i[:, :], sgn[:, :], -1.0, None, ALU.add))
            ch.step(dve.tensor_tensor(key[:, 1, :].bitcast(I32), key[:, 0, :].bitcast(I32), sgn_i[:, :], ALU.add))
            ch.step(dve.tensor_scalar(sgn[:, :], key[:, 0, :], 0.0, 2.0 ** -126, ALU.is_equal, ALU.mult))
            ch.step(dve.tensor_tensor(key[:, 1, :], key[:, 1, :], sgn[:, :], ALU.add))
            dve.sem_inc(kp_r, 1)
            dve.wait_ge(kt_r, 1)
            ch.step(dve.tensor_copy(keyT[:, :, :], kt[0:NT, 0:2 * P].rearrange("b (r f) -> b r f", r=2)))
            dve.sem_inc(kts, 1)
            ch.restart()
            dve.wait_ge(kl, 32)
            dve.sem_inc(m_f, 2)

            def compare(j, s):
                blk = bass.ds(j * P, P)
                kj = key[:, 0, bass.ds(j, 1)]
                dve.wait_ge(m_f, 1)
                dve.sem_inc(m_f, -1)
                ch.mark(dve.tensor_scalar(more[:, s, :], rrow[:, :], kj, None, ALU.is_gt))
                ch.mark(dve.scalar_tensor_tensor(out=tie[:, :], in0=krow[:, blk], scalar=kj, in1=low[:, :],
                                            op0=ALU.is_equal, op1=ALU.mult))
                ch.wait()
                ch.mark(dve.tensor_tensor(more[:, s, blk], more[:, s, blk], tie[:, :], ALU.subtract))
                ch.mark(dve.tensor_copy(rrow[:, blk], krow[:, blk]))
                ch.wait()
                dve.sem_inc(m_r, 1)

            compare(0, 0)
            ch.restart()
            with dve.Fori(0, (NT - 1) // 2) as i:
                compare(i * 2 + 1, 1)
                compare(i * 2 + 2, 0)
                ch.restart()

        @block.gpsimd
        def _(pool):
            pool.wait_ge(key_r, 1)
            pool.affine_select(out=key[:, 0, NT - 1:NT], in_=key[:, 0, NT - 1:NT], compare_op=ALU.is_ge, fill=HUGE,
                               base=NLAST - 1, pattern=[[0, 1]], channel_multiplier=-1).then_inc(pad_r, 1)
            pool.wait_ge(rl, 16)
            pool.wait_ge(xl, 16)
            for b in range(NT):
                pool.indirect_dma_start(A["xs_d"], bass.IndirectOffsetOnAxis(K.rank[:, b:b + 1], 0),
                                        xn[:, b, :], None).then_inc(sc, 16)
            pool.wait_ge(sc, 16 * NT)

        @block.tensor
        def _(pe):
            pe.wait_ge(oh_r, 1)
            pe.matmul(deg[:, 0:NT], zero_b[:, :], zero_b[:, 0:NT], start=True, stop=False, skip_group_check=True)
            with pe.Fori(0, ET // (2 * G)) as i:
                for s in range(2):
                    pe.wait_ge(oh_r, 1)
                    pe.sem_inc(oh_r, -1)
                    for g in range(G):
                        mm = pe.matmul(deg[:, 0:NT], ohl[:, s, g, :], ohh[:, s, g, :], start=False, stop=False,
                                       skip_group_check=True)
                    mm.then_inc(oh_f, 1)
            pe.matmul(deg[:, 0:NT], zero_b[:, :], zero_b[:, 0:NT], start=False, stop=True,
                      skip_group_check=True).then_inc(deg_r, 1)
            pe.wait_ge(kp_r, 1)
            for r in range(2):
                mm = pe.transpose(kt[0:NT, r * P:(r + 1) * P], key[:, r, :], K.ident[:, :])
            mm.then_inc(kt_r, 1)

            def count(s, first=False, last=False):
                pe.wait_ge(m_r, 1)
                pe.sem_inc(m_r, -1)
                for c in range(NCH):
                    q = c // 4
                    mm = pe.matmul(rp[32 * q:32 * q + 1, c % 4, 0:TC], ones_b[:, 0:1],
                                   more[:, s, c * TC:(c + 1) * TC], start=first, stop=last, skip_group_check=True)
                mm.then_inc(m_f, 1)

            count(0, first=True)
            with pe.Fori(0, (NT - 1) // 2) as i:
                count(1)
                count(0)
            pe.drain().then_inc(rp_r, 1)

        @block.scalar
        def _(act):
            ch = Chain(act, ach)
            act.wait_ge(rp_r, 1)
            for q in range(4):
                n = min(4, NCH - 4 * q)
                ch.mark(act.activation(rk[32 * q:32 * q + 1, 0:n, :], rp[32 * q:32 * q + 1, 0:n, 0:TC], ACT.Copy))
            ch.wait()
            act.sem_inc(rk_r, 1)
            ch.restart()


def spread_scores(nc, A, K):
    with ExitStack() as ctx:
        ph = Phase(nc, "spr", ctx)
        dst = ph.sb("dst", [P, ET], I32)
        prev = ph.sb("prev", [P, ET], I32)
        keep = ph.sb("keep", [P, ET])
        v = ph.sb("v", [P, ET, HEADS])
        tc = ph.sb("tc", [P, ET, 2 * HEADS])
        tmp = ph.sb("tmp", [P, ET])
        mx = ph.sb("mx", [P, HEADS])
        dl, vl, hd, mx_r, top_r, tc_r, tw, dch = ph.sems("dl vl hd mx_r top_r tc_r tw dch")
        block = ph.block()

        @block.sync
        def _(sp):
            sp.dma_start(dst[:, :], A["dst"].rearrange("(p c) -> p c", p=P)).then_inc(dl, 16)
            sp.dma_start(prev[:, :], A["dprev"].rearrange("(p c) -> p c", p=P)).then_inc(dl, 16)
            sp.dma_start(v[:, :, :], A["v_d"].rearrange("(p c) h -> p c h", p=P)).then_inc(vl, 16)
            sp.wait_ge(tc_r, 1)
            sp.dma_start(A["tc_d"].rearrange("(p c) h -> p c h", p=P), tc[:, :, :]).then_inc(tw, 16)
            sp.wait_ge(tw, 16)

        @block.gpsimd
        def _(pool):
            pool.wait_ge(mx_r, 1)
            pool.partition_all_reduce(K.top_src[:, :], mx[:, :], P, bass.bass_isa.ReduceOp.max).then_inc(top_r, 1)
            pool.wait_ge(dl, 32)
            pool.wait_ge(vl, 16)
            pool.indirect_dma_start(v[:, 0, :], None, A["stgt_d"],
                                    bass.IndirectOffsetOnAxis(dst[:, 0:1], 0)).then_inc(hd, 16)

        @block.vector
        def _(dve):
            ch = Chain(dve, dch)
            ch.step(dve.tensor_reduce(mx[:, :], K.s_all[:, :, 0:HEADS].rearrange("p t h -> p h t"), AX.X, ALU.max))
            dve.sem_inc(mx_r, 1)
            dve.wait_ge(dl, 32)
            ch.step(dve.tensor_tensor(keep[:, :], dst[:, :], prev[:, :], ALU.is_equal))
            ch.step(dve.memset(keep[:, 0:1], 0.0))
            dve.wait_ge(hd, 16)
            for h in range(HEADS):
                ch.mark(dve.tensor_tensor_scan(tc[:, :, h], keep[:, :], v[:, :, h], 0.0, ALU.mult, ALU.add))
            ch.wait()
            dve.wait_ge(top_r, 1)
            for h in range(HEADS):
                ch.step(dve.tensor_scalar(tmp[:, :], tc[:, :, h], K.top_src[:, h:h + 1], None, ALU.add))
                ch.step(dve.scalar_tensor_tensor(out=tc[:, :, HEADS + h], in0=tmp[:, :], scalar=0.2, in1=tmp[:, :],
                                                 op0=ALU.mult, op1=ALU.max))
            dve.sem_inc(tc_r, 1)
            ch.restart()


def halves(ap):
    return ap.rearrange("(h p) -> p h", p=P)


def mamba_in(nc, A, K):
    with ExitStack() as ctx:
        ph = Phase(nc, "min", ctx)
        inw = ph.sb("inw", [P, 2, 2 * D])
        xpw = ph.sb("xpw", [P, 2, 48])
        dtw = ph.sb("dtw", [NR, D])
        cw = ph.sb("cw", [P, 2, 4])
        vec = ph.sb("vec", [P, 3, 2, 1])
        xs = ph.sb("xs", [TB, NB, D])
        xsT = ph.sb("xsT", [P, 4, TC])
        xcb = ph.sb("xcb", [P, 2, 3 + TC])
        cv = ph.sb("cv", [P, 2, TC])
        xcs = ph.sb("xcs", [P, 4, TC])
        dbc = ph.sb("dbc", [48, TC])
        rest = ph.sb("rest", [48, 2, TC])
        parts = ph.sb("parts", [48, 3, TC], BF16)
        ab = ph.sb("ab", [P, 2, TC])
        ex = ph.sb("ex", [P, 2, TC])
        lg = ph.sb("lg", [P, 2, TC])
        pl = ph.sb("pl", [P, 2, TC])
        rl = ph.sb("rl", [P, 2, TC])
        small = ph.sb("small", [P, 2, TC], I32)
        dtu = ph.sb("dtu", [P, 4, TC])
        szq = ph.sb("szq", [P, 4, TC])
        xt = ph.ps("xt", [P, 2, 512])
        ip = ph.ps("ip", [P, 2, 512])
        dp = ph.ps("dp", [P, 2, 512])
        db = ph.ps("db", [P, 512])
        wl, xl, xt_r, xT_r, ip_r, ip_f, xcb_f, xc_r, sz_r = ph.sems("wl xl xt_r xT_r ip_r ip_f xcb_f xc_r sz_r")
        cv_r, xcs_pe, xcs_v, xcs_f, db_r, dbs_pe, dbs_p, dbc_f, dt_r, dp_f = ph.sems(
            "cv_r xcs_pe xcs_v xcs_f db_r dbs_pe dbs_p dbc_f dt_r dp_f")
        ex_r, ex_f, ln_r, prt_r, dtu_r, szq_r, prt_w, dtu_w, szq_w = ph.sems("ex_r ex_f ln_r prt_r dtu_r szq_r prt_w dtu_w szq_w")
        dch, ach, pch = ph.sems("dch ach pch")
        block = ph.block()

        def half(i, h=0, n=2):
            return bass.ds((i & 1) * 2 + h, n)

        def chunks(eng, turned, body, turn):
            turned(0)
            body(0, True, False)
            turn()
            with eng.Fori(1, NCH) as i:
                body(i, False, False)
                turn()
            body(NCH, False, True)
            turn()

        def nothing(i):
            pass

        @block.sync
        def _(sp):
            c = Counted(sp)
            sp.dma_start(inw[:, :, :], A["in_wT"].rearrange("(c p) f -> p c f", p=P)).then_inc(wl, 16)
            sp.dma_start(xpw[:, :, :], A["xp_wT"].rearrange("(c p) f -> p c f", p=P)).then_inc(wl, 16)
            sp.dma_start(dtw[:, :], A["dt_wT"]).then_inc(wl, 16)
            sp.dma_start(cw[:, :, :], A["conv_w"].rearrange("(h p) k -> p h k", p=P)).then_inc(wl, 16)
            for j, v in enumerate((A["conv_b"], A["dt_b"], A["Dp"])):
                sp.dma_start(vec[:, j, :, 0], halves(v), allow_slow_non_contiguous=True).then_inc(wl, 16)

            def store_szq(i):
                c.wait(szq_r)
                sp.dma_start(A["szq_d"][:, bass.ds(i, 1), :, :].rearrange("p a b t -> p (a b) t"), szq[:, :, :]).then_inc(szq_w, 16)

            def store_parts(i):
                sp.dma_start(A["dbs_d"][:, bass.ds(i * TC, TC)].rearrange("(j r) t -> r j t", j=3), parts[NR:48, :, :]).then_inc(prt_w, 16)

            def store_steps(i):
                sp.dma_start(A["dtu_d"][:, bass.ds(i, 1), :, :].rearrange("p a b t -> p (a b) t"), dtu[:, :, :]).then_inc(dtu_w, 16)

            store_szq(0)
            c.turn()
            with sp.Fori(1, NCH) as i:
                c.wait(prt_r)
                store_parts(i - 1)
                store_szq(i)
                c.wait(dtu_r)
                store_steps(i - 1)
                c.turn()
            c.wait(prt_r)
            c.wait(dtu_r)
            for i in (NCH - 1, NCH):
                store_parts(i)
                store_steps(i)
            c.turn()

        @block.tensor
        def _(pe):
            c = Counted(pe)
            pe.wait_ge(wl, 16 * 7)
            pe.sem_inc(ip_f, 1)
            pe.sem_inc(dp_f, 1)

            def turned(i):
                c.wait(xl, 16)
                for q in range(2):
                    for j in range(NB):
                        t = pe.transpose(xt[:, q, j * TB:(j + 1) * TB], xs[:, j, q * P:(q + 1) * P], K.ident[0:TB, 0:TB])
                t.then_inc(xt_r, 1)

            def project_in(i, z):
                c.wait(ip_f)
                for h in range(2):
                    for q in range(2):
                        mm = pe.matmul(ip[:, h, 0:TC], inw[:, q, (2 * z + h) * P:(2 * z + h + 1) * P],
                                       xsT[:, half(i, q, 1), :].rearrange("p a t -> p (a t)"), start=(q == 0), stop=(q == 1))
                mm.then_inc(ip_r, 1)

            def body(i, first, last):
                if not last:
                    c.wait(xT_r)
                    project_in(i, 0)
                if not first:
                    c.wait(xcs_pe)
                    for q in range(2):
                        mm = pe.matmul(db[0:48, 0:TC], xpw[:, q, :], xcs[:, half(i - 1, q, 1), :].rearrange("p a t -> p (a t)"),
                                       start=(q == 0), stop=(q == 1))
                    mm.then_inc(db_r, 1)
                if not last:
                    turned(i + 1)
                    project_in(i, 1)
                if not first:
                    c.wait(dbs_pe)
                    c.wait(dp_f)
                    for h in range(2):
                        mm = pe.matmul(dp[:, h, 0:TC], dtw[:, h * P:(h + 1) * P], dbc[0:NR, :], start=True, stop=True)
                    mm.then_inc(dt_r, 1)

            chunks(pe, turned, body, c.turn)
            c.wait(xl, 16)
            c.turn()

        @block.scalar
        def _(act):
            c = Counted(act)
            ch = Chain(act, ach)

            def load(i):
                act.dma_start(xs[:, :, :], rows(A["xs_d"], TB)[:, bass.ds(i * NB, NB), :]).then_inc(xl, 16)

            load(0)
            act.wait_ge(wl, 16 * 7)
            act.sem_inc(szq_w, 16)
            act.sem_inc(dbc_f, 1)

            def turned(i):
                c.wait(xt_r)
                load((i + 1) % NCH)
                ch.step(act.activation(xsT[:, half(i), :], xt[:, :, 0:TC], ACT.Copy))
                act.sem_inc(xT_r, 1)

            def body(i, first, last):
                if not last:
                    c.wait(ip_r)
                    c.wait(xcb_f)
                    ch.step(act.activation(xcb[:, :, 3:3 + TC], ip[:, :, 0:TC], ACT.Copy))
                    act.sem_inc(xc_r, 1)
                    act.sem_inc(ip_f, 1)
                if not first:
                    c.wait(db_r)
                    c.wait(dbc_f)
                    ch.step(act.activation(dbc[:, :], db[0:48, 0:TC], ACT.Copy))
                    act.sem_inc(dbs_pe, 1)
                    act.sem_inc(dbs_p, 1)
                if not last:
                    turned(i + 1)
                    c.wait(ip_r)
                    c.wait(szq_w, 16)
                    ch.step(act.activation(szq[:, 0:2, :], ip[:, :, 0:TC], ACT.Silu))
                    act.sem_inc(sz_r, 1)
                    act.sem_inc(ip_f, 1)
                    c.wait(cv_r)
                    c.wait(xcs_f)
                    ch.step(act.activation(xcs[:, half(i), :], cv[:, :, :], ACT.Silu))
                    act.sem_inc(xcs_pe, 1)
                    act.sem_inc(xcs_v, 1)
                if not first:
                    c.wait(dt_r)
                    for h in range(2):
                        ch.mark(act.activation(ab[:, h, :], dp[:, h, 0:TC], ACT.Abs, bias=vec[:, 1, h, :]))
                    ch.wait()
                    c.wait(ex_f)
                    ch.step(act.activation(ex[:, :, :], ab[:, :, :], ACT.Exp, scale=-1.0))
                    act.sem_inc(ex_r, 1)
                    ch.step(act.activation(lg[:, :, :], ex[:, :, :], ACT.Ln, bias=1.0))
                    act.sem_inc(ln_r, 1)

            def turn():
                ch.restart()
                c.turn()

            chunks(act, turned, body, turn)
            act.wait_ge(szq_w, 16)

        @block.gpsimd
        def _(pool):
            c = Counted(pool)
            ch = Chain(pool, pch)
            pool.sem_inc(prt_w, 16)

            def body(i, first, last):
                if first:
                    return
                c.wait(dbs_p)
                c.wait(prt_w, 16)
                ch.step(pool.tensor_copy(parts[:, 0, :], dbc[:, :]))
                ch.step(pool.tensor_tensor(rest[:, 0, :], dbc[:, :], parts[:, 0, :], ALU.subtract))
                pool.sem_inc(dbc_f, 1)
                ch.step(pool.tensor_copy(parts[:, 1, :], rest[:, 0, :]))
                ch.step(pool.tensor_tensor(rest[:, 1, :], rest[:, 0, :], parts[:, 1, :], ALU.subtract))
                ch.step(pool.tensor_copy(parts[:, 2, :], rest[:, 1, :]))
                pool.sem_inc(prt_r, 1)

            def turn():
                ch.restart()
                c.turn()

            chunks(pool, nothing, body, turn)
            pool.wait_ge(prt_w, 32)

        @block.vector
        def _(dve):
            c = Counted(dve)
            ch = Chain(dve, dch)
            dve.wait_ge(wl, 16 * 7)
            ch.step(dve.memset(xcb[:, :, 0:3], 0.0))
            ch.restart()
            dve.sem_inc(xcb_f, 1)
            dve.sem_inc(xcs_f, 2)
            dve.sem_inc(ex_f, 1)
            dve.sem_inc(dtu_w, 16)

            def front(i):
                c.wait(xc_r)
                for h in range(2):
                    ch.mark(dve.tensor_scalar(cv[:, h, :], xcb[:, h, 0:TC], cw[:, h, 0:1], vec[:, 0, h, :], ALU.mult, ALU.add))
                ch.wait()
                for k in range(1, 4):
                    for h in range(2):
                        ch.mark(dve.scalar_tensor_tensor(out=cv[:, h, :], in0=xcb[:, h, k:k + TC], scalar=cw[:, h, k:k + 1],
                                                         in1=cv[:, h, :], op0=ALU.mult, op1=ALU.add))
                    ch.wait()
                dve.sem_inc(cv_r, 1)
                ch.step(dve.tensor_copy(xcb[:, :, 0:3], xcb[:, :, TC:TC + 3]))
                dve.sem_inc(xcb_f, 1)

                c.wait(xcs_v)
                c.wait(sz_r)
                for h in range(2):
                    ch.mark(dve.scalar_tensor_tensor(out=szq[:, 2 + h, :], in0=xcs[:, half(i, h, 1), :].rearrange("p a t -> p (a t)"), scalar=vec[:, 2, h, :],
                                                     in1=szq[:, h, :], op0=ALU.mult, op1=ALU.mult))
                ch.wait()
                dve.sem_inc(szq_r, 1)

            def back(i):
                c.wait(ex_r)
                ch.mark(dve.tensor_scalar(small[:, :, :], ex[:, :, :], 2.0 ** -6, None, ALU.is_lt))
                ch.step(dve.tensor_scalar(pl[:, :, :], ex[:, :, :], 1.0 / 3.0, -0.5, ALU.mult, ALU.add))
                ch.step(dve.tensor_tensor(pl[:, :, :], pl[:, :, :], ex[:, :, :], ALU.mult))
                ch.mark(dve.scalar_tensor_tensor(out=pl[:, :, :], in0=pl[:, :, :], scalar=1.0, in1=ex[:, :, :],
                                                 op0=ALU.add, op1=ALU.mult))
                for h in range(2):
                    ch.mark(dve.tensor_scalar(rl[:, h, :], dp[:, h, 0:TC], vec[:, 1, h, :], 0.0, ALU.add, ALU.max))
                ch.wait()
                dve.sem_inc(dp_f, 1)
                c.wait(ln_r)
                ch.step(dve.copy_predicated(lg[:, :, :], small[:, :, :], pl[:, :, :]))
                c.wait(dtu_w, 16)
                ch.step(dve.tensor_tensor(dtu[:, 0:2, :], rl[:, :, :], lg[:, :, :], ALU.add))
                dve.sem_inc(ex_f, 1)
                ch.step(dve.tensor_tensor(dtu[:, 2:4, :], dtu[:, 0:2, :], xcs[:, half(i), :], ALU.mult))
                dve.sem_inc(dtu_r, 1)
                dve.sem_inc(xcs_f, 1)

            def turn():
                ch.restart()
                c.turn()

            def body(i, first, last):
                if not last:
                    front(i)
                if not first:
                    back(i - 1)

            chunks(dve, nothing, body, turn)
            dve.wait_ge(dtu_w, 32)


def edges_and_scan(nc, A, K):
    GPC = 8
    RING = 4
    AHEAD = 2
    assert ET == NCH * GPC * GRP and NS == 2 * GPC
    early = 4
    with ExitStack() as ctx:
        ph = Phase(nc, "run", ctx)
        idx = ph.sb("idx", [P, ET + AHEAD * GRP], I32)
        tgt_i = ph.sb("tgt_i", [P, ET], I32)
        tgt = ph.sb("tgt", [P, ET])
        ids = ph.sb("ids", [P, GPC, GRP], I32)
        pay = ph.sb("pay", [P, RING, GRP, ROW])
        tc = ph.sb("tc", [P, 2, GRP, 2 * HEADS])
        trow = ph.sb("trow", [P, 2, GRP * P], I32)
        z = ph.sb("z", [P, GRP, HEADS])
        emax = ph.sb("emax", [P, GRP, HEADS])
        em1 = ph.sb("em1", [P, 1])
        wexp = ph.sb("wexp", [P, 2, GRP, HEADS])
        mask = ph.sb("mask", [P, 2, GRP, P])
        ob = ph.sb("ob", [P, 2, GRP, ROW])
        a_log = ph.sb("a_log", [P, 2, NS])
        a_pos = ph.sb("a_pos", [P, 2, NS])
        a_neg = ph.sb("a_neg", [P, 2, NS])
        wo = ph.sb("wo", [P, 2, D])
        sel32 = ph.sb("sel32", [96, 32])
        sel = ph.sb("sel", [96, 32], BF16)
        dt = ph.sb("dt", [P, 4, TC])
        u = ph.sb("u", [P, 4, TC])
        dbs = ph.sb("dbs", [96, 2, TC], BF16)
        szq = ph.sb("szq", [P, 4, TC])
        da = ph.sb("da", [P, 4, TC])
        dbx = ph.sb("dbx", [P, 2, 2, TC])
        hh = ph.sb("hh", [P, 2, 2, TC])
        hc = ph.sb("hc", [P, 2, 2, 2, TC])
        hs = ph.sb("hs", [P, 2, 2, TC])
        state = ph.sb("state", [P, NS, 2])
        yT = ph.sb("yT", [P, 2, TC])
        yo = ph.sb("yo", [TB, NB, D])
        bc = ph.ps("bc", [P, 4, 512])
        ys = ph.ps("ys", [P, 2, 512])
        ep = ph.ps("ep", [P, 2, 512])
        ix_l, al_l, wo_l, a_r, sel_r, dt_l, u_l, b_l, szq_l = ph.sems("ix_l al_l wo_l a_r sel_r dt_l u_l b_l szq_l")
        in_f, in_c, szq_f, pad_r = ph.sems("in_f in_c szq_f pad_r")
        el = ph.sems("el0 el1")
        gat = ph.sems("gat0 gat1 gat2 gat3")
        el_f, pay_f, d_r, w_r, pm_r, ep_r, ep_f = ph.sems("el_f pay_f d_r w_r pm_r ep_r ep_f")
        ob_w = ph.sems("ob_w0 ob_w1")
        bc_r, bc_f, da_r, da_f, hc_r, hs_r, ys_r, yT_r, yp_r, yo_r, yo_w = ph.sems("bc_r bc_f da_r da_f hc_r hs_r ys_r yT_r yp_r yo_r yo_w")
        em_r, dch, ach, pch = ph.sems("em_r dch ach pch")
        block = ph.block()

        def chunks(eng, body, turn):
            body(0, True)
            turn()
            with eng.Fori(1, NCH) as i:
                body(i, False)
                turn()

        def half(i):
            return bass.ds((i & 1) * 2, 2)

        @block.sync
        def _(sp):
            c = Counted(sp)
            sp.dma_start(idx[:, 0:ET], A["srcT"]).then_inc(ix_l, 16)
            sp.dma_start(tgt_i[:, :], A["dstT"]).then_inc(ix_l, 16)
            sp.dma_start(a_log[:, :, :], A["A_log"].rearrange("(h p) n -> p h n", p=P)).then_inc(al_l, 16)
            sp.dma_start(wo[:, :, :], A["out_wT"].rearrange("(c p) f -> p c f", p=P)).then_inc(wo_l, 16)

            def load_chunk(i):
                sp.dma_start(dbs[:, bass.ds(i & 1, 1), :].rearrange("p a t -> p (a t)"), A["dbs_d"][:, bass.ds(i * TC, TC)]).then_inc(b_l, 16)
                sp.dma_start(dt[:, half(i), :], A["dtu_d"][:, bass.ds(i, 1), 0:2, :].rearrange("p a b t -> p (a b) t")).then_inc(dt_l, 16)
                sp.dma_start(u[:, half(i), :], A["dtu_d"][:, bass.ds(i, 1), 2:4, :].rearrange("p a b t -> p (a b) t")).then_inc(u_l, 16)

            load_chunk(0)

            def body(i, first):
                for g in range(GPC):
                    s = g % 2
                    c.wait(el_f)
                    t0 = i * (GPC * GRP) + g * GRP
                    sp.dma_start(tc[:, s, :, :], rows(A["tc_d"])[:, bass.ds(t0, GRP), :]).then_inc(el[s], 16)
                    sp.dma_start(trow[:, s, :], bass.AP(A["dst"].tensor, 0, [[0, P], [1, EP]])[:, bass.ds(t0 * P, GRP * P)])\
                        .then_inc(el[s], 16)
                    if g == 1:
                        c.wait(in_f)
                        c.wait(in_c, 3)
                        load_chunk(i + 1)
                    if g == 3:
                        c.wait(szq_f)
                        sp.dma_start(szq[:, :, :], A["szq_d"][:, bass.ds(i, 1), :, :].rearrange("p a b t -> p (a b) t")).then_inc(szq_l, 16)

            chunks(sp, body, c.turn)

        @block.gpsimd
        def _(pool):
            c = Counted(pool)
            ch = Chain(pool, pch)
            pool.memset(idx[:, ET:], 0).then_inc(pad_r, 1)
            pool.wait_ge(pad_r, 1)
            pool.wait_ge(ix_l, 32)
            pool.sem_inc(pay_f, RING - AHEAD)

            def gather(g, tiles):
                for k in tiles:
                    pool.indirect_dma_start(pay[:, g % RING, k, :], None, A["table"],
                                            bass.IndirectOffsetOnAxis(ids[:, g % GPC, k:k + 1], 0)).then_inc(gat[g % RING], 16)

            def add_pair(m):
                c.wait(hc_r, 2)
                pool.tensor_tensor(hs[:, m % 2, :, :], hc[:, m % 2, 0, :, :], hc[:, m % 2, 1, :, :], ALU.add).then_inc(hs_r, 1)

            def turn():
                ch.restart()
                c.turn()

            for g in range(AHEAD):
                ch.mark(pool.tensor_copy(ids[:, g, :], idx[:, g * GRP:(g + 1) * GRP]))
            ch.restart()
            for g in range(AHEAD):
                gather(g, range(GRP))

            def body(i, first):
                for g in range(GPC):
                    nxt = g + AHEAD
                    c.wait(pay_f)
                    ch.step(pool.tensor_copy(ids[:, nxt % GPC, :], idx[:, bass.ds(i * (GPC * GRP) + nxt * GRP, GRP)]))
                    gather(nxt, range(early))
                    if g or not first:
                        add_pair((g - 1) % GPC)
                    gather(nxt, range(early, GRP))

            chunks(pool, body, turn)
            add_pair(GPC - 1)
            turn()
            for s in range(RING):
                pool.wait_ge(gat[s], 16 * GRP * len(range(s, NCH * GPC + AHEAD, RING)))
            pool.wait_ge(em_r, 1)
            ch.step(pool.partition_all_reduce(K.top_e[:, :], em1[:, :], P, bass.bass_isa.ReduceOp.max))
            ch.restart()

        @block.tensor
        def _(pe):
            c = Counted(pe)
            pe.wait_ge(wo_l, 16)
            pe.wait_ge(sel_r, 1)
            pe.sem_inc(bc_f, 2)
            pe.sem_inc(ep_f, 2)
            pe.sem_inc(yo_r, 1)

            def broadcast(i, n):
                if n == 0:
                    c.wait(b_l, 16)
                    pe.sem_inc(in_c, 1)
                c.wait(bc_f)
                for j in range(2):
                    r = j * NS + n
                    mm = pe.matmul(bc[:, (n % 2) * 2 + j, 0:TC], sel[:, r:r + 1].to_broadcast([96, P]),
                                   dbs[:, bass.ds(i & 1, 1), :].rearrange("p a t -> p (a t)"), start=True, stop=True)
                mm.then_inc(bc_r, 1)

            def add_states(m):
                c.wait(hs_r)
                if m == 0:
                    c.wait(yo_r)
                for h in range(2):
                    mm = pe.matmul(ys[:, h, 0:TC], K.ident[:, :], hs[:, m % 2, h, :], start=(m == 0), stop=(m == GPC - 1))
                if m == GPC - 1:
                    mm.then_inc(ys_r, 1)

            def sum_tiles(g, tiles):
                if 0 in tiles:
                    c.wait(pm_r)
                for k in tiles:
                    c.wait(ep_f)
                    pe.matmul(ep[:, (g * GRP + k) % 2, 0:ROW], mask[:, g % 2, k, :], pay[:, g % RING, k, :],
                              start=True, stop=True).then_inc(ep_r, 1)

            def out_rows(blocks):
                if 0 in blocks:
                    c.wait(yT_r)
                for j in blocks:
                    for h in range(2):
                        mm = pe.matmul(ys[0:TB, j // 2, (j % 2) * D:(j % 2 + 1) * D], yT[:, h, j * TB:(j + 1) * TB], wo[:, h, :],
                                       start=(h == 0), stop=(h == 1))
                if NB - 1 in blocks:
                    mm.then_inc(yp_r, 1)

            def body(i, first):
                for n in range(NS):
                    g = n // 2
                    if n % 2:
                        sum_tiles(g, range(early // 2))
                    elif n or not first:
                        sum_tiles((g - 1) % GPC, range(early, GRP))
                    if n == 4:
                        add_states(0)
                    if n + 1 < NS:
                        broadcast(i, n + 1)
                    else:
                        broadcast(i + 1, 0)
                    if n % 2:
                        sum_tiles(g, range(early // 2, early))
                        if n == 1 and not first:
                            add_states(GPC - 1)
                        elif n > 3:
                            add_states((n - 3) // 2)
                    if n in (2, 3) and not first:
                        out_rows(range((n - 2) * 2, (n - 1) * 2))

            broadcast(0, 0)
            chunks(pe, body, c.turn)
            add_states(GPC - 1)
            sum_tiles(GPC - 1, range(early, GRP))
            out_rows(range(NB))
            c.turn()

        @block.scalar
        def _(act):
            c = Counted(act)
            ch = Chain(act, ach)
            act.wait_ge(al_l, 16)
            act.activation(a_pos[:, :, :], a_log[:, :, :], ACT.Exp).then_inc(a_r, 1)
            act.wait_ge(a_r, 2)
            act.sem_inc(da_f, 2)
            act.sem_inc(yo_w, 16)
            act.sem_inc(ob_w[0], 16)
            act.sem_inc(ob_w[1], 16)

            def decay(i, n):
                if n == 0:
                    c.wait(dt_l, 16)
                    act.sem_inc(in_c, 1)
                c.wait(da_f)
                for h in range(2):
                    act.activation(da[:, (n % 2) * 2 + h, :], dt[:, bass.ds((i & 1) * 2 + h, 1), :].rearrange("p a t -> p (a t)"),
                                   ACT.Exp, scale=a_neg[:, h, n:n + 1]).then_inc(da_r, 1)

            def weights(g):
                c.wait(d_r)
                act.activation(wexp[:, g % 2, :, :], wexp[:, g % 2, :, :], ACT.Exp).then_inc(w_r, 1)

            def leave(t0, g, tiles):
                if 0 in tiles:
                    c.wait(ob_w[g % 2], 16)
                for k in tiles:
                    c.wait(ep_r)
                    ch.step(act.activation(ob[:, g % 2, k, :], ep[:, (g * GRP + k) % 2, 0:ROW], ACT.Copy))
                    act.sem_inc(ep_f, 1)
                if GRP - 1 in tiles:
                    act.sem_inc(pay_f, 1)
                    act.dma_start(rows(A["agg_d"])[:, bass.ds(t0, GRP), :], ob[:, g % 2, :, :]).then_inc(ob_w[g % 2], 16)

            def leave_rows(i):
                c.wait(yp_r)
                c.wait(yo_w, 16)
                ch.step(act.activation(yo[:, :, :].rearrange("p (a b) d -> p a (b d)", a=2), ys[0:TB, :, :], ACT.Copy))
                act.sem_inc(yo_r, 1)
                act.dma_start(rows(A["ym_d"], TB)[:, bass.ds(i * NB, NB), :], yo[:, :, :]).then_inc(yo_w, 16)

            def turn():
                ch.restart()
                c.turn()

            def body(i, first):
                t0 = i * (GPC * GRP)
                decay(i, 0)
                for n in range(NS):
                    g = n // 2
                    if n % 2 == 0:
                        weights(g)
                    if n + 1 < NS:
                        decay(i, n + 1)
                    if n == 4 and not first:
                        leave_rows(i - 1)
                    if n % 2:
                        leave(t0 + g * GRP, g, range(early))
                    elif n or not first:
                        leave(t0 + (g - 1) * GRP, (g - 1) % GPC, range(early, GRP))

            chunks(act, body, turn)
            c.wait(dt_l, 16)
            leave(ET - GRP, GPC - 1, range(early, GRP))
            leave_rows(NCH - 1)
            turn()
            act.wait_ge(yo_w, 16)
            for s in range(2):
                act.wait_ge(ob_w[s], 16)

        @block.vector
        def _(dve):
            c = Counted(dve)
            ch = Chain(dve, dch)
            dve.wait_ge(a_r, 1)
            dve.tensor_scalar(a_neg[:, :, :], a_pos[:, :, :], -1.0, None, ALU.mult).then_inc(a_r, 1)
            ch.mark(dve.memset(state[:, :, :], 0.0))
            ch.mark(dve.memset(emax[:, :, :], -HUGE))
            ch.step(dve.tensor_tensor(sel32[:, :], K.ident[0:96, 0:32], K.ident[0:96, 32:64], ALU.add))
            ch.step(dve.tensor_tensor(sel[:, :], sel32[:, :], K.ident[0:96, 64:96], ALU.add))
            dve.sem_inc(sel_r, 1)
            dve.wait_ge(ix_l, 32)
            ch.mark(dve.tensor_copy(tgt[:, :], tgt_i[:, :]))
            ch.restart()
            dve.sem_inc(el_f, 2)
            dve.sem_inc(in_f, 1)
            dve.sem_inc(szq_f, 1)

            def arrived(i, g):
                dve.wait_ge(gat[g % RING], i * (2 * GRP * 16) + (g // RING + 1) * GRP * 16)
                c.wait(el[g % 2], 32)

            def weigh(i, g):
                s = g % 2
                c.wait(w_r)
                heads = pay[:, g % RING, :, 0:D].rearrange("p t (h f) -> p t h f", h=HEADS)
                ch.mark(dve.tensor_tensor(heads, heads, wexp[:, s, :, :].unsqueeze(3).to_broadcast([P, GRP, HEADS, FOUT]), ALU.mult))
                ch.mark(dve.tensor_copy(pay[:, g % RING, :, D:ROW], wexp[:, s, :, :]))
                cols = tgt[:, bass.ds(i * (GPC * GRP) + g * GRP, GRP)]
                ch.mark(dve.tensor_tensor(mask[:, s, :, :], trow[:, s, :].rearrange("p (t q) -> p t q", q=P),
                                          cols.unsqueeze(2).to_broadcast([P, GRP, P]), ALU.is_equal))
                ch.wait()
                dve.sem_inc(pm_r, 1)
                dve.sem_inc(el_f, 1)

            def keep_and_read(n):
                ch.mark(dve.tensor_copy(state[:, n, :], hh[:, n % 2, :, TC - 1]))
                ch.mark(dve.tensor_tensor(hc[:, n // 2 % 2, n % 2, :, :], hh[:, n % 2, :, :],
                                          bc[:, (n % 2) * 2 + 1, 0:TC].unsqueeze(1).to_broadcast([P, 2, TC]), ALU.mult))
                return ch.n

            def output():
                c.wait(ys_r)
                c.wait(szq_l, 16)
                ch.step(dve.tensor_tensor(yT[:, :, :], ys[:, :, 0:TC], szq[:, 0:2, :], ALU.mult))
                ch.step(dve.tensor_tensor(yT[:, :, :], yT[:, :, :], szq[:, 2:4, :], ALU.add))
                dve.sem_inc(yT_r, 1)
                dve.sem_inc(szq_f, 1)

            def body(i, first):
                scanned = 0
                for n in range(NS):
                    g = n // 2
                    s, q = g % 2, n % 2
                    if q == 0:
                        arrived(i, g)
                        ch.mark(dve.tensor_tensor(z[:, :, :], pay[:, g % RING, :, D:ROW], tc[:, s, :, 0:HEADS], ALU.add))
                        z_at = ch.n
                    if n == 0:
                        c.wait(u_l, 16)
                        dve.sem_inc(in_c, 1)
                    c.wait(bc_r)
                    ch.mark(dve.tensor_tensor(dbx[:, q, :, :], u[:, half(i), :], bc[:, q * 2, 0:TC].unsqueeze(1).to_broadcast([P, 2, TC]), ALU.mult))
                    dbx_at = ch.n
                    if q == 0:
                        ch.after(z_at)
                        ch.mark(dve.scalar_tensor_tensor(out=z[:, :, :], in0=z[:, :, :], scalar=0.2, in1=z[:, :, :],
                                                         op0=ALU.mult, op1=ALU.max))
                        z_at = ch.n
                    read_at = 0
                    if n or not first:
                        if n:
                            ch.after(scanned)
                            dve.sem_inc(da_f, 1)
                        read_at = keep_and_read((n - 1) % NS)
                    if q == 0:
                        ch.after(z_at)
                        dve.tensor_tensor(wexp[:, s, :, :], z[:, :, :], tc[:, s, :, HEADS:2 * HEADS], ALU.subtract).then_inc(d_r, 1)
                        ch.mark(dve.tensor_tensor(emax[:, :, :], emax[:, :, :], z[:, :, :], ALU.max))
                    c.wait(da_r, 2)
                    for h in range(2):
                        ch.after(dbx_at)
                        ch.mark(dve.tensor_tensor_scan(hh[:, q, h, :], da[:, q * 2 + h, :], dbx[:, q, h, :],
                                                       state[:, n, h:h + 1], ALU.mult, ALU.add))
                        if h == 0 and read_at:
                            ch.after(read_at)
                            dve.sem_inc(bc_f, 1)
                            dve.sem_inc(hc_r, 1)
                    scanned = ch.n
                    if q == 0:
                        weigh(i, g)
                    if n == 2 and not first:
                        output()
                ch.after(scanned)
                dve.sem_inc(da_f, 1)
                dve.sem_inc(in_f, 1)

            def turn():
                ch.restart()
                c.turn()

            chunks(dve, body, turn)
            ch.after(keep_and_read(NS - 1))
            dve.sem_inc(bc_f, 1)
            dve.sem_inc(hc_r, 1)
            output()
            c.wait(u_l, 16)
            c.turn()
            ch.step(dve.tensor_reduce(em1[:, :], emax[:, :, :], AX.XY, ALU.max))
            dve.sem_inc(em_r, 1)
            ch.restart()


def combine_nodes(nc, A, K):
    TOK = GRP * P
    HT = TOK // 2
    SPILL = ET // GRP
    assert SPILL <= P
    with ExitStack() as ctx:
        ph = Phase(nc, "com", ctx)
        fi = ph.sb("fi", [SPILL, GRP, 2], I32)
        ff = ph.sb("ff", [SPILL, GRP])
        cont = ph.sb("cont", [SPILL, GRP])
        frow = ph.sb("frow", [SPILL, GRP, ROW])
        first_i = ph.sb("first_i", [SPILL, ET], I32)
        equal = ph.sb("equal", [SPILL, GRP, ET])
        srow = ph.sb("srow", [SPILL, GRP, ROW])
        zrow = ph.sb("zrow", [1, ROW])
        cb = ph.sb("cb", [P, NT, HEADS])
        eps = ph.sb("eps", [P, NT, HEADS])
        vec = ph.sb("vec", [P, 8, D])
        gb = ph.sb("gb", [P, EX])
        f1b = ph.sb("f1b", [P, 4])
        wl = ph.sb("wl", [P, 2, D])
        wg = ph.sb("wg", [P, 2, D])
        w1 = ph.sb("w1", [P, 2, 2 * D])
        w2 = ph.sb("w2", [P, 4, D])
        gw = ph.sb("gw", [P, 2, EX])
        ids = ph.sb("ids", [P, 3, GRP], I32)
        agg = ph.sb("agg", [P, GRP, ROW])
        spl = ph.sb("spl", [P, GRP, ROW])
        yg = ph.sb("yg", [P, GRP, D])
        xn = ph.sb("xn", [P, GRP, D])
        x = ph.sb("x", [P, GRP, D])
        tmp = ph.sb("tmp", [P, GRP, D])
        hl = ph.sb("hl", [P, GRP, D])
        ha = ph.sb("ha", [P, GRP, D])
        gt = ph.sb("gt", [P, GRP, D])
        h = ph.sb("h", [P, GRP, D])
        fo = ph.sb("fo", [P, GRP, D])
        hT = ph.sb("hT", [P, 2, 4, P])
        tT = ph.sb("tT", [P, 2, TOK])
        fT = ph.sb("fT", [P, 4, TOK])
        rec = ph.sb("rec", [P, GRP, HEADS])
        st = ph.sb("st", [P, GRP, 6])
        mva = ph.sb("mva", [P, GRP, 2])
        mvl = ph.sb("mvl", [P, GRP, 2])
        mvb = ph.sb("mvb", [P, GRP, 2])
        rsa = ph.sb("rsa", [P, GRP])
        rsl = ph.sb("rsl", [P, GRP])
        rsb = ph.sb("rsb", [P, GRP])
        lg = ph.sb("lg", [P, GRP, EX])
        m8 = ph.sb("m8", [P, GRP, 8])
        i8 = ph.sb("i8", [P, GRP, 8], mybir.dt.uint32)
        i2 = ph.sb("i2", [P, GRP, 2])
        spp = ph.ps("spp", [P, 2, 512])
        tr = ph.ps("tr", [P, 2, 4, P])
        gp = ph.ps("gp", [P, 2, 512])
        fp = ph.ps("fp", [P, 2, 512])
        cl, vl, wld, ep1, ep2 = ph.sems("cl vl wld ep1 ep2")
        ag, ygs, sg, eq_r, sp_r, sp_f, sr_r, sr_w, zr_r = ph.sems("ag ygs sg eq_r sp_r sp_f sr_r sr_w zr_r")
        xn_l, xn_f, x_l, x_f, g_f, sta, rsa_r, na_r, ga_r, stl, rsl_r, nl_r, gl_pe, gl_v, stb, rsb_r = ph.sems(
            "xn_l xn_f x_l x_f g_f sta rsa_r na_r ga_r stl rsl_r nl_r gl_pe gl_v stb rsb_r")
        mn_r, el_r, tr_r, tr_f, hT_r, gp_r, gp_f, gt_r, h_r, tT_r, fp_r, fp_f, fT_r, fo_r, xm_pe, x1_sp, xm_sp, lg_r = ph.sems(
            "mn_r el_r tr_r tr_f hT_r gp_r gp_f gt_r h_r tT_r fp_r fp_f fT_r fo_r xm_pe x1_sp xm_sp lg_r")
        x1_w, xm_w, dch, ach, pch = ph.sems("x1_w xm_w dch ach pch")
        block = ph.block()
        tiles = range(GRP)

        def passes(eng, first, mid, mix, rest, turn):
            first(0)
            mid(0)
            turn()
            with eng.Fori(0, NG - 1) as g:
                mix(g)
                first(g + 1)
                mid(g + 1)
                rest(g)
                turn()
            mix(NG - 1)
            rest(NG - 1)
            turn()

        def nothing(g):
            pass

        def group(g):
            return bass.ds(g * GRP, GRP)

        @block.sync
        def _(sp):
            c = Counted(sp)
            sp.dma_start(fi[:, :, 0], bass.AP(A["dst"].tensor, 0, [[P, SPILL], [P * SPILL, GRP]]), allow_slow_non_contiguous=True).then_inc(cl, 16)
            sp.dma_start(fi[:, :, 1], bass.AP(A["dprev"].tensor, 0, [[P, SPILL], [P * SPILL, GRP]]), allow_slow_non_contiguous=True).then_inc(cl, 16)
            sp.dma_start(frow[:, :, :], bass.AP(A["agg_d"].tensor, 0, [[P * ROW, SPILL], [P * SPILL * ROW, GRP], [1, ROW]])).then_inc(cl, 16)
            sp.dma_start(first_i[:, :], spread(A["first_d"], ET, SPILL)).then_inc(cl, 16)
            for j, v in enumerate((A["gat_b"], A["lnl_g"], A["lnl_b"], A["lng_g"], A["lng_b"], A["ff2_b"], A["ln2_g"], A["ln2_b"])):
                sp.dma_start(vec[:, j, :], spread(v, D)).then_inc(vl, 16)
            sp.dma_start(gb[:, :], spread(A["gate_b"], EX)).then_inc(vl, 16)
            sp.dma_start(f1b[:, :], A["ff1_b"].rearrange("(m p) -> p m", p=P), allow_slow_non_contiguous=True).then_inc(wld, 16)
            for t, w in ((wl, A["wlT"]), (wg, A["wgT"]), (w1, A["ff1_wT"]), (w2, A["ff2_wT"]), (gw, A["gate_w"])):
                sp.dma_start(t[:, :, :], w.rearrange("(c p) f -> p c f", p=P)).then_inc(wld, 16)

            sp.wait_ge(zr_r, 1)
            sp.dma_start(A["spill_d"][ET:ET + 1, :], zrow[:, :]).then_inc(sr_w, 16)
            sp.wait_ge(sr_r, 1)
            sp.dma_start(A["spill_d"][0:ET, :].rearrange("(a p) d -> p a d", p=SPILL), srow[:, :, :]).then_inc(sr_w, 16)

            def load_xn(g):
                c.wait(xn_f)
                sp.dma_start(xn[:, :, :], rows(A["xn_d"])[:, group(g), :]).then_inc(xn_l, 16)

            def load_x(g):
                c.wait(x_f)
                sp.dma_start(x[:, :, :], rows(A["x"])[:, group(g), :]).then_inc(x_l, 16)

            def store(g):
                c.wait(x1_sp)
                sp.dma_start(rows(A["x1_d"])[:, group(g), :], x[:, :, :]).then_inc(x1_w, 16)
                c.wait(xm_sp)
                sp.dma_start(rows(A["xm_d"])[:, group(g), :], fo[:, :, :]).then_inc(xm_w, 16)

            passes(sp, load_xn, nothing, load_x, store, c.turn)

        @block.gpsimd
        def _(pool):
            c = Counted(pool)
            ch = Chain(pool, pch)
            pool.wait_ge(vl, 16 * 9)

            def scaled(t, gain, bias):
                for j, op in ((gain, ALU.mult), (bias, ALU.add)):
                    ch.step(pool.tensor_tensor(t[:, :, :], t[:, :, :], vec[:, j, :].unsqueeze(1).to_broadcast([P, GRP, D]), op))

            def first(g):
                c.wait(g_f)
                ch.mark(pool.tensor_copy(ids[:, 0, :], K.start[:, group(g)]))
                ch.mark(pool.tensor_copy(ids[:, 1, :], K.rank[:, group(g)]))
                ch.mark(pool.tensor_copy(ids[:, 2, :], K.spill[:, group(g)]))
                ch.wait()
                for k in tiles:
                    pool.indirect_dma_start(yg[:, k, :], None, A["ym_d"], bass.IndirectOffsetOnAxis(ids[:, 1, k:k + 1], 0)).then_inc(ygs, 16)
                for k in tiles:
                    pool.indirect_dma_start(agg[:, k, :], None, A["agg_d"], bass.IndirectOffsetOnAxis(ids[:, 0, k:k + 1], 0)).then_inc(ag, 16)
                pool.wait_ge(sr_w, 32)
                for k in tiles:
                    pool.indirect_dma_start(spl[:, k, :], None, A["spill_d"], bass.IndirectOffsetOnAxis(ids[:, 2, k:k + 1], 0)).then_inc(sg, 16)
                c.wait(sta)
                inverse_deviation(pool, ch, K, rsa[:, :], mva[:, :, 1])
                pool.sem_inc(rsa_r, 1)
                c.wait(na_r)
                scaled(ha, 3, 4)
                c.wait(stl)
                inverse_deviation(pool, ch, K, rsl[:, :], mvl[:, :, 1])
                pool.sem_inc(rsl_r, 1)
                c.wait(nl_r)
                scaled(hl, 1, 2)
                pool.sem_inc(gl_pe, 1)
                pool.sem_inc(gl_v, 1)

            def rest(g):
                for _ in range(2):
                    c.wait(stb)
                    inverse_deviation(pool, ch, K, rsb[:, :], mvb[:, :, 1])
                    pool.sem_inc(rsb_r, 1)

            def turn():
                ch.restart()
                c.turn()

            passes(pool, first, nothing, nothing, rest, turn)

        @block.tensor
        def _(pe):
            c = Counted(pe)
            pe.wait_ge(wld, 16 * 6)
            pe.sem_inc(tr_f, 2)
            pe.sem_inc(gp_f, 2)
            pe.sem_inc(fp_f, 2)

            pe.wait_ge(eq_r, 1)
            pe.sem_inc(sp_f, 2)
            for a in range(GRP):
                c.wait(sp_f)
                for j in range(GRP):
                    mm = pe.matmul(spp[0:SPILL, a % 2, 0:ROW], equal[:, j, a * SPILL:(a + 1) * SPILL], frow[:, j, :],
                                   start=(j == 0), stop=(j == GRP - 1))
                mm.then_inc(sp_r, 1)
            c.turn()

            def turned(parts, s):
                c.wait(tr_f)
                for j, part in enumerate(parts):
                    t = pe.transpose(tr[:, s, j, :], part, K.ident[:, :])
                t.then_inc(tr_r, 1)

            def both(k):
                turned([t[:, k, j * P:(j + 1) * P] for t in (hl, ha) for j in range(2)], k % 2)

            def gate(g):
                c.wait(gl_pe)
                both(0)
                for k in tiles:
                    if k + 1 < GRP:
                        both(k + 1)
                    c.wait(hT_r)
                    c.wait(gp_f)
                    for j in range(4):
                        mm = pe.matmul(gp[:, k % 2, 0:D], hT[:, k % 2, j, :], (wl if j < 2 else wg)[:, j % 2, :], start=(j == 0), stop=(j == 3))
                    mm.then_inc(gp_r, 1)

            def forward(g):
                c.wait(h_r)
                for k in tiles:
                    turned([h[:, k, j * P:(j + 1) * P] for j in range(2)], k % 2)
                c.wait(tT_r, GRP)
                for m in range(4):
                    for s in range(2):
                        c.wait(fp_f)
                        for j in range(2):
                            mm = pe.matmul(fp[:, s, 0:HT], w1[:, j, m * P:(m + 1) * P], tT[:, j, s * HT:(s + 1) * HT], start=(j == 0), stop=(j == 1))
                        mm.then_inc(fp_r, 1)
                c.wait(fT_r, 8)
                for k in tiles:
                    c.wait(gp_f)
                    for m in range(4):
                        mm = pe.matmul(gp[:, k % 2, 0:D], fT[:, m, k * P:(k + 1) * P], w2[:, m, :], start=(m == 0), stop=(m == 3))
                    mm.then_inc(gp_r, 1)

            def logits(g):
                c.wait(xm_pe)
                for k in tiles:
                    turned([fo[:, k, j * P:(j + 1) * P] for j in range(2)], k % 2)
                c.wait(tT_r, GRP)
                for k in tiles:
                    for j in range(2):
                        mm = pe.matmul(fp[:, 0, k * EX:(k + 1) * EX], tT[:, j, k * P:(k + 1) * P], gw[:, j, :], start=(j == 0), stop=(j == 1))
                mm.then_inc(lg_r, 1)

            passes(pe, nothing, gate, forward, logits, c.turn)

        @block.scalar
        def _(act):
            c = Counted(act)
            ch = Chain(act, ach)
            act.wait_ge(wld, 16 * 6)
            act.wait_ge(ep1, 1)
            ch.step(act.activation(eps[:, :, :], cb[:, :, :], ACT.Exp))
            act.sem_inc(ep2, 1)
            for a in range(GRP):
                c.wait(sp_r)
                ch.step(act.activation(srow[:, a, :], spp[0:SPILL, a % 2, 0:ROW], ACT.Copy))
                act.sem_inc(sp_f, 1)
            act.sem_inc(sr_r, 1)
            c.turn()

            def elu(g):
                c.wait(mn_r)
                act.activation(tmp[:, :, :], tmp[:, :, :], ACT.Exp).then_inc(el_r, 1)

            def gate(g):
                def leave(k):
                    c.wait(tr_r)
                    ch.step(act.activation(hT[:, k % 2, :, :], tr[:, k % 2, :, :], ACT.Copy))
                    act.sem_inc(tr_f, 1)
                    act.sem_inc(hT_r, 1)

                leave(0)
                for k in tiles:
                    if k + 1 < GRP:
                        leave(k + 1)
                    c.wait(gp_r)
                    ch.step(act.activation(gt[:, k, :], gp[:, k % 2, 0:D], ACT.Sigmoid))
                    act.sem_inc(gp_f, 1)
                act.sem_inc(gt_r, 1)

            def leave_pairs():
                for k in tiles:
                    c.wait(tr_r)
                    ch.step(act.activation(tT[:, :, k * P:(k + 1) * P], tr[:, k % 2, 0:2, :], ACT.Copy))
                    act.sem_inc(tr_f, 1)
                    act.sem_inc(tT_r, 1)

            def forward(g):
                leave_pairs()
                for m in range(4):
                    for s in range(2):
                        c.wait(fp_r)
                        ch.step(act.activation(fT[:, m, s * HT:(s + 1) * HT], fp[:, s, 0:HT], ACT.Relu, bias=f1b[:, m:m + 1]))
                        act.sem_inc(fp_f, 1)
                        act.sem_inc(fT_r, 1)
                for k in tiles:
                    c.wait(gp_r)
                    if k == 0:
                        c.wait(xm_w, 16)
                    ch.step(act.activation(fo[:, k, :], gp[:, k % 2, 0:D], ACT.Copy))
                    act.sem_inc(gp_f, 1)
                act.sem_inc(fo_r, 1)

            def logits(g):
                leave_pairs()

            def turn():
                ch.restart()
                c.turn()

            act.sem_inc(xm_w, 16)
            passes(act, elu, gate, forward, logits, turn)
            act.wait_ge(xm_w, 16)

        @block.vector
        def _(dve):
            c = Counted(dve)
            ch = Chain(dve, dch)
            ch.step(dve.memset(zrow[:, :], 0.0))
            dve.sem_inc(zr_r, 1)
            dve.wait_ge(cl, 64)
            ch.step(dve.tensor_tensor(cont[:, :], fi[:, :, 0], fi[:, :, 1], ALU.is_equal))
            ch.step(dve.tensor_copy(ff[:, :], fi[:, :, 0]))
            ch.step(dve.scalar_tensor_tensor(out=ff[:, :], in0=ff[:, :], scalar=1.0, in1=cont[:, :], op0=ALU.add, op1=ALU.mult))
            ch.step(dve.tensor_scalar(ff[:, :], ff[:, :], -1.0, None, ALU.add))
            for j in range(GRP):
                ch.mark(dve.tensor_scalar(equal[:, j, :], first_i[:, :], ff[:, j:j + 1], None, ALU.is_equal))
            ch.wait()
            dve.sem_inc(eq_r, 1)
            for q in range(HEADS):
                ch.mark(dve.tensor_scalar(cb[:, :, q], K.s_all[:, :, HEADS + q], K.top_src[:, q:q + 1], None, ALU.add))
            ch.wait()
            ch.step(dve.scalar_tensor_tensor(out=cb[:, :, :], in0=cb[:, :, :], scalar=0.2, in1=cb[:, :, :], op0=ALU.mult, op1=ALU.max))
            ch.step(dve.tensor_scalar(cb[:, :, :], cb[:, :, :], -1.0, K.top_e[:, 0:1], ALU.mult, ALU.add))
            ch.step(dve.tensor_scalar(cb[:, :, :], cb[:, :, :], 80.0, None, ALU.min))
            dve.sem_inc(ep1, 1)
            dve.wait_ge(ep2, 1)
            ch.step(dve.tensor_scalar(eps[:, :, :], eps[:, :, :], DEN_EPS, 1e-37, ALU.mult, ALU.max))
            ch.restart()
            dve.wait_ge(vl, 16 * 9)
            dve.sem_inc(xn_f, 1)
            dve.sem_inc(x_f, 1)
            dve.sem_inc(g_f, 1)
            dve.sem_inc(x1_w, 16)

            def row(j):
                return vec[:, j, :].unsqueeze(1).to_broadcast([P, GRP, D])

            def stats(t, mv, sem):
                for k in tiles:
                    ch.mark(dve.bn_stats(st[:, k, :], t[:, k, :]))
                ch.wait()
                for k in tiles:
                    ch.mark(dve.bn_aggr(mv[:, k, :], st[:, k, :]))
                ch.wait()
                dve.sem_inc(sem, 1)

            def normed(out, t, mv, rs):
                for k in tiles:
                    ch.mark(dve.tensor_scalar(out[:, k, :], t[:, k, :], mv[:, k, 0:1], rs[:, k:k + 1], ALU.subtract, ALU.mult))
                ch.wait()

            def first(g):
                c.wait(xn_l, 16)
                dve.wait_ge(ygs, g * (16 * GRP) + 16 * GRP)
                ch.step(dve.tensor_tensor(ha[:, :, :], yg[:, :, :], xn[:, :, :], ALU.add))
                stats(ha, mva, sta)
                c.wait(rsa_r)
                normed(ha, ha, mva, rsa)
                dve.sem_inc(na_r, 1)
                dve.wait_ge(ag, g * (16 * GRP) + 16 * GRP)

                dve.wait_ge(sg, g * (16 * GRP) + 16 * GRP)
                for k in tiles:
                    ch.mark(dve.scalar_tensor_tensor(out=agg[:, k, :], in0=agg[:, k, :], scalar=K.some[:, bass.ds(g * GRP + k, 1)],
                                                     in1=spl[:, k, :], op0=ALU.mult, op1=ALU.add))
                ch.wait()
                ch.step(dve.tensor_tensor(rec[:, :, :], agg[:, :, D:ROW], eps[:, group(g), :], ALU.add))
                ch.step(dve.reciprocal(rec[:, :, :], rec[:, :, :]))
                ch.step(dve.tensor_tensor(hl[:, :, :].rearrange("p t (q f) -> p t q f", q=HEADS),
                                          agg[:, :, 0:D].rearrange("p t (q f) -> p t q f", q=HEADS),
                                          rec[:, :, :].unsqueeze(3).to_broadcast([P, GRP, HEADS, FOUT]), ALU.mult))
                dve.sem_inc(g_f, 1)
                ch.step(dve.tensor_tensor(hl[:, :, :], hl[:, :, :], xn[:, :, :], ALU.add))
                dve.sem_inc(xn_f, 1)
                ch.step(dve.tensor_tensor(hl[:, :, :], hl[:, :, :], row(0), ALU.add))
                ch.step(dve.tensor_scalar(tmp[:, :, :], hl[:, :, :], 0.0, None, ALU.min))
                dve.sem_inc(mn_r, 1)
                ch.step(dve.tensor_scalar(hl[:, :, :], hl[:, :, :], 0.0, -1.0, ALU.max, ALU.add))
                c.wait(el_r)
                ch.step(dve.tensor_tensor(hl[:, :, :], hl[:, :, :], tmp[:, :, :], ALU.add))
                stats(hl, mvl, stl)
                c.wait(rsl_r)
                normed(hl, hl, mvl, rsl)
                dve.sem_inc(nl_r, 1)

            def mix(g):
                c.wait(gl_v)
                c.wait(gt_r)
                ch.step(dve.tensor_tensor(h[:, :, :], hl[:, :, :], ha[:, :, :], ALU.subtract))
                ch.step(dve.tensor_tensor(h[:, :, :], h[:, :, :], gt[:, :, :], ALU.mult))
                ch.step(dve.tensor_tensor(h[:, :, :], h[:, :, :], ha[:, :, :], ALU.add))
                dve.sem_inc(h_r, 1)

            def rest(g):
                c.wait(fo_r)
                ch.step(dve.tensor_tensor(h[:, :, :], h[:, :, :], fo[:, :, :], ALU.add))
                ch.step(dve.tensor_tensor(h[:, :, :], h[:, :, :], row(5), ALU.add))
                stats(h, mvb, stb)
                c.wait(rsb_r)
                normed(h, h, mvb, rsb)
                ch.step(dve.tensor_tensor(h[:, :, :], h[:, :, :], row(6), ALU.mult))
                ch.step(dve.tensor_tensor(h[:, :, :], h[:, :, :], row(7), ALU.add))
                c.wait(x_l, 16)
                ch.step(dve.tensor_tensor(x[:, :, :], x[:, :, :], h[:, :, :], ALU.add))
                dve.sem_inc(x1_sp, 1)
                stats(x, mvb, stb)
                c.wait(rsb_r)
                normed(fo, x, mvb, rsb)
                dve.sem_inc(xm_pe, 1)
                dve.sem_inc(xm_sp, 1)
                c.wait(lg_r)
                ch.step(dve.tensor_tensor(lg[:, :, :], fp[:, 0, 0:GRP * EX].rearrange("p (t e) -> p t e", e=EX),
                                          gb[:, :].unsqueeze(1).to_broadcast([P, GRP, EX]), ALU.add))
                for k in tiles:
                    ch.mark(dve.max(m8[:, k, :], lg[:, k, :]))
                ch.wait()
                for k in tiles:
                    ch.mark(dve.max_index(i8[:, k, :], m8[:, k, :], lg[:, k, :]))
                ch.wait()
                ch.mark(dve.tensor_tensor(K.gap[:, group(g)], m8[:, :, 1], m8[:, :, 0], ALU.subtract))
                ch.step(dve.tensor_copy(i2[:, :, :], i8[:, :, 0:2]))
                ch.step(dve.tensor_tensor(K.hot[:, group(g), :, :], K.iota[:, 0:EX].unsqueeze(1).unsqueeze(1).to_broadcast([P, GRP, 2, EX]),
                                          i2[:, :, :].unsqueeze(3).to_broadcast([P, GRP, 2, EX]), ALU.is_equal))
                c.wait(x1_w, 16)
                dve.sem_inc(x_f, 1)

            def turn():
                ch.restart()
                c.turn()

            dve.sem_inc(x1_w, -16)
            passes(dve, first, nothing, mix, rest, turn)


def dispatch(nc, A, K):
    with ExitStack() as ctx:
        ph = Phase(nc, "dis", ctx)
        xm = ph.sb("xm", [P, NT, D])
        zero = ph.sb("zero", [P, 2048])
        osum = ph.sb("osum", [P, NT, EX])
        tot = ph.sb("tot", [P, NT, EX])
        pos = ph.sb("pos", [P, NT, EX])
        sel = ph.sb("sel", [P, NT, EX])
        two = ph.sb("two", [P, 2, NT])
        inc = ph.sb("inc", [P, EX])
        pad = ph.sb("pad", [P, EX])
        pad_i = ph.sb("pad_i", [P, EX], I32)
        offi = ph.sb("offi", [P, EX])
        one = ph.sb("one", [P, P])
        tj_i = ph.sb("tj_i", [P, MT], I32)
        tj = ph.sb("tj", [P, MT])
        te = ph.sb("te", [P, MT, EX])
        ti = ph.sb("ti", [P, MT])
        e1 = ph.sb("e1", [P, NT])
        wi = ph.ps("wi", [P, 2, 512])
        to = ph.ps("to", [P, 2, 512])
        xl, zr, zw, tj_r, os_r, mm_r, ps_r, ex_r, sc, dch, ach, pch = ph.sems("xl zr zw tj_r os_r mm_r ps_r ex_r sc dch ach pch")
        block = ph.block()
        halves_ = [(0, 25), (25, NT)]
        whole = MT * P * D // (P * 2048)

        @block.sync
        def _(sp):
            sp.dma_start(xm[:, :, :], rows(A["xm_d"])).then_inc(xl, 16)
            sp.wait_ge(zr, 1)
            flat = A["disp_d"].rearrange("r d -> (r d)")
            for j in range(whole):
                sp.dma_start(flat[j * P * 2048:(j + 1) * P * 2048].rearrange("(p f) -> p f", p=P), zero[:, :]).then_inc(zw, 16)
            left = (MT * P * D - whole * P * 2048) // P
            if left:
                sp.dma_start(flat[whole * P * 2048:].rearrange("(p f) -> p f", p=P), zero[:, 0:left]).then_inc(zw, 16)

        stores = whole + (1 if (MT * P * D) % (P * 2048) else 0)

        @block.gpsimd
        def _(pool):
            pool.iota(tj_i[:, :], pattern=[[P, MT]], base=0, channel_multiplier=0).then_inc(tj_r, 1)
            pool.wait_ge(ps_r, 1)
            pool.wait_ge(xl, 16)
            pool.wait_ge(zw, 16 * stores)
            for b in range(NT):
                for q in range(2):
                    pool.indirect_dma_start(A["disp_d"], bass.IndirectOffsetOnAxis(K.pos[:, q, b:b + 1], 0), xm[:, b, :], None).then_inc(sc, 16)
            pool.wait_ge(sc, 16 * 2 * NT)

        @block.tensor
        def _(pe):
            pe.wait_ge(os_r, 1)
            for j, (a, b) in enumerate(halves_):
                pe.matmul(wi[:, j, 0:(b - a) * EX], K.upper[:, :], osum[:, a:b, :].rearrange("p t e -> p (t e)"), start=True, stop=True)
                mm = pe.matmul(to[:, j, 0:(b - a) * EX], K.ones[:, :], osum[:, a:b, :].rearrange("p t e -> p (t e)"), start=True, stop=True)
            mm.then_inc(mm_r, 1)

        @block.scalar
        def _(act):
            act.activation(e1[:, :], K.gap[:, :], ACT.Exp).then_inc(ex_r, 1)

        @block.vector
        def _(dve):
            ch = Chain(dve, dch)
            dve.memset(zero[:, :], 0.0).then_inc(zr, 1)
            ch.mark(dve.memset(one[:, :], 1.0))
            ch.step(dve.tensor_tensor(osum[:, :, :], K.hot[:, :, 0, :], K.hot[:, :, 1, :], ALU.add))
            dve.sem_inc(os_r, 1)
            dve.wait_ge(ex_r, 1)
            ch.step(dve.tensor_scalar(K.wts[:, 1, :], e1[:, :], 1.0, None, ALU.add))
            ch.step(dve.reciprocal(K.wts[:, 0, :], K.wts[:, 1, :]))
            ch.step(dve.tensor_tensor(K.wts[:, 1, :], e1[:, :], K.wts[:, 0, :], ALU.mult))
            dve.wait_ge(mm_r, 1)
            for j, (a, b) in enumerate(halves_):
                ch.mark(dve.tensor_copy(tot[:, a:b, :].rearrange("p t e -> p (t e)"), to[:, j, 0:(b - a) * EX]))
            ch.wait()
            for e in range(EX):
                ch.mark(dve.tensor_tensor_scan(pos[:, :, e], one[:, 0:NT], tot[:, :, e], 0.0, ALU.mult, ALU.add))
            ch.wait()
            ch.step(dve.tensor_copy(inc[:, :], pos[:, NT - 1, :]))
            ch.step(dve.tensor_tensor(pos[:, :, :], pos[:, :, :], tot[:, :, :], ALU.subtract))
            for j, (a, b) in enumerate(halves_):
                ch.mark(dve.tensor_tensor(pos[:, a:b, :].rearrange("p t e -> p (t e)"), pos[:, a:b, :].rearrange("p t e -> p (t e)"),
                                     wi[:, j, 0:(b - a) * EX], ALU.add))
            ch.wait()
            ch.step(dve.tensor_scalar(pad[:, :], inc[:, :], float(P - 1), None, ALU.add))
            ch.step(dve.tensor_copy(pad_i[:, :], pad[:, :]))
            ch.step(dve.tensor_scalar(pad_i[:, :], pad_i[:, :], 7, 7, ALU.logical_shift_right, ALU.logical_shift_left))
            ch.step(dve.tensor_copy(pad[:, :], pad_i[:, :]))
            ch.step(dve.tensor_tensor_scan(offi[:, :], one[:, 0:EX], pad[:, :], 0.0, ALU.mult, ALU.add))
            ch.step(dve.tensor_tensor(pad[:, :], offi[:, :], pad[:, :], ALU.subtract))
            ch.step(dve.tensor_tensor(pos[:, :, :], pos[:, :, :], pad[:, :].unsqueeze(1).to_broadcast([P, NT, EX]), ALU.add))
            for q in range(2):
                ch.step(dve.tensor_tensor(sel[:, :, :], pos[:, :, :], K.hot[:, :, q, :], ALU.mult))
                ch.step(dve.tensor_reduce(two[:, q, :], sel[:, :, :], AX.X, ALU.add))
            ch.step(dve.tensor_copy(K.pos[:, :, :], two[:, :, :]))
            dve.sem_inc(ps_r, 1)
            dve.wait_ge(tj_r, 1)
            ch.step(dve.tensor_copy(tj[:, :], tj_i[:, :]))
            ch.step(dve.tensor_tensor(te[:, :, :], tj[:, :].unsqueeze(2).to_broadcast([P, MT, EX]),
                                      offi[:, :].unsqueeze(1).to_broadcast([P, MT, EX]), ALU.is_ge))
            ch.step(dve.tensor_reduce(ti[:, :], te[:, :, :], AX.X, ALU.add))
            ch.step(dve.tensor_scalar(ti[:, :], ti[:, :], float(EX - 1), float(P), ALU.min, ALU.mult))
            ch.step(dve.tensor_scalar(ti[:, :], ti[:, :], K.node[:, 0:1], None, ALU.add))
            ch.step(dve.tensor_copy(K.wrow[:, :], ti[:, :]))
            ch.restart()


def experts(nc, A, K):
    KC, FC = D // P, FF // P
    with ExitStack() as ctx:
        ph = Phase(nc, "exp", ctx)
        ids = ph.sb("ids", [P, 2], I32)
        xt = ph.sb("xt", [P, 2, D])
        w1 = ph.sb("w1", [P, 2, KC * FF])
        w2 = ph.sb("w2", [P, 2, FC * D])
        b1 = ph.sb("b1", [P, 2, FC])
        xT = ph.sb("xT", [P, 2, KC, P])
        hT = ph.sb("hT", [P, 2, FC, P])
        yo = ph.sb("yo", [P, 2, D])
        tr = ph.ps("tr", [P, 2, 512])
        hp = ph.ps("hp", [P, 2, 512])
        op = ph.ps("op", [P, 2, 512])
        xl, wg_, yw = ph.sems("xl0 xl1"), ph.sems("wg0 wg1"), ph.sems("yw0 yw1")
        x_f, w_f, tr_r, xT_r, hp_r, hT_r, op_r, yo_r, ach, dch, pch = ph.sems("x_f w_f tr_r xT_r hp_r hT_r op_r yo_r ach dch pch")
        block = ph.block()
        w1_rows = A["w1"].rearrange("e (p k) f -> (e p) (k f)", k=KC)
        w2_rows = A["w2"].rearrange("e (p k) d -> (e p) (k d)", k=FC)
        b1_rows = A["b1"].rearrange("e (p k) -> (e p) k", k=FC)

        @block.sync
        def _(sp):
            c = Counted(sp)
            with sp.Fori(0, MT // 2) as i:
                for s in range(2):
                    c.wait(x_f)
                    sp.dma_start(xt[:, s, :], rows(A["disp_d"])[:, bass.ds(i * 2 + s, 1), :].rearrange("p a d -> p (a d)")).then_inc(xl[s], 16)
                for s in range(2):
                    c.wait(yo_r)
                    sp.dma_start(rows(A["eout_d"])[:, bass.ds(i * 2 + s, 1), :].rearrange("p a d -> p (a d)"), yo[:, s, :]).then_inc(yw[s], 16)
                c.turn()

        @block.gpsimd
        def _(pool):
            c = Counted(pool)
            ch = Chain(pool, pch)
            pool.sem_inc(w_f, 2)
            with pool.Fori(0, MT // 2) as i:
                for s in range(2):
                    c.wait(w_f)
                    ch.step(pool.tensor_copy(ids[:, s:s + 1], K.wrow[:, bass.ds(i * 2 + s, 1)]))
                    for t, w in ((w1, w1_rows), (w2, w2_rows), (b1, b1_rows)):
                        pool.indirect_dma_start(t[:, s, :], None, w, bass.IndirectOffsetOnAxis(ids[:, s:s + 1], 0)).then_inc(wg_[s], 16)
                ch.restart()
                c.turn()

        @block.tensor
        def _(pe):
            c = Counted(pe)
            pe.sem_inc(x_f, 2)
            with pe.Fori(0, MT // 2) as i:
                def turned(s):
                    c.wait(xl[s], 16)
                    for k in range(KC):
                        t = pe.transpose(tr[:, s, k * P:(k + 1) * P], xt[:, s, :].rearrange("p (q k) -> p k q", k=KC)[:, k, :], K.ident[:, :])
                    t.then_inc(tr_r, 1)

                def up(s):
                    pe.wait_ge(wg_[s], i * 48 + 48)
                    c.wait(xT_r)
                    w = w1[:, s, :].rearrange("p (k q m) -> p k m q", k=KC, m=FC)
                    for m in range(FC):
                        for k in range(KC):
                            mm = pe.matmul(hp[:, s, m * P:(m + 1) * P], w[:, k, m, :], xT[:, s, k, :], start=(k == 0), stop=(k == KC - 1))
                    mm.then_inc(hp_r, 1)

                def down(s):
                    c.wait(hT_r)
                    for m in range(FC):
                        mm = pe.matmul(op[:, s, 0:D], hT[:, s, m, :], w2[:, s, m * D:(m + 1) * D], start=(m == 0), stop=(m == FC - 1))
                    mm.then_inc(op_r, 1)

                turned(0)
                turned(1)
                up(0)
                up(1)
                down(0)
                down(1)
                c.turn()

        @block.scalar
        def _(act):
            c = Counted(act)
            ch = Chain(act, ach)
            with act.Fori(0, MT // 2) as i:
                for s in range(2):
                    c.wait(tr_r)
                    ch.step(act.activation(xT[:, s, :, :], tr[:, s, 0:KC * P].rearrange("p (k q) -> p k q", k=KC), ACT.Copy))
                    act.sem_inc(xT_r, 1)
                    act.sem_inc(x_f, 1)
                for s in range(2):
                    c.wait(hp_r)
                    for m in range(FC):
                        ch.mark(act.activation(hT[:, s, m, :], hp[:, s, m * P:(m + 1) * P], ACT.Relu, bias=b1[:, s, m:m + 1]))
                    ch.wait()
                    act.sem_inc(hT_r, 1)
                ch.restart()
                c.turn()

        @block.vector
        def _(dve):
            c = Counted(dve)
            ch = Chain(dve, dch)
            for s in range(2):
                dve.sem_inc(yw[s], 16)
            with dve.Fori(0, MT // 2) as i:
                for s in range(2):
                    c.wait(op_r)
                    c.wait(yw[s], 16)
                    ch.step(dve.tensor_copy(yo[:, s, :], op[:, s, 0:D]))
                    dve.sem_inc(yo_r, 1)
                    dve.sem_inc(w_f, 1)
                ch.restart()
                c.turn()
            for s in range(2):
                dve.wait_ge(yw[s], 16)


def finish(nc, A, K):
    with ExitStack() as ctx:
        ph = Phase(nc, "fin", ctx)
        ids = ph.sb("ids", [P, 2, GRP], I32)
        e = ph.sb("e", [P, 2, GRP, D])
        xm = ph.sb("xm", [P, GRP, D])
        x1 = ph.sb("x1", [P, GRP, D])
        g = ph.sb("g", [P, NT, EX])
        g1 = ph.sb("g1", [P, NT, EX])
        gs = ph.sb("gs", [P, GRP, EX])
        gT = ph.sb("gT", [EX, 2, P])
        b2 = ph.sb("b2", [EX, D])
        vec = ph.sb("vec", [P, 2, D])
        y = ph.sb("y", [P, GRP, D])
        st = ph.sb("st", [P, GRP, 6])
        mv = ph.sb("mv", [P, GRP, 2])
        rs = ph.sb("rs", [P, GRP])
        tp = ph.ps("tp", [EX, 2, 512])
        bp = ph.ps("bp", [P, 2, 512])
        cl, eg, xm_l, x1_l, in_f, e_f, y_w = ph.sems("cl eg xm_l x1_l in_f e_f y_w")
        g_r, gs_r, tp_r, gT_r, bp_r, bp_f, st_r, rs_r, y_r, dch, pch, ach = ph.sems("g_r gs_r tp_r gT_r bp_r bp_f st_r rs_r y_r dch pch ach")
        block = ph.block()
        tiles = range(GRP)

        @block.sync
        def _(sp):
            c = Counted(sp)
            sp.dma_start(b2[:, :], A["b2"]).then_inc(cl, 16)
            for j, v in enumerate((A["gamma"], A["beta"])):
                sp.dma_start(vec[:, j, :], spread(v, D)).then_inc(cl, 16)

            def load(i):
                c.wait(in_f)
                sp.dma_start(xm[:, :, :], rows(A["xm_d"])[:, bass.ds(i * GRP, GRP), :]).then_inc(xm_l, 16)
                sp.dma_start(x1[:, :, :], rows(A["x1_d"])[:, bass.ds(i * GRP, GRP), :]).then_inc(x1_l, 16)

            with sp.Fori(0, NG - 1) as i:
                load(i)
                c.wait(y_r)
                sp.dma_start(rows(A["out"][0:(NT - 1) * P, :])[:, bass.ds(i * GRP, GRP), :], y[:, :, :]).then_inc(y_w, 16)
                c.turn()
            load(NG - 1)
            c.wait(y_r)
            t0 = (NG - 1) * GRP
            c.turn()
            sp.dma_start(rows(A["out"][t0 * P:(NT - 1) * P, :]), y[:, 0:GRP - 1, :]).then_inc(y_w, 16)
            sp.dma_start(A["out"][(NT - 1) * P:N, :], y[0:NLAST, GRP - 1, :]).then_inc(y_w, 16)

        @block.gpsimd
        def _(pool):
            c = Counted(pool)
            ch = Chain(pool, pch)
            with pool.Fori(0, NG) as i:
                c.wait(e_f)
                ch.step(pool.tensor_copy(ids[:, :, :], K.pos[:, :, bass.ds(i * GRP, GRP)]))
                for q in range(2):
                    for k in tiles:
                        pool.indirect_dma_start(e[:, q, k, :], None, A["eout_d"],
                                                bass.IndirectOffsetOnAxis(ids[:, q, k:k + 1], 0)).then_inc(eg, 16)
                c.wait(st_r)
                inverse_deviation(pool, ch, K, rs[:, :], mv[:, :, 1])
                pool.sem_inc(rs_r, 1)
                ch.restart()
                c.turn()

        @block.tensor
        def _(pe):
            c = Counted(pe)
            pe.wait_ge(cl, 48)
            pe.sem_inc(bp_f, 2)
            with pe.Fori(0, NG):
                c.wait(gs_r)
                for k in tiles:
                    pe.transpose(tp[:, k % 2, 0:P], gs[:, k, :], K.ident[:, :]).then_inc(tp_r, 1)
                    c.wait(gT_r)
                    if k != 1:
                        c.wait(bp_f, 2 if k == 0 else 1)
                    pe.matmul(bp[:, k % 2, 0:D], gT[:, k % 2, :], b2[:, :], start=True, stop=True).then_inc(bp_r, 1)
                c.turn()

        @block.scalar
        def _(act):
            c = Counted(act)
            act.wait_ge(g_r, 1)
            with act.Fori(0, NG) as i:
                act.activation(gs[:, :, :], g[:, bass.ds(i * GRP, GRP), :], ACT.Copy).then_inc(gs_r, 1)
                for k in tiles:
                    c.wait(tp_r)
                    act.activation(gT[:, k % 2, :], tp[:, k % 2, 0:P], ACT.Copy).then_inc(gT_r, 1)
                c.turn()

        @block.vector
        def _(dve):
            c = Counted(dve)
            ch = Chain(dve, dch)
            for q, t in ((0, g), (1, g1)):
                ch.mark(dve.tensor_tensor(t[:, :, :], K.hot[:, :, q, :], K.wts[:, q, :].unsqueeze(2).to_broadcast([P, NT, EX]), ALU.mult))
            ch.wait()
            ch.step(dve.tensor_tensor(g[:, :, :], g[:, :, :], g1[:, :, :], ALU.add))
            dve.sem_inc(g_r, 1)
            ch.restart()
            dve.wait_ge(cl, 48)
            dve.sem_inc(in_f, 1)
            dve.sem_inc(e_f, 1)
            dve.sem_inc(y_w, 16)

            def group(i):
                c.wait(y_w, 16)
                c.wait(xm_l, 16)
                for k in tiles:
                    c.wait(bp_r)
                    ch.step(dve.tensor_tensor(y[:, k, :], bp[:, k % 2, 0:D], xm[:, k, :], ALU.add))
                    dve.sem_inc(bp_f, 1)
                dve.wait_ge(eg, i * (16 * 2 * GRP) + 16 * 2 * GRP)
                for q in range(2):
                    for k in tiles:
                        ch.mark(dve.scalar_tensor_tensor(out=y[:, k, :], in0=e[:, q, k, :], scalar=K.wts[:, q, bass.ds(i * GRP + k, 1)],
                                                    in1=y[:, k, :], op0=ALU.mult, op1=ALU.add))
                    ch.wait()
                dve.sem_inc(e_f, 1)
                for k in tiles:
                    ch.mark(dve.bn_stats(st[:, k, :], y[:, k, :]))
                ch.wait()
                for k in tiles:
                    ch.mark(dve.bn_aggr(mv[:, k, :], st[:, k, :]))
                ch.wait()
                dve.sem_inc(st_r, 1)
                c.wait(rs_r)
                for k in tiles:
                    ch.mark(dve.tensor_scalar(y[:, k, :], y[:, k, :], mv[:, k, 0:1], rs[:, k:k + 1], ALU.subtract, ALU.mult))
                ch.wait()
                for j, op in ((0, ALU.mult), (1, ALU.add)):
                    ch.step(dve.tensor_tensor(y[:, :, :], y[:, :, :], vec[:, j, :].unsqueeze(1).to_broadcast([P, GRP, D]), op))
                c.wait(x1_l, 16)
                ch.step(dve.tensor_tensor(y[:, :, :], y[:, :, :], x1[:, :, :], ALU.add))
                dve.sem_inc(y_r, 1)
                dve.sem_inc(in_f, 1)
                ch.restart()
                c.turn()

            with dve.Fori(0, NG) as i:
                group(i)
            dve.wait_ge(y_w, 32)


_INS = {
    "x": ((NP, D), F32), "src": ((EP,), I32), "dst": ((EP,), I32), "dprev": ((EP,), I32), "srcT": ((P, ET), I32), "dstT": ((P, ET), I32), "noise": ((P, NT), F32),
    "gat_w": ((D, D), F32), "gat_wT": ((D, D), F32), "a_src": ((HEADS, FOUT), F32), "a_tgt": ((HEADS, FOUT), F32),
    "gat_b": ((D,), F32), "lnl_g": ((D,), F32), "lnl_b": ((D,), F32), "lng_g": ((D,), F32), "lng_b": ((D,), F32),
    "ln2_g": ((D,), F32), "ln2_b": ((D,), F32), "in_wT": ((D, 2 * D), F32), "conv_w": ((D, 4), F32),
    "conv_b": ((D,), F32), "xp_wT": ((D, 48), F32), "dt_wT": ((NR, D), F32), "dt_b": ((D,), F32),
    "A_log": ((D, NS), F32), "Dp": ((D,), F32), "out_wT": ((D, D), F32), "wlT": ((D, D), F32), "wgT": ((D, D), F32),
    "ff1_wT": ((D, 2 * D), F32), "ff1_b": ((2 * D,), F32), "ff2_wT": ((2 * D, D), F32), "ff2_b": ((D,), F32),
    "gate_w": ((D, EX), F32), "gate_b": ((EX,), F32), "w1": ((EX, D, FF), F32), "b1": ((EX, FF), F32),
    "w2": ((EX, FF, D), F32), "b2": ((EX, D), F32), "gamma": ((D,), F32), "beta": ((D,), F32),
}

_SCRATCH = {
    "xn_d": ((NP, D), F32), "table": ((NP, ROW), F32), "stgt_d": ((NP, HEADS), F32),
    "keys_d": ((2, NP), F32), "rank_d": ((NP,), I32), "first_d": ((ET,), I32), "v_d": ((EP, HEADS), F32),
    "tc_d": ((EP, 2 * HEADS), F32), "xs_d": ((NP, D), F32), "dbs_d": ((96, NP + TC), BF16),
    "dtu_d": ((P, NCH + 1, 4, TC), F32), "szq_d": ((P, NCH, 4, TC), F32), "agg_d": ((EP, ROW), F32),
    "spill_d": ((ET + 1, ROW), F32), "ym_d": ((NP, D), F32), "x1_d": ((NP, D), F32), "xm_d": ((NP, D), F32),
    "disp_d": ((MT * P, D), F32), "eout_d": ((MT * P, D), F32),
}


class Shared:
    pass


def gnn_ffn_kernel(nc, ins, out, debug=(), upto=99):
    Phase.used = []
    scratch = {}
    for name, (shape, dt) in _SCRATCH.items():
        kind = "ExternalOutput" if name in debug else "Internal"
        scratch[name] = nc.dram_tensor(name, shape, dt, kind=kind).ap()
    A = dict(ins, out=out, **scratch)
    with ExitStack() as ctx:
        def keep(name, shape, dt=F32):
            return ctx.enter_context(nc.sbuf_tensor("k_" + name, shape, dt))

        K = Shared()
        K.ident = keep("ident", [P, P])
        K.upper = keep("upper", [P, P])
        K.ones = keep("ones", [P, P])
        K.iota = keep("iota", [P, P])
        K.nhalf = keep("nhalf", [P, 16])
        K.iota_i = keep("iota_i", [P, P], I32)
        K.node = keep("node", [P, NT])
        K.node_i = keep("node_i", [P, NT], I32)
        K.s_all = keep("s_all", [P, NT, 2 * HEADS])
        K.rank = keep("rank", [P, NT], I32)
        K.start = keep("start", [P, NT], I32)
        K.some = keep("some", [P, NT])
        K.spill = keep("spill", [P, NT], I32)
        K.top_src = keep("top_src", [P, HEADS])
        K.top_e = keep("top_e", [P, 1])
        K.gap = keep("gap", [P, NT])
        K.hot = keep("hot", [P, NT, 2, EX])
        K.wts = keep("wts", [P, 2, NT])
        K.pos = keep("pos", [P, 2, NT], I32)
        K.wrow = keep("wrow", [P, MT], I32)
        phases = [constants, project, locate, order, spread_scores, mamba_in, edges_and_scan,
                  combine_nodes, dispatch, experts, finish]
        for n, phase in enumerate(phases):
            if n <= upto:
                phase(nc, A, K)
                if phase in (order, edges_and_scan):
                    clear_semaphores(nc)


def kernel(**inputs):
    import numpy as np
    import concourse.bacc as _bacc
    from concourse.bass_utils import run_bass_kernel_spmd as _run

    nc = _bacc.Bacc("TRN2", target_bir_lowering=False, num_devices=1)
    arrays = layout(inputs)
    ins = {n: nc.dram_tensor("in_" + n, s, t, kind="ExternalInput").ap() for n, (s, t) in _INS.items()}
    out = nc.dram_tensor("out", (N, D), F32, kind="ExternalOutput").ap()
    gnn_ffn_kernel(nc, ins, out)
    r = _run(nc, [arrays], core_ids=[0])
    return np.asarray(r.results[0]["out"])


def layout(inputs):
    import numpy as np

    v = {k.replace("L0_gnn_", "").replace("L0_ffn_", ""): np.asarray(a) for k, a in inputs.items()}
    tail = np.full(EP - E, NP - 1, np.int32)
    noise = np.concatenate([v["node_vec"], np.zeros(NP - N, np.float32)])
    dst = np.concatenate([v["dst"], tail])
    a = {
        "srcT": np.concatenate([v["src"], tail]).reshape(ET, P).T, "dstT": dst.reshape(ET, P).T,
        "x": np.concatenate([v["x"], np.zeros((NP - N, D), np.float32)]),
        "src": np.concatenate([v["src"], tail]),
        "dst": dst, "dprev": np.concatenate([np.full(1, -1, np.int32), v["dst"], tail])[:EP],
        "noise": noise.reshape(NT, P).T, "gat_w": v["gat_w"], "gat_wT": v["gat_w"].T,
        "a_src": v["gat_a_src"], "a_tgt": v["gat_a_tgt"], "gat_b": v["gat_b"],
        "lnl_g": v["ln_local_g"], "lnl_b": v["ln_local_b"], "lng_g": v["ln_global_g"], "lng_b": v["ln_global_b"],
        "ln2_g": v["ln2_g"], "ln2_b": v["ln2_b"], "in_wT": v["in_proj_w"].T, "conv_w": v["conv_w"],
        "conv_b": v["conv_b"], "xp_wT": v["x_proj_w"].T, "dt_wT": v["dt_proj_w"].T, "dt_b": v["dt_proj_b"],
        "A_log": v["A_log"], "Dp": v["D_param"], "out_wT": v["out_proj_w"].T, "wlT": v["wl"].T, "wgT": v["wg"].T,
        "ff1_wT": v["ff1_w"].T, "ff1_b": v["ff1_b"], "ff2_wT": v["ff2_w"].T, "ff2_b": v["ff2_b"],
        "gate_w": v["gate_w"], "gate_b": v["gate_b"], "w1": v["w1"], "b1": v["b1"], "w2": v["w2"], "b2": v["b2"],
        "gamma": v["gamma"], "beta": v["beta"],
    }
    return {"in_" + n: np.ascontiguousarray(x) for n, x in a.items()}
```

```python
from contextlib import ExitStack

import concourse.bass as bass
from concourse import mybir

P = 128
F32 = mybir.dt.float32
BF16 = mybir.dt.bfloat16
I32 = mybir.dt.int32
ALU = mybir.AluOpType
ACT = mybir.ActivationFunctionType
AX = mybir.AxisListType

N, E, D = 6250, 100000, 256
NT = -(-N // P)
NP = NT * P
NLAST = N - (NT - 1) * P
GRP = 7
NG = NT // GRP
ET = 784
EP = ET * P
HEADS, FOUT = 4, 64
ROW = D + HEADS
NS, NR = 16, 16
TC = 448
NCH = NP // TC
TB = 112
NB = TC // TB
EX, FF = 16, 512
EXT = 2 * P
MT = (2 * NP + EX * (EXT - 1)) // EXT
MT += -MT % 4
LN_EPS = 1e-5
DEN_EPS = 1e-16
FAR = 1.0e6
HUGE = 3.0e38
assert NT % GRP == 0 and NP % TC == 0 and ET >= -(-E // P) and ET % (NCH * 8) == 0


class Chain:

    def __init__(self, eng, sem):
        self.eng, self.sem, self.n = eng, sem, 0

    def mark(self, ins):
        ins.then_inc(self.sem, 1)
        self.n += 1

    def wait(self):
        self.eng.wait_ge(self.sem, self.n)

    def after(self, n):
        self.eng.wait_ge(self.sem, n)

    def step(self, ins):
        self.mark(ins)
        self.wait()

    def restart(self):
        if self.n:
            self.eng.wait_ge(self.sem, self.n)
            self.eng.sem_inc(self.sem, -self.n)
        self.n = 0


class Counted:

    def __init__(self, eng):
        self.eng, self.seen = eng, {}

    def wait(self, sem, n=1):
        self.seen[sem.name] = (sem, self.seen.get(sem.name, (sem, 0))[1] + n)
        self.eng.wait_ge(sem, self.seen[sem.name][1])

    def turn(self):
        for sem, n in self.seen.values():
            self.eng.sem_inc(sem, -n)
        self.seen = {}


class Phase:

    used = []

    def __init__(self, nc, tag, ctx):
        self.nc, self.tag, self.ctx = nc, tag, ctx

    def sb(self, name, shape, dt=F32):
        return self.ctx.enter_context(self.nc.sbuf_tensor(f"{self.tag}_{name}", shape, dt))

    def ps(self, name, shape, dt=F32):
        return self.ctx.enter_context(self.nc.psum_tensor(f"{self.tag}_{name}", shape, dt))

    def sem(self, name):
        s = self.nc.alloc_semaphore(name=f"{self.tag}_{name}")
        self.used.append(s)
        return s

    def sems(self, names):
        return [self.sem(n) for n in names.split()]

    def block(self):
        return self.ctx.enter_context(self.nc.Block())


def clear_semaphores(nc):
    nc.clear_and_free_semaphores(Phase.used)
    Phase.used = []
    nc.all_engine_barrier()


def rows(ap, p=P):
    return ap.rearrange("(t p) d -> p t d", p=p)


def spread(ap, n, parts=P):
    return bass.AP(ap.tensor, ap.offset, [[0, parts], [1, n]])


def inverse_deviation(pool, ch, K, rstd, var):
    ch.step(pool.tensor_scalar(rstd, var, LN_EPS, None, ALU.add))
    ch.step(pool.tensor_tensor(rstd, rstd, K.nhalf[:, 0:rstd.shape[1]], ALU.pow))


def constants(nc, A, K):
    with ExitStack() as ctx:
        ph = Phase(nc, "cst", ctx)
        made, = ph.sems("made")
        block = ph.block()

        @block.gpsimd
        def _(pool):
            ch = Chain(pool, made)
            ch.mark(pool.memset(K.ident[:, :], 0.0))
            ch.mark(pool.memset(K.upper[:, :], 1.0))
            ch.mark(pool.memset(K.ones[:, :], 1.0))
            ch.mark(pool.memset(K.nhalf[:, :], -0.5))
            ch.wait()
            ch.mark(pool.affine_select(out=K.ident[:, :], in_=K.ident[:, :], compare_op=ALU.not_equal, fill=1.0,
                                  base=0, pattern=[[-1, P]], channel_multiplier=1))
            ch.mark(pool.affine_select(out=K.upper[:, :], in_=K.upper[:, :], compare_op=ALU.is_gt, fill=0.0,
                                  base=0, pattern=[[1, P]], channel_multiplier=-1))
            ch.mark(pool.iota(K.iota_i[:, :], pattern=[[1, P]], base=0, channel_multiplier=0))
            ch.mark(pool.iota(K.node_i[:, :], pattern=[[P, NT]], base=0, channel_multiplier=1))
            ch.wait()
            ch.mark(pool.tensor_copy(K.iota[:, :], K.iota_i[:, :]))
            ch.mark(pool.tensor_copy(K.node[:, :], K.node_i[:, :]))
            ch.restart()


def project(nc, A, K):
    G = 8
    assert ET == NG * GRP * 2 * G
    with ExitStack() as ctx:
        ph = Phase(nc, "prj", ctx)
        xin = ph.sb("xin", [P, GRP, D])
        xn = ph.sb("xn", [P, GRP, D])
        st = ph.sb("st", [P, GRP, 6])
        mv = ph.sb("mv", [P, GRP, 2])
        rstd = ph.sb("rstd", [P, GRP])
        xT = ph.sb("xT", [P, 2, 2, P])
        pj = ph.sb("pj", [P, GRP, D + 8])
        gat = ph.sb("gat", [P, 2, D])
        w = ph.sb("w", [P, 2, D + 8])
        adiag = ph.sb("adiag", [P, 2, 8])
        tp = [ph.ps(f"tp{i}", [P, 2, P]) for i in range(2)]
        pp = [ph.ps(f"pp{i}", [P, 512]) for i in range(2)]
        wl, wz, wf, wr = ph.sems("wl wz wf wr")
        xl, xfree, st_r, rs_r, xn_pe, xn_sp = ph.sems("xl xfree st_r rs_r xn_pe xn_sp")
        tp_r, xT_r, pp_r, pp_free, pj_r, xn_w, pj_w, pad, padded, stgt = ph.sems("tp_r xT_r pp_r pp_free pj_r xn_w pj_w pad padded stgt")
        dch, ach, pch = ph.sems("dch ach pch")
        fr_i = ph.sb("fr_i", [P, ET], I32)
        fr = ph.sb("fr", [P, ET])
        junk = ph.sb("junk", [P, ET])
        src_i = ph.sb("src_i", [P, ET], I32)
        part = ph.sb("part", [P, ET], I32)
        lo = ph.sb("lo", [P, ET])
        hi = ph.sb("hi", [P, ET])
        iota_b = ph.sb("iota_b", [P, P], BF16)
        zero_b = ph.sb("zero_b", [P, P], BF16)
        ohl = ph.sb("ohl", [P, 2, G, P], BF16)
        ohh = ph.sb("ohh", [P, 2, G, NT], BF16)
        deg = ph.ps("deg", [P, 512])
        fw, fl, ld, jch, och, oh_r, oh_f, zb_r, deg_r = ph.sems("fw fl ld jch och oh_r oh_f zb_r deg_r")
        block = ph.block()

        @block.sync
        def _(sp):
            sp.dma_start(src_i[:, :], A["src"].rearrange("(p c) -> p c", p=P)).then_inc(ld, 16)
            sp.dma_start(A["first_d"], bass.AP(A["dst"].tensor, 0, [[P, ET]]),
                         allow_slow_non_contiguous=True).then_inc(fw, 16)
            sp.wait_ge(fw, 16)
            sp.dma_start(fr_i[:, :], spread(A["first_d"], ET)).then_inc(fl, 16)
            sp.dma_start(gat[:, :, :], A["gat_w"].rearrange("(c p) d -> p c d", p=P)).then_inc(wl, 16)
            sp.dma_start(w[:, :, 0:D], A["gat_wT"].rearrange("(c p) f -> p c f", p=P)).then_inc(wl, 16)
            sp.wait_ge(wz, 1)
            for a, off in ((A["a_src"], 0), (A["a_tgt"], HEADS)):
                for h in range(HEADS):
                    q = (h % 2) * FOUT
                    sp.dma_start(adiag[q:q + FOUT, h // 2, off + h:off + h + 1],
                                 a[h:h + 1, :].rearrange("a f -> f a")).then_inc(wl, 16)
            with sp.Fori(0, NG) as i:
                sp.wait_ge(xfree, 1)
                sp.sem_inc(xfree, -1)
                sp.dma_start(xin[:, :, :], rows(A["x"])[:, bass.ds(i * GRP, GRP), :]).then_inc(xl, 16)
                sp.wait_ge(xn_sp, 1)
                sp.sem_inc(xn_sp, -1)
                sp.dma_start(rows(A["xn_d"])[:, bass.ds(i * GRP, GRP), :], xn[:, :, :]).then_inc(xn_w, 16)
                sp.wait_ge(pj_r, GRP)
                sp.sem_inc(pj_r, -GRP)
                sp.dma_start(rows(A["table"])[:, bass.ds(i * GRP, GRP), :], pj[:, :, 0:ROW]).then_inc(pj_w, 16)
            sp.wait_ge(padded, 1)
            sp.dma_start(rows(A["stgt_d"]), K.s_all[:, :, HEADS:2 * HEADS]).then_inc(stgt, 16)
            sp.wait_ge(stgt, 16)
            sp.wait_ge(xn_w, 16)
            sp.wait_ge(pj_w, 16)

        @block.vector
        def _(dve):
            ch = Chain(dve, dch)
            dve.memset(adiag[:, :, :], 0.0).then_inc(wz, 1)
            dve.sem_inc(xfree, 1)
            dve.sem_inc(xn_w, 16)
            ch.mark(dve.tensor_copy(iota_b[:, :], K.iota[:, :]))
            ch.step(dve.memset(zero_b[:, :], 0.0))
            dve.sem_inc(zb_r, 1)
            dve.wait_ge(ld, 16)
            ch.step(dve.tensor_scalar(part[:, :], src_i[:, :], P - 1, None, ALU.bitwise_and))
            ch.step(dve.tensor_copy(lo[:, :], part[:, :]))
            ch.step(dve.tensor_scalar(part[:, :], src_i[:, :], 7, None, ALU.logical_shift_right))
            ch.mark(dve.tensor_copy(hi[:, :], part[:, :]))
            dve.wait_ge(fl, 16)
            ch.mark(dve.tensor_copy(fr[:, :], fr_i[:, :]))
            ch.restart()
            dve.sem_inc(oh_f, 2)
            jc = Chain(dve, jch)
            oc = Chain(dve, och)

            def compare(i, k):
                b = bass.ds(i * GRP + k, 1)
                jc.wait()
                jc.mark(dve.tensor_scalar(junk[:, :], fr[:, :], K.node[:, b], None, ALU.is_lt, ALU.add, accum_out=K.below[:, b]))

            def made(n):
                oc.after(n)
                dve.sem_inc(oh_r, 1)

            def one_hots(i, k, before):
                for s in range(2):
                    dve.wait_ge(oh_f, 1)
                    dve.sem_inc(oh_f, -1)
                    t0 = (i * GRP + k) * (2 * G) + s * G
                    oc.mark(dve.tensor_tensor(ohh[:, s, :, :], iota_b[:, 0:NT].unsqueeze(1).to_broadcast([P, G, NT]),
                                              hi[:, bass.ds(t0, G)].unsqueeze(2).to_broadcast([P, G, NT]), ALU.is_equal))
                    for g in range(G):
                        oc.mark(dve.tensor_scalar(ohl[:, s, g, :], iota_b[:, :], lo[:, bass.ds(t0 + g, 1)],
                                                  None, ALU.is_equal))
                        if g == 0 and before:
                            made(before)
                    before = oc.n
                return before

            with dve.Fori(0, NG) as i:
                for k in range(GRP - 2):
                    compare(i, k)
                dve.wait_ge(xl, 16)
                dve.sem_inc(xl, -16)
                for k in range(GRP):
                    ch.mark(dve.bn_stats(st[:, k, :], xin[:, k, :]))
                ch.wait()
                for k in range(GRP):
                    ch.mark(dve.bn_aggr(mv[:, k, :], st[:, k, :]))
                ch.wait()
                dve.sem_inc(st_r, 1)
                for k in range(GRP - 2, GRP):
                    compare(i, k)
                dve.wait_ge(rs_r, 1)
                dve.sem_inc(rs_r, -1)
                dve.wait_ge(xn_w, 16)
                dve.sem_inc(xn_w, -16)
                for k in range(GRP):
                    ch.step(dve.tensor_scalar(xn[:, k, :], xin[:, k, :], mv[:, k, 0:1], rstd[:, k:k + 1],
                                              ALU.subtract, ALU.mult))
                    dve.sem_inc(xn_pe, 1)
                dve.sem_inc(xn_sp, 1)
                dve.sem_inc(xfree, 1)
                before = 0
                for k in range(GRP):
                    before = one_hots(i, k, before)
                made(before)
                for chain in (ch, jc, oc):
                    chain.restart()
            dve.wait_ge(deg_r, 1)
            ch.step(dve.tensor_copy(K.deg[:, :], deg[:, 0:NT]))
            ch.restart()

        @block.gpsimd
        def _(pool):
            ch = Chain(pool, pch)
            with pool.Fori(0, NG) as i:
                pool.wait_ge(st_r, 1)
                pool.sem_inc(st_r, -1)
                inverse_deviation(pool, ch, K, rstd[:, :], mv[:, :, 1])
                pool.sem_inc(rs_r, 1)
                ch.restart()
            pool.wait_ge(pad, 1)
            ch.step(pool.affine_select(out=K.s_all[:, NT - 1, HEADS:2 * HEADS], in_=K.s_all[:, NT - 1, HEADS:2 * HEADS],
                                       compare_op=ALU.is_ge, fill=-1.0e30, base=NLAST - 1,
                                       pattern=[[0, HEADS]], channel_multiplier=-1))
            pool.sem_inc(padded, 1)
            ch.restart()

        @block.tensor
        def _(pe):
            pe.wait_ge(wl, 16 * (2 + 2 * HEADS))
            for m in range(2):
                for c in range(2):
                    mm = pe.matmul(pp[0][:, m * 8:m * 8 + 8], gat[:, c, m * P:(m + 1) * P], adiag[:, c, :],
                                   start=(c == 0), stop=(c == 1))
            mm.then_inc(wf, 1)
            pe.wait_ge(wr, 1)
            pe.sem_inc(pp_free, 2)
            pe.wait_ge(zb_r, 1)
            pe.matmul(deg[:, 0:NT], zero_b[:, :], zero_b[:, 0:NT], start=True, stop=False, skip_group_check=True)

            def count():
                for s in range(2):
                    pe.wait_ge(oh_r, 1)
                    pe.sem_inc(oh_r, -1)
                    for g in range(G):
                        mm = pe.matmul(deg[:, 0:NT], ohl[:, s, g, :], ohh[:, s, g, :], start=False, stop=False,
                                       skip_group_check=True)
                    mm.then_inc(oh_f, 1)

            with pe.Fori(0, NG) as i:
                def turn(k):
                    pe.wait_ge(xn_pe, k + 1)
                    for c in range(2):
                        t = pe.transpose(tp[k % 2][:, c, :], xn[:, k, c * P:(c + 1) * P], K.ident[:, :])
                    t.then_inc(tp_r, 1)

                turn(0)
                for k in range(GRP):
                    if k + 1 < GRP:
                        turn(k + 1)
                    pe.wait_ge(xT_r, k + 1)
                    pe.wait_ge(pp_free, 1)
                    pe.sem_inc(pp_free, -1)
                    for c in range(2):
                        mm = pe.matmul(pp[k % 2][:, 0:D + 8], xT[:, k % 2, c, :], w[:, c, :], start=(c == 0), stop=(c == 1))
                    mm.then_inc(pp_r, 1)
                    count()
                pe.sem_inc(xn_pe, -GRP)
                pe.sem_inc(xT_r, -GRP)
            pe.matmul(deg[:, 0:NT], zero_b[:, :], zero_b[:, 0:NT], start=False, stop=True,
                      skip_group_check=True).then_inc(deg_r, 1)

        @block.scalar
        def _(act):
            ch = Chain(act, ach)
            act.wait_ge(wf, 1)
            act.activation(w[:, :, D:D + 8], pp[0][:, 0:16].rearrange("p (m e) -> p m e", m=2), ACT.Copy).then_inc(wr, 1)
            act.sem_inc(pj_w, 16)
            with act.Fori(0, NG) as i:
                act.wait_ge(pj_w, 16)
                act.sem_inc(pj_w, -16)

                def copy(k):
                    act.wait_ge(tp_r, k + 1)
                    act.activation(xT[:, k % 2, :, :], tp[k % 2][:, :, :], ACT.Copy).then_inc(xT_r, 1)

                copy(0)
                for k in range(GRP):
                    act.wait_ge(pp_r, k + 1)
                    ch.mark(act.activation(K.s_all[:, bass.ds(i * GRP + k, 1), :],
                                      pp[k % 2][:, D:D + 8].rearrange("p (a e) -> p a e", a=1), ACT.Copy))
                    ch.step(act.activation(pj[:, k, :], pp[k % 2][:, 0:D + 8], ACT.Copy))
                    act.sem_inc(pj_r, 1)
                    act.sem_inc(pp_free, 1)
                    if k + 1 < GRP:
                        copy(k + 1)
                act.sem_inc(tp_r, -GRP)
                act.sem_inc(pp_r, -GRP)
                ch.restart()
            act.sem_inc(pad, 1)


def order(nc, A, K):
    with ExitStack() as ctx:
        ph = Phase(nc, "ord", ctx)
        ones_b = ph.sb("ones_b", [P, P], BF16)
        at = ph.sb("at", [P, NT])
        upto = ph.sb("upto", [P, NT])
        at_i = ph.sb("at_i", [P, NT], I32)
        b2 = ph.sb("b2", [P, NT])
        s2 = ph.sb("s2", [P, NT])
        full = ph.sb("full", [P, NT])
        none = ph.sb("none", [P, NT])
        over = ph.sb("over", [P, NT])
        rw_i = ph.sb("rw_i", [P, NT, P], I32)
        cm = ph.sb("cm", [P, NT, P], BF16)
        far = ph.sb("far", [P, NT])
        far_i = ph.sb("far_i", [P, NT], I32)
        zero = ph.sb("zero", [P, 8 * D])
        noise = ph.sb("noise", [P, NT])
        key = ph.sb("key", [P, 2, NT])
        sgn = ph.sb("sgn", [P, NT])
        sgn_i = ph.sb("sgn_i", [P, NT], I32)
        keyT = ph.sb("keyT", [NT, 2, P])
        low = ph.sb("low", [P, P])
        krow = ph.sb("krow", [P, NP])
        rrow = ph.sb("rrow", [P, NP])
        more = ph.sb("more", [P, 2, NP], BF16)
        tie = ph.sb("tie", [P, 2, P], BF16)
        rk = ph.sb("rk", [P, 4, TC], I32)
        xn = ph.sb("xn", [P, 2, GRP, D])
        kt = ph.ps("kt", [P, 512])
        rp = ph.ps("rp", [P, 4, 512])
        nl, xf, zw, ul, ut_r, dch, ach, got, at_r, far_r, zr, vz, vs = ph.sems("nl xf zw ul ut_r dch ach got at_r far_r zr vz vs")
        key_r, pad_r, kp_r, kt_r, kts, kw, kl = ph.sems("key_r pad_r kp_r kt_r kts kw kl")
        m_r, m_f, rp_r, rk_r, rw, rl, sc = ph.sems("m_r m_f rp_r rk_r rw rl sc")
        xl = ph.sems("xl0 xl1")
        block = ph.block()

        @block.sync
        def _(sp):
            sp.dma_start(noise[:, :], A["noise"]).then_inc(nl, 16)
            sp.wait_ge(zr, 1)
            v = A["v_d"].rearrange("(p c) h -> p (c h)", p=P)
            for j in range(4):
                sp.dma_start(v[:, j * ET:(j + 1) * ET], zero[:, 0:ET]).then_inc(vz, 16)
            for g in range(2):
                sp.dma_start(xn[:, g, :, :], rows(A["xn_d"])[:, g * GRP:(g + 1) * GRP, :]).then_inc(xl[g % 2], 16)
            sp.wait_ge(kts, 1)
            sp.dma_start(A["keys_d"].rearrange("r (b f) -> b r f", f=P), keyT[:, :, :]).then_inc(kw, 16)
            sp.wait_ge(kw, 16)
            sp.dma_start(krow[:, :], spread(A["keys_d"], NP)).then_inc(kl, 16)
            sp.dma_start(rrow[:, :], bass.AP(A["keys_d"].tensor, NP, [[0, P], [1, NP]])).then_inc(kl, 16)
            lists = A["disp_d"].rearrange("(j p q) d -> j p (q d)", p=P, q=8)
            for j in range(lists.shape[0]):
                sp.dma_start(lists[j], zero[:, :]).then_inc(zw, 16)
            sp.wait_ge(ut_r, 1)
            sp.dma_start(upto[0:P - 1, :], K.below[1:P, :], allow_slow_non_contiguous=True).then_inc(ul, 16)
            sp.dma_start(upto[P - 1:P, 0:NT - 1], K.below[0:1, 1:NT], allow_slow_non_contiguous=True).then_inc(ul, 16)
            sp.wait_ge(rk_r, 1)
            for q in range(4):
                n = min(4, NCH - 4 * q)
                sp.dma_start(A["rank_d"][4 * q * TC:(4 * q + n) * TC].rearrange("(a b f) -> a b f", a=1, f=TC),
                             rk[32 * q:32 * q + 1, 0:n, :]).then_inc(rw, 16)
            sp.wait_ge(rw, 64)
            sp.dma_start(K.rank[:, :], A["rank_d"].rearrange("(b p) -> p b", p=P),
                         allow_slow_non_contiguous=True).then_inc(rl, 16)
            sp.wait_ge(zw, 16 * lists.shape[0])
            for g in range(2, NG):
                sp.wait_ge(xf, g - 1)
                sp.dma_start(xn[:, g % 2, :, :], rows(A["xn_d"])[:, g * GRP:(g + 1) * GRP, :]).then_inc(xl[g % 2], 16)

        @block.vector
        def _(dve):
            ch = Chain(dve, dch)
            ch.mark(dve.memset(upto[:, NT - 1:NT], float(ET)))
            ch.step(dve.tensor_scalar(at[:, :], K.below[:, :], -1.0, 0.0, ALU.add, ALU.max))
            dve.sem_inc(ut_r, 1)
            ch.step(dve.tensor_copy(at_i[:, :], at[:, :]))
            dve.sem_inc(at_r, 1)
            ch.mark(dve.memset(ones_b[:, :], 1.0))
            ch.step(dve.memset(zero[:, :], 0.0))
            dve.sem_inc(zr, 1)
            ch.mark(dve.tensor_scalar(low[:, :], K.upper[:, :], -1.0, 1.0, ALU.mult, ALU.add))
            dve.wait_ge(nl, 16)
            ch.step(dve.tensor_tensor(key[:, 0, :], K.deg[:, :], noise[:, :], ALU.add))
            dve.sem_inc(key_r, 1)
            dve.wait_ge(pad_r, 1)
            ch.step(dve.tensor_scalar(sgn[:, :], key[:, 0, :], 0.0, 2.0, ALU.is_ge, ALU.mult))
            ch.step(dve.tensor_scalar(sgn_i[:, :], sgn[:, :], -1.0, None, ALU.add))
            ch.step(dve.tensor_tensor(key[:, 1, :].bitcast(I32), key[:, 0, :].bitcast(I32), sgn_i[:, :], ALU.add))
            ch.step(dve.tensor_scalar(sgn[:, :], key[:, 0, :], 0.0, 2.0 ** -126, ALU.is_equal, ALU.mult))
            ch.step(dve.tensor_tensor(key[:, 1, :], key[:, 1, :], sgn[:, :], ALU.add))
            dve.sem_inc(kp_r, 1)
            dve.wait_ge(kt_r, 1)
            ch.step(dve.tensor_copy(keyT[:, :, :], kt[0:NT, 0:2 * P].rearrange("b (r f) -> b r f", r=2)))
            dve.sem_inc(kts, 1)
            ch.restart()
            dve.wait_ge(kl, 32)
            dve.sem_inc(m_f, 2)

            def ties(j, s):
                kj = key[:, 0, bass.ds(j, 1)]
                ch.mark(dve.scalar_tensor_tensor(out=tie[:, s, :], in0=krow[:, bass.ds(j * P, P)], scalar=kj, in1=low[:, :],
                                                 op0=ALU.is_equal, op1=ALU.mult))

            def compare(j, s):
                blk = bass.ds(j * P, P)
                dve.wait_ge(m_f, 1)
                dve.sem_inc(m_f, -1)
                ch.step(dve.tensor_scalar(more[:, s, :], rrow[:, :], key[:, 0, bass.ds(j, 1)], None, ALU.is_gt))
                ch.mark(dve.tensor_copy(rrow[:, blk], krow[:, blk]))
                ch.mark(dve.tensor_tensor(more[:, s, blk], more[:, s, blk], tie[:, s, :], ALU.subtract))
                done = ch.n
                ties((j + 1) % NT, 1 - s)
                ch.after(done)
                dve.sem_inc(m_r, 1)

            ties(0, 0)
            ch.wait()
            def first_edges():
                dve.wait_ge(ul, 32)
                ch.step(dve.tensor_tensor(K.same[:, :], upto[:, :], K.below[:, :], ALU.subtract))
                dve.wait_ge(got, 16 * NT)
                nb = K.node[:, :].unsqueeze(2).to_broadcast([P, NT, P])
                ch.step(dve.tensor_tensor(cm[:, :, :], rw_i[:, :, :], nb, ALU.is_lt))
                ch.step(dve.tensor_reduce(b2[:, :], cm[:, :, :], AX.X, ALU.add))
                ch.step(dve.tensor_tensor(cm[:, :, :], rw_i[:, :, :], nb, ALU.is_equal))
                ch.step(dve.tensor_reduce(s2[:, :], cm[:, :, :], AX.X, ALU.add))
                ch.mark(dve.tensor_scalar(full[:, :], b2[:, :], float(P), None, ALU.is_ge))
                ch.mark(dve.tensor_scalar(none[:, :], b2[:, :], 0.0, None, ALU.is_le))
                ch.wait()
                ch.mark(dve.tensor_tensor(none[:, :], none[:, :], full[:, :], ALU.add))
                ch.mark(dve.tensor_tensor(full[:, :], full[:, :], at[:, :], ALU.add))
                ch.wait()
                ch.step(dve.tensor_tensor(over[:, :], K.same[:, :], none[:, :], ALU.is_gt))
                ch.step(dve.scalar_tensor_tensor(out=over[:, :], in0=full[:, :], scalar=float(1 - ET), in1=over[:, :],
                                                 op0=ALU.add, op1=ALU.mult))
                ch.step(dve.tensor_scalar(K.spill[:, :], over[:, :], float(ET), None, ALU.add))
                ch.step(dve.scalar_tensor_tensor(out=b2[:, :], in0=at[:, :], scalar=float(P), in1=b2[:, :],
                                                 op0=ALU.mult, op1=ALU.add))
                ch.step(dve.tensor_tensor(s2[:, :], s2[:, :], K.same[:, :], ALU.add))
                ch.step(dve.tensor_scalar(K.some[:, :], s2[:, :], 0.0, None, ALU.is_gt))
                ch.step(dve.tensor_scalar(far[:, :], K.some[:, :], -FAR, FAR, ALU.mult, ALU.add))
                ch.step(dve.tensor_tensor(far[:, :], far[:, :], b2[:, :], ALU.add))
                ch.step(dve.tensor_copy(far_i[:, :], far[:, :]))
                ch.step(dve.tensor_scalar(b2[:, :], b2[:, :], float(EP - 1), None, ALU.min))
                ch.step(dve.tensor_copy(K.start[:, :], b2[:, :]))
                dve.sem_inc(far_r, 1)
                ch.restart()

            compare(0, 0)
            ch.restart()
            for t0, t1 in ((0, (NT - 1) // 4), ((NT - 1) // 4, (NT - 1) // 2)):
                with dve.Fori(t0, t1) as i:
                    compare(i * 2 + 1, 1)
                    compare(i * 2 + 2, 0)
                    ch.restart()
                if t0 == 0:
                    first_edges()

        @block.gpsimd
        def _(pool):
            pool.wait_ge(key_r, 1)
            pool.affine_select(out=key[:, 0, NT - 1:NT], in_=key[:, 0, NT - 1:NT], compare_op=ALU.is_ge, fill=HUGE,
                               base=NLAST - 1, pattern=[[0, 1]], channel_multiplier=-1).then_inc(pad_r, 1)
            pool.wait_ge(at_r, 1)
            for b in range(NT):
                pool.indirect_dma_start(rw_i[:, b, :], None, A["dst"].rearrange("(t q) -> t q", q=P),
                                        bass.IndirectOffsetOnAxis(at_i[:, b:b + 1], 0)).then_inc(got, 16)
            pool.wait_ge(far_r, 1)
            pool.wait_ge(vz, 64)
            for b in range(NT):
                pool.indirect_dma_start(A["v_d"], bass.IndirectOffsetOnAxis(far_i[:, b:b + 1], 0),
                                        K.s_all[:, b, HEADS:2 * HEADS], None,
                                        bounds_check=EP - 1, oob_is_err=False).then_inc(vs, 16)
            pool.wait_ge(rl, 16)
            for g in range(NG):
                pool.wait_ge(xl[g % 2], 16 * (g // 2 + 1))
                for b in range(GRP):
                    pool.indirect_dma_start(A["xs_d"], bass.IndirectOffsetOnAxis(K.rank[:, g * GRP + b:g * GRP + b + 1], 0),
                                            xn[:, g % 2, b, :], None).then_inc(sc, 16)
                if g < NG - 2:
                    pool.wait_ge(sc, 16 * GRP * (g + 1))
                    pool.sem_inc(xf, 1)
            pool.wait_ge(sc, 16 * NT)
            pool.wait_ge(vs, 16 * NT)

        @block.tensor
        def _(pe):
            pe.wait_ge(kp_r, 1)
            for r in range(2):
                mm = pe.transpose(kt[0:NT, r * P:(r + 1) * P], key[:, r, :], K.ident[:, :])
            mm.then_inc(kt_r, 1)

            def count(s, first=False, last=False):
                pe.wait_ge(m_r, 1)
                pe.sem_inc(m_r, -1)
                for c in range(NCH):
                    q = c // 4
                    mm = pe.matmul(rp[32 * q:32 * q + 1, c % 4, 0:TC], ones_b[:, 0:1],
                                   more[:, s, c * TC:(c + 1) * TC], start=first, stop=last, skip_group_check=True)
                mm.then_inc(m_f, 1)

            count(0, first=True)
            with pe.Fori(0, (NT - 1) // 2) as i:
                count(1)
                count(0)
            pe.drain().then_inc(rp_r, 1)

        @block.scalar
        def _(act):
            ch = Chain(act, ach)
            act.wait_ge(rp_r, 1)
            for q in range(4):
                n = min(4, NCH - 4 * q)
                ch.mark(act.activation(rk[32 * q:32 * q + 1, 0:n, :], rp[32 * q:32 * q + 1, 0:n, 0:TC], ACT.Copy))
            ch.wait()
            act.sem_inc(rk_r, 1)
            ch.restart()


def spread_scores(nc, A, K):
    with ExitStack() as ctx:
        ph = Phase(nc, "spr", ctx)
        dst = ph.sb("dst", [P, ET], I32)
        prev = ph.sb("prev", [P, ET], I32)
        keep = ph.sb("keep", [P, ET])
        v = ph.sb("v", [P, ET, HEADS])
        tc = ph.sb("tc", [P, ET, 2 * HEADS])
        tmp = ph.sb("tmp", [P, ET])
        mx = ph.sb("mx", [P, HEADS])
        dl, vl, hd, mx_r, top_r, tc_r, tw, dch = ph.sems("dl vl hd mx_r top_r tc_r tw dch")
        block = ph.block()

        @block.sync
        def _(sp):
            sp.dma_start(dst[:, :], A["dst"].rearrange("(p c) -> p c", p=P)).then_inc(dl, 16)
            sp.dma_start(prev[:, :], A["dprev"].rearrange("(p c) -> p c", p=P)).then_inc(dl, 16)
            sp.dma_start(v[:, :, :], A["v_d"].rearrange("(p c) h -> p c h", p=P)).then_inc(vl, 16)
            sp.wait_ge(tc_r, 1)
            sp.dma_start(A["tc_d"].rearrange("(p c) h -> p c h", p=P), tc[:, :, :]).then_inc(tw, 16)
            sp.wait_ge(tw, 16)

        @block.gpsimd
        def _(pool):
            pool.wait_ge(mx_r, 1)
            pool.partition_all_reduce(K.top_src[:, :], mx[:, :], P, bass.bass_isa.ReduceOp.max).then_inc(top_r, 1)
            pool.wait_ge(dl, 32)
            pool.wait_ge(vl, 16)
            pool.indirect_dma_start(v[:, 0, :], None, A["stgt_d"],
                                    bass.IndirectOffsetOnAxis(dst[:, 0:1], 0)).then_inc(hd, 16)

        @block.vector
        def _(dve):
            ch = Chain(dve, dch)
            ch.step(dve.tensor_reduce(mx[:, :], K.s_all[:, :, 0:HEADS].rearrange("p t h -> p h t"), AX.X, ALU.max))
            dve.sem_inc(mx_r, 1)
            dve.wait_ge(dl, 32)
            ch.step(dve.tensor_tensor(keep[:, :], dst[:, :], prev[:, :], ALU.is_equal))
            ch.step(dve.memset(keep[:, 0:1], 0.0))
            dve.wait_ge(hd, 16)
            for h in range(HEADS):
                ch.mark(dve.tensor_tensor_scan(tc[:, :, h], keep[:, :], v[:, :, h], 0.0, ALU.mult, ALU.add))
            ch.wait()
            dve.wait_ge(top_r, 1)
            for h in range(HEADS):
                ch.step(dve.tensor_scalar(tmp[:, :], tc[:, :, h], K.top_src[:, h:h + 1], None, ALU.add))
                ch.step(dve.scalar_tensor_tensor(out=tc[:, :, HEADS + h], in0=tmp[:, :], scalar=0.2, in1=tmp[:, :],
                                                 op0=ALU.mult, op1=ALU.max))
            dve.sem_inc(tc_r, 1)
            ch.restart()


def halves(ap):
    return ap.rearrange("(h p) -> p h", p=P)


def mamba_in(nc, A, K):
    with ExitStack() as ctx:
        ph = Phase(nc, "min", ctx)
        inw = ph.sb("inw", [P, 2, 2 * D])
        xpw = ph.sb("xpw", [P, 2, 48])
        dtw = ph.sb("dtw", [NR, D])
        cw = ph.sb("cw", [P, 2, 4])
        vec = ph.sb("vec", [P, 3, 2, 1])
        xs = ph.sb("xs", [TB, NB, D])
        xsT = ph.sb("xsT", [P, 4, TC])
        xcb = ph.sb("xcb", [P, 2, 3 + TC])
        cv = ph.sb("cv", [P, 2, TC])
        xcs = ph.sb("xcs", [P, 4, TC])
        dbc = ph.sb("dbc", [48, TC])
        rest = ph.sb("rest", [48, 2, TC])
        parts = ph.sb("parts", [48, 3, TC], BF16)
        ab = ph.sb("ab", [P, 2, TC])
        ex = ph.sb("ex", [P, 2, TC])
        lg = ph.sb("lg", [P, 2, TC])
        pl = ph.sb("pl", [P, 2, TC])
        rl = ph.sb("rl", [P, 2, TC])
        small = ph.sb("small", [P, 2, TC], I32)
        dtu = ph.sb("dtu", [P, 4, TC])
        szq = ph.sb("szq", [P, 4, TC])
        xt = ph.ps("xt", [P, 2, 512])
        ip = ph.ps("ip", [P, 2, 512])
        dp = ph.ps("dp", [P, 2, 512])
        db = ph.ps("db", [P, 512])
        wl, xl, xt_r, xT_r, ip_r, ip_f, xcb_f, xc_r, sz_r = ph.sems("wl xl xt_r xT_r ip_r ip_f xcb_f xc_r sz_r")
        cv_r, xcs_pe, xcs_v, xcs_f, db_r, dbs_pe, dbs_p, dbc_f, dt_r, dp_f = ph.sems(
            "cv_r xcs_pe xcs_v xcs_f db_r dbs_pe dbs_p dbc_f dt_r dp_f")
        ex_r, ex_f, ln_r, prt_r, dtu_r, szq_r, prt_w, dtu_w, szq_w = ph.sems("ex_r ex_f ln_r prt_r dtu_r szq_r prt_w dtu_w szq_w")
        dch, ach, pch = ph.sems("dch ach pch")
        block = ph.block()

        def half(i, h=0, n=2):
            return bass.ds((i & 1) * 2 + h, n)

        def chunks(eng, turned, body, turn):
            turned(0)
            body(0, True, False)
            turn()
            with eng.Fori(1, NCH) as i:
                body(i, False, False)
                turn()
            body(NCH, False, True)
            turn()

        def nothing(i):
            pass

        @block.sync
        def _(sp):
            c = Counted(sp)
            sp.dma_start(inw[:, :, :], A["in_wT"].rearrange("(c p) f -> p c f", p=P)).then_inc(wl, 16)
            sp.dma_start(xpw[:, :, :], A["xp_wT"].rearrange("(c p) f -> p c f", p=P)).then_inc(wl, 16)
            sp.dma_start(dtw[:, :], A["dt_wT"]).then_inc(wl, 16)
            sp.dma_start(cw[:, :, :], A["conv_w"].rearrange("(h p) k -> p h k", p=P)).then_inc(wl, 16)
            for j, v in enumerate((A["conv_b"], A["dt_b"], A["Dp"])):
                sp.dma_start(vec[:, j, :, 0], halves(v), allow_slow_non_contiguous=True).then_inc(wl, 16)

            def store_szq(i):
                c.wait(szq_r)
                sp.dma_start(A["szq_d"][:, bass.ds(i, 1), :, :].rearrange("p a b t -> p (a b) t"), szq[:, :, :]).then_inc(szq_w, 16)

            def store_parts(i):
                sp.dma_start(A["dbs_d"][:, bass.ds(i * TC, TC)].rearrange("(j r) t -> r j t", j=3), parts[NR:48, :, :]).then_inc(prt_w, 16)

            def store_steps(i):
                sp.dma_start(A["dtu_d"][:, bass.ds(i, 1), :, :].rearrange("p a b t -> p (a b) t"), dtu[:, :, :]).then_inc(dtu_w, 16)

            store_szq(0)
            c.turn()
            with sp.Fori(1, NCH) as i:
                c.wait(prt_r)
                store_parts(i - 1)
                c.wait(dtu_r)
                store_steps(i - 1)
                store_szq(i)
                c.turn()
            c.wait(prt_r)
            c.wait(dtu_r)
            for i in (NCH - 1, NCH):
                store_parts(i)
                store_steps(i)
            c.turn()

        @block.tensor
        def _(pe):
            c = Counted(pe)
            pe.wait_ge(wl, 16 * 7)
            pe.sem_inc(ip_f, 1)
            pe.sem_inc(dp_f, 1)

            def turned(i):
                c.wait(xl, 16)
                for q in range(2):
                    for j in range(NB):
                        t = pe.transpose(xt[:, q, j * TB:(j + 1) * TB], xs[:, j, q * P:(q + 1) * P], K.ident[0:TB, 0:TB])
                t.then_inc(xt_r, 1)

            def project_in(i, z):
                c.wait(ip_f)
                for h in range(2):
                    for q in range(2):
                        mm = pe.matmul(ip[:, h, 0:TC], inw[:, q, (2 * z + h) * P:(2 * z + h + 1) * P],
                                       xsT[:, half(i, q, 1), :].rearrange("p a t -> p (a t)"), start=(q == 0), stop=(q == 1))
                mm.then_inc(ip_r, 1)

            def body(i, first, last):
                if not last:
                    c.wait(xT_r)
                    project_in(i, 0)
                if not first:
                    c.wait(xcs_pe)
                    for q in range(2):
                        mm = pe.matmul(db[0:48, 0:TC], xpw[:, q, :], xcs[:, half(i - 1, q, 1), :].rearrange("p a t -> p (a t)"),
                                       start=(q == 0), stop=(q == 1))
                    mm.then_inc(db_r, 1)
                if not last:
                    turned(i + 1)
                if not first:
                    c.wait(dbs_pe)
                    c.wait(dp_f)
                    for h in range(2):
                        mm = pe.matmul(dp[:, h, 0:TC], dtw[:, h * P:(h + 1) * P], dbc[0:NR, :], start=True, stop=True)
                    mm.then_inc(dt_r, 1)
                if not last:
                    project_in(i, 1)

            chunks(pe, turned, body, c.turn)
            c.wait(xl, 16)
            c.turn()

        @block.scalar
        def _(act):
            c = Counted(act)
            ch = Chain(act, ach)

            def load(i):
                act.dma_start(xs[:, :, :], rows(A["xs_d"], TB)[:, bass.ds(i * NB, NB), :]).then_inc(xl, 16)

            load(0)
            act.wait_ge(wl, 16 * 7)
            act.sem_inc(szq_w, 16)
            act.sem_inc(dbc_f, 1)

            def turned(i):
                c.wait(xt_r)
                load((i + 1) % NCH)
                ch.step(act.activation(xsT[:, half(i), :], xt[:, :, 0:TC], ACT.Copy))
                act.sem_inc(xT_r, 1)

            def body(i, first, last):
                if not last:
                    c.wait(ip_r)
                    c.wait(xcb_f)
                    ch.step(act.activation(xcb[:, :, 3:3 + TC], ip[:, :, 0:TC], ACT.Copy))
                    act.sem_inc(xc_r, 1)
                    act.sem_inc(ip_f, 1)
                if not first:
                    c.wait(db_r)
                    c.wait(dbc_f)
                    ch.step(act.activation(dbc[:, :], db[0:48, 0:TC], ACT.Copy))
                    act.sem_inc(dbs_pe, 1)
                    act.sem_inc(dbs_p, 1)
                if not last:
                    turned(i + 1)
                if not first:
                    c.wait(dt_r)
                    for h in range(2):
                        ch.mark(act.activation(ab[:, h, :], dp[:, h, 0:TC], ACT.Abs, bias=vec[:, 1, h, :]))
                    ch.wait()
                    c.wait(ex_f)
                    ch.step(act.activation(ex[:, :, :], ab[:, :, :], ACT.Exp, scale=-1.0))
                    act.sem_inc(ex_r, 1)
                    ch.step(act.activation(lg[:, :, :], ex[:, :, :], ACT.Ln, bias=1.0))
                    act.sem_inc(ln_r, 1)
                if not last:
                    c.wait(ip_r)
                    c.wait(szq_w, 16)
                    ch.step(act.activation(szq[:, 0:2, :], ip[:, :, 0:TC], ACT.Silu))
                    act.sem_inc(sz_r, 1)
                    act.sem_inc(ip_f, 1)
                    c.wait(cv_r)
                    c.wait(xcs_f)
                    ch.step(act.activation(xcs[:, half(i), :], cv[:, :, :], ACT.Silu))
                    act.sem_inc(xcs_pe, 1)
                    act.sem_inc(xcs_v, 1)

            def turn():
                ch.restart()
                c.turn()

            chunks(act, turned, body, turn)
            act.wait_ge(szq_w, 16)

        @block.gpsimd
        def _(pool):
            c = Counted(pool)
            ch = Chain(pool, pch)
            pool.sem_inc(prt_w, 16)

            def body(i, first, last):
                if first:
                    return
                c.wait(dbs_p)
                c.wait(prt_w, 16)
                ch.step(pool.tensor_copy(parts[:, 0, :], dbc[:, :]))
                ch.step(pool.tensor_tensor(rest[:, 0, :], dbc[:, :], parts[:, 0, :], ALU.subtract))
                pool.sem_inc(dbc_f, 1)
                ch.step(pool.tensor_copy(parts[:, 1, :], rest[:, 0, :]))
                ch.step(pool.tensor_tensor(rest[:, 1, :], rest[:, 0, :], parts[:, 1, :], ALU.subtract))
                ch.step(pool.tensor_copy(parts[:, 2, :], rest[:, 1, :]))
                pool.sem_inc(prt_r, 1)

            def turn():
                ch.restart()
                c.turn()

            chunks(pool, nothing, body, turn)
            pool.wait_ge(prt_w, 32)

        @block.vector
        def _(dve):
            c = Counted(dve)
            ch = Chain(dve, dch)
            dve.wait_ge(wl, 16 * 7)
            ch.step(dve.memset(xcb[:, :, 0:3], 0.0))
            ch.restart()
            dve.sem_inc(xcb_f, 1)
            dve.sem_inc(xcs_f, 2)
            dve.sem_inc(ex_f, 1)
            dve.sem_inc(dtu_w, 16)

            def front(i):
                c.wait(xc_r)
                for h in range(2):
                    ch.mark(dve.tensor_scalar(cv[:, h, :], xcb[:, h, 0:TC], cw[:, h, 0:1], vec[:, 0, h, :], ALU.mult, ALU.add))
                ch.wait()
                for k in range(1, 4):
                    for h in range(2):
                        ch.mark(dve.scalar_tensor_tensor(out=cv[:, h, :], in0=xcb[:, h, k:k + TC], scalar=cw[:, h, k:k + 1],
                                                         in1=cv[:, h, :], op0=ALU.mult, op1=ALU.add))
                    ch.wait()
                dve.sem_inc(cv_r, 1)
                ch.step(dve.tensor_copy(xcb[:, :, 0:3], xcb[:, :, TC:TC + 3]))
                dve.sem_inc(xcb_f, 1)

            def direct(i):
                c.wait(xcs_v)
                c.wait(sz_r)
                for h in range(2):
                    ch.mark(dve.scalar_tensor_tensor(out=szq[:, 2 + h, :], in0=xcs[:, half(i, h, 1), :].rearrange("p a t -> p (a t)"), scalar=vec[:, 2, h, :],
                                                     in1=szq[:, h, :], op0=ALU.mult, op1=ALU.mult))
                ch.wait()
                dve.sem_inc(szq_r, 1)

            def back(i):
                c.wait(ex_r)
                ch.mark(dve.tensor_scalar(small[:, :, :], ex[:, :, :], 2.0 ** -6, None, ALU.is_lt))
                ch.step(dve.tensor_scalar(pl[:, :, :], ex[:, :, :], 1.0 / 3.0, -0.5, ALU.mult, ALU.add))
                ch.step(dve.tensor_tensor(pl[:, :, :], pl[:, :, :], ex[:, :, :], ALU.mult))
                ch.mark(dve.scalar_tensor_tensor(out=pl[:, :, :], in0=pl[:, :, :], scalar=1.0, in1=ex[:, :, :],
                                                 op0=ALU.add, op1=ALU.mult))
                for h in range(2):
                    ch.mark(dve.tensor_scalar(rl[:, h, :], dp[:, h, 0:TC], vec[:, 1, h, :], 0.0, ALU.add, ALU.max))
                ch.wait()
                dve.sem_inc(dp_f, 1)
                c.wait(ln_r)
                ch.step(dve.copy_predicated(lg[:, :, :], small[:, :, :], pl[:, :, :]))
                c.wait(dtu_w, 16)
                ch.step(dve.tensor_tensor(dtu[:, 0:2, :], rl[:, :, :], lg[:, :, :], ALU.add))
                dve.sem_inc(ex_f, 1)
                ch.step(dve.tensor_tensor(dtu[:, 2:4, :], dtu[:, 0:2, :], xcs[:, half(i), :], ALU.mult))
                dve.sem_inc(dtu_r, 1)
                dve.sem_inc(xcs_f, 1)

            def turn():
                ch.restart()
                c.turn()

            def body(i, first, last):
                if not last:
                    front(i)
                if not first:
                    back(i - 1)
                if not last:
                    direct(i)

            chunks(dve, nothing, body, turn)
            dve.wait_ge(dtu_w, 32)


def edges_and_scan(nc, A, K):
    GPC = 8
    RING = 4
    AHEAD = 2
    assert ET == NCH * GPC * GRP and NS == 2 * GPC
    early = 4
    with ExitStack() as ctx:
        ph = Phase(nc, "run", ctx)
        idx = ph.sb("idx", [P, ET + AHEAD * GRP], I32)
        tgt_i = ph.sb("tgt_i", [P, ET], I32)
        tgt = ph.sb("tgt", [P, ET])
        ids = ph.sb("ids", [P, GPC, GRP], I32)
        pay = ph.sb("pay", [P, RING, GRP, ROW])
        tc = ph.sb("tc", [P, 2, GRP, 2 * HEADS])
        trow = ph.sb("trow", [P, 2, GRP * P], I32)
        z = ph.sb("z", [P, GRP, HEADS])
        emax = ph.sb("emax", [P, GRP, HEADS])
        em1 = ph.sb("em1", [P, 1])
        wexp = ph.sb("wexp", [P, 2, GRP, HEADS])
        mask = ph.sb("mask", [P, 2, GRP, P])
        ob = ph.sb("ob", [P, 2, GRP, ROW])
        a_log = ph.sb("a_log", [P, 2, NS])
        a_pos = ph.sb("a_pos", [P, 2, NS])
        a_neg = ph.sb("a_neg", [P, 2, NS])
        wo = ph.sb("wo", [P, 2, D])
        sel32 = ph.sb("sel32", [96, 32])
        sel = ph.sb("sel", [96, 32], BF16)
        dt = ph.sb("dt", [P, 4, TC])
        u = ph.sb("u", [P, 4, TC])
        dbs = ph.sb("dbs", [96, 2, TC], BF16)
        szq = ph.sb("szq", [P, 4, TC])
        da = ph.sb("da", [P, 4, TC])
        dbx = ph.sb("dbx", [P, 2, 2, TC])
        hh = ph.sb("hh", [P, 2, 2, TC])
        hc = ph.sb("hc", [P, 2, 2, 2, TC])
        hs = ph.sb("hs", [P, 4, 2, TC])
        state = ph.sb("state", [P, NS, 2])
        yT = ph.sb("yT", [P, 2, TC])
        yo = ph.sb("yo", [TB, NB, D])
        bc = ph.ps("bc", [P, 4, 512])
        ys = ph.ps("ys", [P, 2, 512])
        ep = ph.ps("ep", [P, 2, 512])
        ix_l, al_l, wo_l, a_r, sel_r, dt_l, u_l, b_l, szq_l = ph.sems("ix_l al_l wo_l a_r sel_r dt_l u_l b_l szq_l")
        in_f, in_c, szq_f, pad_r = ph.sems("in_f in_c szq_f pad_r")
        el = ph.sems("el0 el1")
        gat = ph.sems("gat0 gat1 gat2 gat3")
        el_f, pay_f, d_r, w_r, pm_r, ep_r, ep_f = ph.sems("el_f pay_f d_r w_r pm_r ep_r ep_f")
        ob_w = ph.sems("ob_w0 ob_w1")
        bc_r, bc_f, da_r, da_f, hc_r, hs_r, ys_r, yT_r, yp_r, yo_r, yo_w = ph.sems("bc_r bc_f da_r da_f hc_r hs_r ys_r yT_r yp_r yo_r yo_w")
        em_r, dch, ach, pch = ph.sems("em_r dch ach pch")
        block = ph.block()

        def chunks(eng, body, turn):
            body(0, True)
            turn()
            with eng.Fori(1, NCH) as i:
                body(i, False)
                turn()

        def half(i):
            return bass.ds((i & 1) * 2, 2)

        @block.sync
        def _(sp):
            c = Counted(sp)
            sp.dma_start(idx[:, 0:ET], A["srcT"]).then_inc(ix_l, 16)
            sp.dma_start(tgt_i[:, :], A["dstT"]).then_inc(ix_l, 16)
            sp.dma_start(a_log[:, :, :], A["A_log"].rearrange("(h p) n -> p h n", p=P)).then_inc(al_l, 16)
            sp.dma_start(wo[:, :, :], A["out_wT"].rearrange("(c p) f -> p c f", p=P)).then_inc(wo_l, 16)

            def load_chunk(i):
                sp.dma_start(dbs[:, bass.ds(i & 1, 1), :].rearrange("p a t -> p (a t)"), A["dbs_d"][:, bass.ds(i * TC, TC)]).then_inc(b_l, 16)
                sp.dma_start(dt[:, half(i), :], A["dtu_d"][:, bass.ds(i, 1), 0:2, :].rearrange("p a b t -> p (a b) t")).then_inc(dt_l, 16)
                sp.dma_start(u[:, half(i), :], A["dtu_d"][:, bass.ds(i, 1), 2:4, :].rearrange("p a b t -> p (a b) t")).then_inc(u_l, 16)

            load_chunk(0)

            def body(i, first):
                for g in range(GPC):
                    s = g % 2
                    c.wait(el_f)
                    t0 = i * (GPC * GRP) + g * GRP
                    sp.dma_start(tc[:, s, :, :], rows(A["tc_d"])[:, bass.ds(t0, GRP), :]).then_inc(el[s], 16)
                    sp.dma_start(trow[:, s, :], bass.AP(A["dst"].tensor, 0, [[0, P], [1, EP]])[:, bass.ds(t0 * P, GRP * P)])\
                        .then_inc(el[s], 16)
                    if g == 1:
                        c.wait(in_f)
                        c.wait(in_c, 3)
                        load_chunk(i + 1)
                    if g == 3:
                        c.wait(szq_f)
                        sp.dma_start(szq[:, :, :], A["szq_d"][:, bass.ds(i, 1), :, :].rearrange("p a b t -> p (a b) t")).then_inc(szq_l, 16)

            chunks(sp, body, c.turn)

        @block.gpsimd
        def _(pool):
            c = Counted(pool)
            ch = Chain(pool, pch)
            pool.memset(idx[:, ET:], 0).then_inc(pad_r, 1)
            pool.wait_ge(pad_r, 1)
            pool.wait_ge(ix_l, 32)
            pool.sem_inc(pay_f, RING - AHEAD)

            def gather(g, tiles):
                for k in tiles:
                    pool.indirect_dma_start(pay[:, g % RING, k, :], None, A["table"],
                                            bass.IndirectOffsetOnAxis(ids[:, g % GPC, k:k + 1], 0)).then_inc(gat[g % RING], 16)

            def add_pair(m):
                c.wait(hc_r, 2)
                pool.tensor_tensor(hs[:, m % 4, :, :], hc[:, m % 2, 0, :, :], hc[:, m % 2, 1, :, :], ALU.add).then_inc(hs_r, 1)

            def turn():
                ch.restart()
                c.turn()

            for g in range(AHEAD):
                ch.mark(pool.tensor_copy(ids[:, g, :], idx[:, g * GRP:(g + 1) * GRP]))
            ch.restart()
            for g in range(AHEAD):
                gather(g, range(GRP))

            def body(i, first):
                for g in range(GPC):
                    nxt = g + AHEAD
                    c.wait(pay_f)
                    ch.step(pool.tensor_copy(ids[:, nxt % GPC, :], idx[:, bass.ds(i * (GPC * GRP) + nxt * GRP, GRP)]))
                    gather(nxt, range(early))
                    if g or not first:
                        add_pair((g - 1) % GPC)
                    gather(nxt, range(early, GRP))

            chunks(pool, body, turn)
            add_pair(GPC - 1)
            turn()
            for s in range(RING):
                pool.wait_ge(gat[s], 16 * GRP * len(range(s, NCH * GPC + AHEAD, RING)))
            pool.wait_ge(em_r, 1)
            ch.step(pool.partition_all_reduce(K.top_e[:, :], em1[:, :], P, bass.bass_isa.ReduceOp.max))
            ch.restart()

        @block.tensor
        def _(pe):
            c = Counted(pe)
            pe.wait_ge(wo_l, 16)
            pe.wait_ge(sel_r, 1)
            pe.sem_inc(bc_f, 2)
            pe.sem_inc(ep_f, 2)
            pe.sem_inc(yo_r, 1)

            def broadcast(i, n):
                if n == 0:
                    c.wait(b_l, 16)
                    pe.sem_inc(in_c, 1)
                c.wait(bc_f)
                for j in range(2):
                    r = j * NS + n
                    mm = pe.matmul(bc[:, (n % 2) * 2 + j, 0:TC], sel[:, r:r + 1].to_broadcast([96, P]),
                                   dbs[:, bass.ds(i & 1, 1), :].rearrange("p a t -> p (a t)"), start=True, stop=True)
                mm.then_inc(bc_r, 1)

            def add_states(m):
                if m:
                    c.wait(hs_r)
                if m == 0:
                    c.wait(yo_r)
                for h in range(2):
                    mm = pe.matmul(ys[:, h, 0:TC], K.ident[:, :], hs[:, m % 4, h, :], start=(m == 0), stop=(m == GPC - 1))
                if m == GPC - 1:
                    mm.then_inc(ys_r, 1)

            def sum_tiles(g, tiles):
                if 0 in tiles:
                    c.wait(pm_r)
                for k in tiles:
                    c.wait(ep_f)
                    pe.matmul(ep[:, (g * GRP + k) % 2, 0:ROW], mask[:, g % 2, k, :], pay[:, g % RING, k, :],
                              start=True, stop=True).then_inc(ep_r, 1)

            def out_rows(blocks):
                if 0 in blocks:
                    c.wait(yT_r)
                for j in blocks:
                    for h in range(2):
                        mm = pe.matmul(ys[0:TB, j // 2, (j % 2) * D:(j % 2 + 1) * D], yT[:, h, j * TB:(j + 1) * TB], wo[:, h, :],
                                       start=(h == 0), stop=(h == 1))
                if NB - 1 in blocks:
                    mm.then_inc(yp_r, 1)

            def body(i, first):
                for n in range(NS):
                    g = n // 2
                    if n % 2:
                        sum_tiles(g, range(early // 2))
                    elif n or not first:
                        sum_tiles((g - 1) % GPC, range(early, GRP))
                    if n == 4:
                        c.wait(hs_r)
                    if n + 1 < NS:
                        broadcast(i, n + 1)
                    else:
                        broadcast(i + 1, 0)
                    if n % 2:
                        sum_tiles(g, range(early // 2, early))
                        if n == 1 and not first:
                            add_states(GPC - 1)
                        elif n > 3:
                            add_states((n - 3) // 2)
                    if n == 3 and not first:
                        out_rows(range(NB))
                    if n == 4:
                        add_states(0)

            broadcast(0, 0)
            chunks(pe, body, c.turn)
            add_states(GPC - 1)
            sum_tiles(GPC - 1, range(early, GRP))
            out_rows(range(NB))
            c.turn()

        @block.scalar
        def _(act):
            c = Counted(act)
            ch = Chain(act, ach)
            act.wait_ge(al_l, 16)
            act.activation(a_pos[:, :, :], a_log[:, :, :], ACT.Exp).then_inc(a_r, 1)
            act.wait_ge(a_r, 2)
            act.sem_inc(da_f, 2)
            act.sem_inc(yo_w, 16)
            act.sem_inc(ob_w[0], 16)
            act.sem_inc(ob_w[1], 16)

            def decay(i, n):
                if n == 0:
                    c.wait(dt_l, 16)
                    act.sem_inc(in_c, 1)
                c.wait(da_f)
                for h in range(2):
                    act.activation(da[:, (n % 2) * 2 + h, :], dt[:, bass.ds((i & 1) * 2 + h, 1), :].rearrange("p a t -> p (a t)"),
                                   ACT.Exp, scale=a_neg[:, h, n:n + 1]).then_inc(da_r, 1)

            def weights(g):
                c.wait(d_r)
                act.activation(wexp[:, g % 2, :, :], wexp[:, g % 2, :, :], ACT.Exp).then_inc(w_r, 1)

            def leave(t0, g, tiles):
                if 0 in tiles:
                    c.wait(ob_w[g % 2], 16)
                for k in tiles:
                    c.wait(ep_r)
                    ch.step(act.activation(ob[:, g % 2, k, :], ep[:, (g * GRP + k) % 2, 0:ROW], ACT.Copy))
                    act.sem_inc(ep_f, 1)
                if GRP - 1 in tiles:
                    act.sem_inc(pay_f, 1)
                    act.dma_start(rows(A["agg_d"])[:, bass.ds(t0, GRP), :], ob[:, g % 2, :, :]).then_inc(ob_w[g % 2], 16)

            def leave_rows(i):
                c.wait(yp_r)
                c.wait(yo_w, 16)
                ch.step(act.activation(yo[:, :, :].rearrange("p (a b) d -> p a (b d)", a=2), ys[0:TB, :, :], ACT.Copy))
                act.sem_inc(yo_r, 1)
                act.dma_start(rows(A["ym_d"], TB)[:, bass.ds(i * NB, NB), :], yo[:, :, :]).then_inc(yo_w, 16)

            def turn():
                ch.restart()
                c.turn()

            def body(i, first):
                t0 = i * (GPC * GRP)
                decay(i, 0)
                for n in range(NS):
                    g = n // 2
                    if n % 2 == 0:
                        weights(g)
                    if n + 1 < NS:
                        decay(i, n + 1)
                    if n == 4 and not first:
                        leave_rows(i - 1)
                    if n % 2:
                        leave(t0 + g * GRP, g, range(early))
                    elif n or not first:
                        leave(t0 + (g - 1) * GRP, (g - 1) % GPC, range(early, GRP))

            chunks(act, body, turn)
            c.wait(dt_l, 16)
            leave(ET - GRP, GPC - 1, range(early, GRP))
            leave_rows(NCH - 1)
            turn()
            act.wait_ge(yo_w, 16)
            for s in range(2):
                act.wait_ge(ob_w[s], 16)

        @block.vector
        def _(dve):
            c = Counted(dve)
            ch = Chain(dve, dch)
            dve.wait_ge(a_r, 1)
            dve.tensor_scalar(a_neg[:, :, :], a_pos[:, :, :], -1.0, None, ALU.mult).then_inc(a_r, 1)
            ch.mark(dve.memset(state[:, :, :], 0.0))
            ch.mark(dve.memset(emax[:, :, :], -HUGE))
            ch.step(dve.tensor_tensor(sel32[:, :], K.ident[0:96, 0:32], K.ident[0:96, 32:64], ALU.add))
            ch.step(dve.tensor_tensor(sel[:, :], sel32[:, :], K.ident[0:96, 64:96], ALU.add))
            dve.sem_inc(sel_r, 1)
            dve.wait_ge(ix_l, 32)
            ch.mark(dve.tensor_copy(tgt[:, :], tgt_i[:, :]))
            ch.restart()
            dve.sem_inc(el_f, 2)
            dve.sem_inc(in_f, 1)
            dve.sem_inc(szq_f, 1)

            def arrived(i, g):
                dve.wait_ge(gat[g % RING], i * (2 * GRP * 16) + (g // RING + 1) * GRP * 16)
                c.wait(el[g % 2], 32)

            def weigh(i, g):
                s = g % 2
                c.wait(w_r)
                heads = pay[:, g % RING, :, 0:D].rearrange("p t (h f) -> p t h f", h=HEADS)
                ch.mark(dve.tensor_tensor(heads, heads, wexp[:, s, :, :].unsqueeze(3).to_broadcast([P, GRP, HEADS, FOUT]), ALU.mult))
                ch.mark(dve.tensor_copy(pay[:, g % RING, :, D:ROW], wexp[:, s, :, :]))
                cols = tgt[:, bass.ds(i * (GPC * GRP) + g * GRP, GRP)]
                ch.mark(dve.tensor_tensor(mask[:, s, :, :], trow[:, s, :].rearrange("p (t q) -> p t q", q=P),
                                          cols.unsqueeze(2).to_broadcast([P, GRP, P]), ALU.is_equal))
                return ch.n

            def weighed(n):
                ch.after(n)
                dve.sem_inc(pm_r, 1)
                dve.sem_inc(el_f, 1)

            def keep_and_read(n):
                ch.mark(dve.tensor_copy(state[:, n, :], hh[:, n % 2, :, TC - 1]))
                ch.mark(dve.tensor_tensor(hc[:, n // 2 % 2, n % 2, :, :], hh[:, n % 2, :, :],
                                          bc[:, (n % 2) * 2 + 1, 0:TC].unsqueeze(1).to_broadcast([P, 2, TC]), ALU.mult))
                return ch.n

            def output():
                c.wait(ys_r)
                c.wait(szq_l, 16)
                ch.step(dve.tensor_tensor(yT[:, :, :], ys[:, :, 0:TC], szq[:, 0:2, :], ALU.mult))
                ch.step(dve.tensor_tensor(yT[:, :, :], yT[:, :, :], szq[:, 2:4, :], ALU.add))
                dve.sem_inc(yT_r, 1)
                dve.sem_inc(szq_f, 1)

            def body(i, first):
                scanned = 0
                for n in range(NS):
                    g = n // 2
                    s, q = g % 2, n % 2
                    if q == 0:
                        arrived(i, g)
                        ch.mark(dve.tensor_tensor(z[:, :, :], pay[:, g % RING, :, D:ROW], tc[:, s, :, 0:HEADS], ALU.add))
                        z_at = ch.n
                    if n == 0:
                        c.wait(u_l, 16)
                        dve.sem_inc(in_c, 1)
                    c.wait(bc_r)
                    ch.mark(dve.tensor_tensor(dbx[:, q, :, :], u[:, half(i), :], bc[:, q * 2, 0:TC].unsqueeze(1).to_broadcast([P, 2, TC]), ALU.mult))
                    dbx_at = ch.n
                    if q:
                        weighed(weighed_at)
                    if q == 0:
                        ch.after(z_at)
                        ch.mark(dve.scalar_tensor_tensor(out=z[:, :, :], in0=z[:, :, :], scalar=0.2, in1=z[:, :, :],
                                                         op0=ALU.mult, op1=ALU.max))
                        z_at = ch.n
                    read_at = 0
                    if n or not first:
                        if n:
                            ch.after(scanned)
                            dve.sem_inc(da_f, 1)
                        read_at = keep_and_read((n - 1) % NS)
                    if q == 0:
                        ch.after(z_at)
                        dve.tensor_tensor(wexp[:, s, :, :], z[:, :, :], tc[:, s, :, HEADS:2 * HEADS], ALU.subtract).then_inc(d_r, 1)
                        ch.mark(dve.tensor_tensor(emax[:, :, :], emax[:, :, :], z[:, :, :], ALU.max))
                    c.wait(da_r, 2)
                    for h in range(2):
                        ch.after(dbx_at)
                        ch.mark(dve.tensor_tensor_scan(hh[:, q, h, :], da[:, q * 2 + h, :], dbx[:, q, h, :],
                                                       state[:, n, h:h + 1], ALU.mult, ALU.add))
                        if h == 0 and read_at:
                            ch.after(read_at)
                            dve.sem_inc(bc_f, 1)
                            dve.sem_inc(hc_r, 1)
                    scanned = ch.n
                    if q == 0:
                        weighed_at = weigh(i, g)
                    if n == 2 and not first:
                        output()
                ch.after(scanned)
                dve.sem_inc(da_f, 1)
                dve.sem_inc(in_f, 1)

            def turn():
                ch.restart()
                c.turn()

            chunks(dve, body, turn)
            ch.after(keep_and_read(NS - 1))
            dve.sem_inc(bc_f, 1)
            dve.sem_inc(hc_r, 1)
            output()
            c.wait(u_l, 16)
            c.turn()
            ch.step(dve.tensor_reduce(em1[:, :], emax[:, :, :], AX.XY, ALU.max))
            dve.sem_inc(em_r, 1)
            ch.restart()


def combine_nodes(nc, A, K):
    TOK = GRP * P
    HT = TOK // 2
    HALF = (GRP + 1) // 2
    SPILL = ET // GRP
    assert SPILL <= P
    with ExitStack() as ctx:
        ph = Phase(nc, "com", ctx)
        fi = ph.sb("fi", [SPILL, GRP, 2], I32)
        ff = ph.sb("ff", [SPILL, GRP])
        cont = ph.sb("cont", [SPILL, GRP])
        frow = ph.sb("frow", [SPILL, GRP, ROW])
        first_i = ph.sb("first_i", [SPILL, ET], I32)
        equal = ph.sb("equal", [SPILL, GRP, ET])
        srow = ph.sb("srow", [SPILL, GRP, ROW])
        zrow = ph.sb("zrow", [1, ROW])
        cb = ph.sb("cb", [P, NT, HEADS])
        eps = ph.sb("eps", [P, NT, HEADS])
        vec = ph.sb("vec", [P, 8, D])
        gb = ph.sb("gb", [P, EX])
        f1b = ph.sb("f1b", [P, 4])
        wl = ph.sb("wl", [P, 2, D])
        wg = ph.sb("wg", [P, 2, D])
        w1 = ph.sb("w1", [P, 2, 2 * D])
        w2 = ph.sb("w2", [P, 4, D])
        gw = ph.sb("gw", [P, 2, EX])
        ids = ph.sb("ids", [P, 3, GRP], I32)
        agg = ph.sb("agg", [P, GRP, ROW])
        spl = ph.sb("spl", [P, GRP, ROW])
        yg = ph.sb("yg", [P, GRP, D])
        xn = ph.sb("xn", [P, GRP, D])
        x = ph.sb("x", [P, GRP, D])
        tmp = ph.sb("tmp", [P, GRP, D])
        hl = ph.sb("hl", [P, GRP, D])
        ha = ph.sb("ha", [P, GRP, D])
        gt = ph.sb("gt", [P, GRP, D])
        h = ph.sb("h", [P, GRP, D])
        fo = ph.sb("fo", [P, GRP, D])
        hT = ph.sb("hT", [P, 2, 4, P])
        tT = ph.sb("tT", [P, 2, TOK])
        fT = ph.sb("fT", [P, 4, TOK])
        rec = ph.sb("rec", [P, GRP, HEADS])
        st = ph.sb("st", [P, GRP, 6])
        mva = ph.sb("mva", [P, GRP, 2])
        mvl = ph.sb("mvl", [P, GRP, 2])
        mvb = ph.sb("mvb", [P, GRP, 2])
        rsa = ph.sb("rsa", [P, GRP])
        rsl = ph.sb("rsl", [P, GRP])
        rsb = ph.sb("rsb", [P, GRP])
        lg = ph.sb("lg", [P, GRP, EX])
        m8 = ph.sb("m8", [P, GRP, 8])
        i8 = ph.sb("i8", [P, GRP, 8], mybir.dt.uint32)
        i2 = ph.sb("i2", [P, GRP, 2])
        spp = ph.ps("spp", [P, 2, 512])
        tr = ph.ps("tr", [P, 2, 4, P])
        gp = ph.ps("gp", [P, 2, 512])
        fp = ph.ps("fp", [P, 2, 512])
        cl, vl, wld, ep1, ep2 = ph.sems("cl vl wld ep1 ep2")
        ag, ygs, yg_f, sg, eq_r, sp_r, sp_f, sr_r, sr_w, zr_r = ph.sems("ag ygs yg_f sg eq_r sp_r sp_f sr_r sr_w zr_r")
        xn_l, xn_f, x_l, x_f, g_f, sta, rsa_r, na_r, stl, rsl_r, nl_r, gl_pe, gl_v, stb, rsb_r = ph.sems(
            "xn_l xn_f x_l x_f g_f sta rsa_r na_r stl rsl_r nl_r gl_pe gl_v stb rsb_r")
        mn_r, el_r, tr_r, tr_f, hT_r, gp_r, gp_f, gt_r, h_r, tT_r, fp_r, fp_f, fT_r, fo_r, xm_pe, x1_sp, xm_sp, lg_r = ph.sems(
            "mn_r el_r tr_r tr_f hT_r gp_r gp_f gt_r h_r tT_r fp_r fp_f fT_r fo_r xm_pe x1_sp xm_sp lg_r")
        x1_w, xm_w, dch, ach, pch = ph.sems("x1_w xm_w dch ach pch")
        block = ph.block()
        tiles = range(GRP)

        def passes(eng, first, mid, mix, rest, turn):
            first(0)
            mid(0)
            turn()
            with eng.Fori(0, NG - 1) as g:
                mix(g)
                first(g + 1)
                mid(g + 1)
                rest(g)
                turn()
            mix(NG - 1)
            rest(NG - 1)
            turn()

        def nothing(g):
            pass

        def group(g):
            return bass.ds(g * GRP, GRP)

        @block.sync
        def _(sp):
            c = Counted(sp)
            sp.dma_start(fi[:, :, 0], bass.AP(A["dst"].tensor, 0, [[P, SPILL], [P * SPILL, GRP]]), allow_slow_non_contiguous=True).then_inc(cl, 16)
            sp.dma_start(fi[:, :, 1], bass.AP(A["dprev"].tensor, 0, [[P, SPILL], [P * SPILL, GRP]]), allow_slow_non_contiguous=True).then_inc(cl, 16)
            sp.dma_start(frow[:, :, :], bass.AP(A["agg_d"].tensor, 0, [[P * ROW, SPILL], [P * SPILL * ROW, GRP], [1, ROW]])).then_inc(cl, 16)
            sp.dma_start(first_i[:, :], spread(A["first_d"], ET, SPILL)).then_inc(cl, 16)
            for j, v in enumerate((A["gat_b"], A["lnl_g"], A["lnl_b"], A["lng_g"], A["lng_b"], A["ff2_b"], A["ln2_g"], A["ln2_b"])):
                sp.dma_start(vec[:, j, :], spread(v, D)).then_inc(vl, 16)
            sp.dma_start(gb[:, :], spread(A["gate_b"], EX)).then_inc(vl, 16)
            sp.dma_start(f1b[:, :], A["ff1_b"].rearrange("(m p) -> p m", p=P), allow_slow_non_contiguous=True).then_inc(wld, 16)
            for t, w in ((wl, A["wlT"]), (wg, A["wgT"]), (w1, A["ff1_wT"]), (w2, A["ff2_wT"]), (gw, A["gate_w"])):
                sp.dma_start(t[:, :, :], w.rearrange("(c p) f -> p c f", p=P)).then_inc(wld, 16)

            sp.wait_ge(zr_r, 1)
            sp.dma_start(A["spill_d"][ET:ET + 1, :], zrow[:, :]).then_inc(sr_w, 16)
            sp.wait_ge(sr_r, 1)
            sp.dma_start(A["spill_d"][0:ET, :].rearrange("(a p) d -> p a d", p=SPILL), srow[:, :, :]).then_inc(sr_w, 16)

            def load_xn(g):
                c.wait(xn_f)
                sp.dma_start(xn[:, :, :], rows(A["xn_d"])[:, group(g), :]).then_inc(xn_l, 16)

            def load_x(g):
                c.wait(x_f)
                sp.dma_start(x[:, :, :], rows(A["x"])[:, group(g), :]).then_inc(x_l, 16)

            def store(g):
                c.wait(x1_sp)
                sp.dma_start(rows(A["x1_d"])[:, group(g), :], x[:, :, :]).then_inc(x1_w, 16)
                c.wait(xm_sp)
                sp.dma_start(rows(A["xm_d"])[:, group(g), :], fo[:, :, :]).then_inc(xm_w, 16)

            load_xn(0)
            c.turn()
            with sp.Fori(0, NG - 1) as g:
                load_xn(g + 1)
                load_x(g)
                store(g)
                c.turn()
            load_x(NG - 1)
            store(NG - 1)
            c.turn()

        @block.gpsimd
        def _(pool):
            c = Counted(pool)
            ch = Chain(pool, pch)
            pool.wait_ge(vl, 16 * 9)

            def scaled(t, gain, bias, k0=0, k1=GRP):
                for j, op in ((gain, ALU.mult), (bias, ALU.add)):
                    ch.step(pool.tensor_tensor(t[:, k0:k1, :], t[:, k0:k1, :], vec[:, j, :].unsqueeze(1).to_broadcast([P, k1 - k0, D]), op))

            def gather(j, t, rows_, sem):
                for k in tiles:
                    pool.indirect_dma_start(t[:, k, :], None, rows_, bass.IndirectOffsetOnAxis(ids[:, j, k:k + 1], 0)).then_inc(sem, 16)

            def gather_rows(g):
                c.wait(yg_f)
                ch.step(pool.tensor_copy(ids[:, 0, :], K.rank[:, group(g)]))
                gather(0, yg, A["ym_d"], ygs)

            def gather_sums(g):
                c.wait(g_f)
                ch.mark(pool.tensor_copy(ids[:, 1, :], K.start[:, group(g)]))
                ch.mark(pool.tensor_copy(ids[:, 2, :], K.spill[:, group(g)]))
                ch.wait()
                gather(1, agg, A["agg_d"], ag)
                gather(2, spl, A["spill_d"], sg)

            gather_rows(0)
            ch.restart()
            c.turn()
            pool.wait_ge(sr_w, 32)

            def first(g):
                gather_sums(g)
                c.wait(sta)
                inverse_deviation(pool, ch, K, rsa[:, :], mva[:, :, 1])
                pool.sem_inc(rsa_r, 1)
                c.wait(na_r)
                scaled(ha, 3, 4)
                gather_rows((g + 1) % NG)
                c.wait(stl)
                inverse_deviation(pool, ch, K, rsl[:, :], mvl[:, :, 1])
                pool.sem_inc(rsl_r, 1)
                c.wait(nl_r)
                for k0, k1 in ((0, HALF), (HALF, GRP)):
                    scaled(hl, 1, 2, k0, k1)
                    pool.sem_inc(gl_pe, 1)
                pool.sem_inc(gl_v, 1)

            def rest(g):
                for _ in range(2):
                    c.wait(stb)
                    inverse_deviation(pool, ch, K, rsb[:, :], mvb[:, :, 1])
                    pool.sem_inc(rsb_r, 1)

            def turn():
                ch.restart()
                c.turn()

            passes(pool, first, nothing, nothing, rest, turn)
            pool.wait_ge(ygs, 16 * GRP * (NG + 1))

        @block.tensor
        def _(pe):
            c = Counted(pe)
            pe.wait_ge(wld, 16 * 6)
            pe.sem_inc(tr_f, 2)
            pe.sem_inc(gp_f, 2)
            pe.sem_inc(fp_f, 2)

            pe.wait_ge(eq_r, 1)
            pe.sem_inc(sp_f, 2)
            for a in range(GRP):
                c.wait(sp_f)
                for j in range(GRP):
                    mm = pe.matmul(spp[0:SPILL, a % 2, 0:ROW], equal[:, j, a * SPILL:(a + 1) * SPILL], frow[:, j, :],
                                   start=(j == 0), stop=(j == GRP - 1))
                mm.then_inc(sp_r, 1)
            c.turn()

            def turned(parts, s):
                c.wait(tr_f)
                for j, part in enumerate(parts):
                    t = pe.transpose(tr[:, s, j, :], part, K.ident[:, :])
                t.then_inc(tr_r, 1)

            def both(k):
                turned([t[:, k, j * P:(j + 1) * P] for t in (hl, ha) for j in range(2)], k % 2)

            def gate(g):
                c.wait(gl_pe)
                both(0)
                for k in tiles:
                    if k + 1 < GRP:
                        if k + 1 == HALF:
                            c.wait(gl_pe)
                        both(k + 1)
                    c.wait(hT_r)
                    c.wait(gp_f)
                    for j in range(4):
                        mm = pe.matmul(gp[:, k % 2, 0:D], hT[:, k % 2, j, :], (wl if j < 2 else wg)[:, j % 2, :], start=(j == 0), stop=(j == 3))
                    mm.then_inc(gp_r, 1)

            def forward(g):
                c.wait(h_r)
                for k in tiles:
                    turned([h[:, k, j * P:(j + 1) * P] for j in range(2)], k % 2)
                c.wait(tT_r, GRP)
                for m in range(4):
                    for s in range(2):
                        c.wait(fp_f)
                        for j in range(2):
                            mm = pe.matmul(fp[:, s, 0:HT], w1[:, j, m * P:(m + 1) * P], tT[:, j, s * HT:(s + 1) * HT], start=(j == 0), stop=(j == 1))
                        mm.then_inc(fp_r, 1)
                c.wait(fT_r, 8)
                for k in tiles:
                    c.wait(gp_f)
                    for m in range(4):
                        mm = pe.matmul(gp[:, k % 2, 0:D], fT[:, m, k * P:(k + 1) * P], w2[:, m, :], start=(m == 0), stop=(m == 3))
                    mm.then_inc(gp_r, 1)

            def logits(g):
                c.wait(xm_pe)
                for k in tiles:
                    turned([fo[:, k, j * P:(j + 1) * P] for j in range(2)], k % 2)
                c.wait(tT_r, GRP)
                for k in tiles:
                    for j in range(2):
                        mm = pe.matmul(spp[:, 0, k * EX:(k + 1) * EX], tT[:, j, k * P:(k + 1) * P], gw[:, j, :], start=(j == 0), stop=(j == 1))
                mm.then_inc(lg_r, 1)

            passes(pe, nothing, gate, forward, logits, c.turn)

        @block.scalar
        def _(act):
            c = Counted(act)
            ch = Chain(act, ach)
            act.wait_ge(wld, 16 * 6)
            act.wait_ge(ep1, 1)
            ch.step(act.activation(eps[:, :, :], cb[:, :, :], ACT.Exp))
            act.sem_inc(ep2, 1)
            for a in range(GRP):
                c.wait(sp_r)
                ch.step(act.activation(srow[:, a, :], spp[0:SPILL, a % 2, 0:ROW], ACT.Copy))
                act.sem_inc(sp_f, 1)
            act.sem_inc(sr_r, 1)
            c.turn()

            def elu(g):
                c.wait(mn_r)
                act.activation(tmp[:, :, :], tmp[:, :, :], ACT.Exp).then_inc(el_r, 1)

            def gate(g):
                def leave(k):
                    c.wait(tr_r)
                    ch.step(act.activation(hT[:, k % 2, :, :], tr[:, k % 2, :, :], ACT.Copy))
                    act.sem_inc(tr_f, 1)
                    act.sem_inc(hT_r, 1)

                leave(0)
                for k in tiles:
                    if k + 1 < GRP:
                        leave(k + 1)
                    c.wait(gp_r)
                    ch.step(act.activation(gt[:, k, :], gp[:, k % 2, 0:D], ACT.Sigmoid))
                    act.sem_inc(gp_f, 1)
                act.sem_inc(gt_r, 1)

            def leave_pairs():
                for k in tiles:
                    c.wait(tr_r)
                    ch.step(act.activation(tT[:, :, k * P:(k + 1) * P], tr[:, k % 2, 0:2, :], ACT.Copy))
                    act.sem_inc(tr_f, 1)
                    act.sem_inc(tT_r, 1)

            def forward(g, last=False):
                leave_pairs()
                for m in range(4):
                    for s in range(2):
                        c.wait(fp_r)
                        ch.step(act.activation(fT[:, m, s * HT:(s + 1) * HT], fp[:, s, 0:HT], ACT.Relu, bias=f1b[:, m:m + 1]))
                        act.sem_inc(fp_f, 1)
                        act.sem_inc(fT_r, 1)
                if not last:
                    elu(g + 1)
                for k in tiles:
                    c.wait(gp_r)
                    if k == 0:
                        c.wait(xm_w, 16)
                    ch.step(act.activation(fo[:, k, :], gp[:, k % 2, 0:D], ACT.Copy))
                    act.sem_inc(gp_f, 1)
                act.sem_inc(fo_r, 1)

            def logits(g):
                leave_pairs()

            def turn():
                ch.restart()
                c.turn()

            act.sem_inc(xm_w, 16)
            elu(0)
            gate(0)
            turn()
            with act.Fori(0, NG - 1) as g:
                forward(g)
                gate(g + 1)
                logits(g)
                turn()
            forward(NG - 1, True)
            logits(NG - 1)
            turn()
            act.wait_ge(xm_w, 16)

        @block.vector
        def _(dve):
            c = Counted(dve)
            ch = Chain(dve, dch)
            ch.step(dve.memset(zrow[:, :], 0.0))
            dve.sem_inc(zr_r, 1)
            dve.wait_ge(cl, 64)
            ch.step(dve.tensor_tensor(cont[:, :], fi[:, :, 0], fi[:, :, 1], ALU.is_equal))
            ch.step(dve.tensor_copy(ff[:, :], fi[:, :, 0]))
            ch.step(dve.scalar_tensor_tensor(out=ff[:, :], in0=ff[:, :], scalar=1.0, in1=cont[:, :], op0=ALU.add, op1=ALU.mult))
            ch.step(dve.tensor_scalar(ff[:, :], ff[:, :], -1.0, None, ALU.add))
            for j in range(GRP):
                ch.mark(dve.tensor_scalar(equal[:, j, :], first_i[:, :], ff[:, j:j + 1], None, ALU.is_equal))
            ch.wait()
            dve.sem_inc(eq_r, 1)
            for q in range(HEADS):
                ch.mark(dve.tensor_scalar(cb[:, :, q], K.s_all[:, :, HEADS + q], K.top_src[:, q:q + 1], None, ALU.add))
            ch.wait()
            ch.step(dve.scalar_tensor_tensor(out=cb[:, :, :], in0=cb[:, :, :], scalar=0.2, in1=cb[:, :, :], op0=ALU.mult, op1=ALU.max))
            ch.step(dve.tensor_scalar(cb[:, :, :], cb[:, :, :], -1.0, K.top_e[:, 0:1], ALU.mult, ALU.add))
            ch.step(dve.tensor_scalar(cb[:, :, :], cb[:, :, :], 80.0, None, ALU.min))
            dve.sem_inc(ep1, 1)
            dve.wait_ge(ep2, 1)
            ch.step(dve.tensor_scalar(eps[:, :, :], eps[:, :, :], DEN_EPS, 1e-37, ALU.mult, ALU.max))
            ch.restart()
            dve.wait_ge(vl, 16 * 9)
            dve.sem_inc(xn_f, 1)
            dve.sem_inc(x_f, 1)
            dve.sem_inc(g_f, 1)
            dve.sem_inc(yg_f, 1)

            def row(j):
                return vec[:, j, :].unsqueeze(1).to_broadcast([P, GRP, D])

            def stats(t, mv, sem):
                for k in tiles:
                    ch.mark(dve.bn_stats(st[:, k, :], t[:, k, :]))
                ch.wait()
                for k in tiles:
                    ch.mark(dve.bn_aggr(mv[:, k, :], st[:, k, :]))
                ch.wait()
                dve.sem_inc(sem, 1)

            def normed(out, t, mv, rs):
                for k in tiles:
                    ch.mark(dve.tensor_scalar(out[:, k, :], t[:, k, :], mv[:, k, 0:1], rs[:, k:k + 1], ALU.subtract, ALU.mult))
                ch.wait()

            def first(g):
                c.wait(xn_l, 16)
                dve.wait_ge(ygs, g * (16 * GRP) + 16 * GRP)
                ch.step(dve.tensor_tensor(ha[:, :, :], yg[:, :, :], xn[:, :, :], ALU.add))
                dve.sem_inc(yg_f, 1)
                stats(ha, mva, sta)
                c.wait(rsa_r)
                normed(ha, ha, mva, rsa)
                dve.sem_inc(na_r, 1)
                dve.wait_ge(ag, g * (16 * GRP) + 16 * GRP)

                dve.wait_ge(sg, g * (16 * GRP) + 16 * GRP)
                for k in tiles:
                    ch.mark(dve.scalar_tensor_tensor(out=agg[:, k, :], in0=agg[:, k, :], scalar=K.some[:, bass.ds(g * GRP + k, 1)],
                                                     in1=spl[:, k, :], op0=ALU.mult, op1=ALU.add))
                ch.wait()
                ch.step(dve.tensor_tensor(rec[:, :, :], agg[:, :, D:ROW], eps[:, group(g), :], ALU.add))
                ch.step(dve.reciprocal(rec[:, :, :], rec[:, :, :]))
                ch.step(dve.tensor_tensor(hl[:, :, :].rearrange("p t (q f) -> p t q f", q=HEADS),
                                          agg[:, :, 0:D].rearrange("p t (q f) -> p t q f", q=HEADS),
                                          rec[:, :, :].unsqueeze(3).to_broadcast([P, GRP, HEADS, FOUT]), ALU.mult))
                dve.sem_inc(g_f, 1)
                ch.step(dve.tensor_tensor(hl[:, :, :], hl[:, :, :], xn[:, :, :], ALU.add))
                dve.sem_inc(xn_f, 1)
                ch.step(dve.tensor_tensor(hl[:, :, :], hl[:, :, :], row(0), ALU.add))
                ch.step(dve.tensor_scalar(tmp[:, :, :], hl[:, :, :], 0.0, None, ALU.min))
                dve.sem_inc(mn_r, 1)
                ch.step(dve.tensor_scalar(hl[:, :, :], hl[:, :, :], 0.0, -1.0, ALU.max, ALU.add))
                c.wait(el_r)
                ch.step(dve.tensor_tensor(hl[:, :, :], hl[:, :, :], tmp[:, :, :], ALU.add))
                stats(hl, mvl, stl)
                c.wait(rsl_r)
                normed(hl, hl, mvl, rsl)
                dve.sem_inc(nl_r, 1)

            def mix(g):
                c.wait(gl_v)
                c.wait(gt_r)
                ch.step(dve.tensor_tensor(h[:, :, :], hl[:, :, :], ha[:, :, :], ALU.subtract))
                ch.step(dve.tensor_tensor(h[:, :, :], h[:, :, :], gt[:, :, :], ALU.mult))
                ch.step(dve.tensor_tensor(h[:, :, :], h[:, :, :], ha[:, :, :], ALU.add))
                dve.sem_inc(h_r, 1)

            def rest(g):
                c.wait(fo_r)
                ch.step(dve.tensor_tensor(h[:, :, :], h[:, :, :], fo[:, :, :], ALU.add))
                ch.step(dve.tensor_tensor(h[:, :, :], h[:, :, :], row(5), ALU.add))
                stats(h, mvb, stb)
                c.wait(rsb_r)
                normed(h, h, mvb, rsb)
                ch.step(dve.tensor_tensor(h[:, :, :], h[:, :, :], row(6), ALU.mult))
                ch.step(dve.tensor_tensor(h[:, :, :], h[:, :, :], row(7), ALU.add))
                c.wait(x_l, 16)
                ch.step(dve.tensor_tensor(x[:, :, :], x[:, :, :], h[:, :, :], ALU.add))
                dve.sem_inc(x1_sp, 1)
                stats(x, mvb, stb)
                c.wait(rsb_r)
                normed(fo, x, mvb, rsb)
                dve.sem_inc(xm_pe, 1)
                dve.sem_inc(xm_sp, 1)

            def free_x():
                c.wait(x1_w, 16)
                dve.sem_inc(x_f, 1)

            def take_logits():
                c.wait(lg_r)
                ch.step(dve.tensor_tensor(lg[:, :, :], spp[:, 0, 0:GRP * EX].rearrange("p (t e) -> p t e", e=EX),
                                          gb[:, :].unsqueeze(1).to_broadcast([P, GRP, EX]), ALU.add))

            def choose(g):
                for k in tiles:
                    ch.mark(dve.max(m8[:, k, :], lg[:, k, :]))
                ch.wait()
                for k in tiles:
                    ch.mark(dve.max_index(i8[:, k, :], m8[:, k, :], lg[:, k, :]))
                ch.wait()
                ch.mark(dve.tensor_tensor(K.gap[:, group(g)], m8[:, :, 1], m8[:, :, 0], ALU.subtract))
                ch.step(dve.tensor_copy(i2[:, :, :], i8[:, :, 0:2]))
                ch.step(dve.tensor_tensor(K.hot[:, group(g), :, :], K.iota[:, 0:EX].unsqueeze(1).unsqueeze(1).to_broadcast([P, GRP, 2, EX]),
                                          i2[:, :, :].unsqueeze(3).to_broadcast([P, GRP, 2, EX]), ALU.is_equal))

            def turn():
                ch.restart()
                c.turn()

            first(0)
            turn()
            mix(0)
            first(1)
            rest(0)
            turn()
            with dve.Fori(1, NG - 1) as g:
                mix(g)
                free_x()
                first(g + 1)
                take_logits()
                rest(g)
                choose(g - 1)
                turn()
            mix(NG - 1)
            free_x()
            take_logits()
            rest(NG - 1)
            choose(NG - 2)
            take_logits()
            choose(NG - 1)
            free_x()
            turn()


def dispatch(nc, A, K):
    with ExitStack() as ctx:
        ph = Phase(nc, "dis", ctx)
        xm = ph.sb("xm", [P, NT, D])
        osum = ph.sb("osum", [P, NT, EX])
        tot = ph.sb("tot", [P, NT, EX])
        pos = ph.sb("pos", [P, NT, EX])
        sel = ph.sb("sel", [P, NT, EX])
        two = ph.sb("two", [P, 2, NT])
        inc = ph.sb("inc", [P, EX])
        pad = ph.sb("pad", [P, EX])
        pad_i = ph.sb("pad_i", [P, EX], I32)
        offi = ph.sb("offi", [P, EX])
        one = ph.sb("one", [P, P])
        tj_i = ph.sb("tj_i", [P, MT], I32)
        tj = ph.sb("tj", [P, MT])
        te = ph.sb("te", [P, MT, EX])
        ti = ph.sb("ti", [P, MT])
        e1 = ph.sb("e1", [P, NT])
        wi = ph.ps("wi", [P, 2, 512])
        to = ph.ps("to", [P, 2, 512])
        xl, tj_r, os_r, mm_r, ps_r, ex_r, sc, dch = ph.sems("xl tj_r os_r mm_r ps_r ex_r sc dch")
        block = ph.block()
        halves_ = [(0, 25), (25, NT)]

        @block.sync
        def _(sp):
            sp.dma_start(xm[:, :, :], rows(A["xm_d"])).then_inc(xl, 16)

        @block.gpsimd
        def _(pool):
            pool.iota(tj_i[:, :], pattern=[[EXT, MT]], base=0, channel_multiplier=0).then_inc(tj_r, 1)
            pool.wait_ge(ps_r, 1)
            pool.wait_ge(xl, 16)
            for b in range(NT):
                for q in range(2):
                    pool.indirect_dma_start(A["disp_d"], bass.IndirectOffsetOnAxis(K.pos[:, q, b:b + 1], 0), xm[:, b, :], None).then_inc(sc, 16)
            pool.wait_ge(sc, 16 * 2 * NT)

        @block.tensor
        def _(pe):
            pe.wait_ge(os_r, 1)
            for j, (a, b) in enumerate(halves_):
                pe.matmul(wi[:, j, 0:(b - a) * EX], K.upper[:, :], osum[:, a:b, :].rearrange("p t e -> p (t e)"), start=True, stop=True)
                mm = pe.matmul(to[:, j, 0:(b - a) * EX], K.ones[:, :], osum[:, a:b, :].rearrange("p t e -> p (t e)"), start=True, stop=True)
            mm.then_inc(mm_r, 1)

        @block.scalar
        def _(act):
            act.activation(e1[:, :], K.gap[:, :], ACT.Exp).then_inc(ex_r, 1)

        @block.vector
        def _(dve):
            ch = Chain(dve, dch)
            ch.mark(dve.memset(one[:, :], 1.0))
            ch.step(dve.tensor_tensor(osum[:, :, :], K.hot[:, :, 0, :], K.hot[:, :, 1, :], ALU.add))
            dve.sem_inc(os_r, 1)
            dve.wait_ge(ex_r, 1)
            ch.step(dve.tensor_scalar(K.wts[:, 1, :], e1[:, :], 1.0, None, ALU.add))
            ch.step(dve.reciprocal(K.wts[:, 0, :], K.wts[:, 1, :]))
            ch.step(dve.tensor_tensor(K.wts[:, 1, :], e1[:, :], K.wts[:, 0, :], ALU.mult))
            dve.wait_ge(mm_r, 1)
            for j, (a, b) in enumerate(halves_):
                ch.mark(dve.tensor_copy(tot[:, a:b, :].rearrange("p t e -> p (t e)"), to[:, j, 0:(b - a) * EX]))
            ch.wait()
            for e in range(EX):
                ch.mark(dve.tensor_tensor_scan(pos[:, :, e], one[:, 0:NT], tot[:, :, e], 0.0, ALU.mult, ALU.add))
            ch.wait()
            ch.step(dve.tensor_copy(inc[:, :], pos[:, NT - 1, :]))
            ch.step(dve.tensor_tensor(pos[:, :, :], pos[:, :, :], tot[:, :, :], ALU.subtract))
            for j, (a, b) in enumerate(halves_):
                ch.mark(dve.tensor_tensor(pos[:, a:b, :].rearrange("p t e -> p (t e)"), pos[:, a:b, :].rearrange("p t e -> p (t e)"),
                                     wi[:, j, 0:(b - a) * EX], ALU.add))
            ch.wait()
            ch.step(dve.tensor_scalar(pad[:, :], inc[:, :], float(EXT - 1), None, ALU.add))
            ch.step(dve.tensor_copy(pad_i[:, :], pad[:, :]))
            ch.step(dve.tensor_scalar(pad_i[:, :], pad_i[:, :], 8, 8, ALU.logical_shift_right, ALU.logical_shift_left))
            ch.step(dve.tensor_copy(pad[:, :], pad_i[:, :]))
            ch.step(dve.tensor_tensor_scan(offi[:, :], one[:, 0:EX], pad[:, :], 0.0, ALU.mult, ALU.add))
            ch.step(dve.tensor_tensor(pad[:, :], offi[:, :], pad[:, :], ALU.subtract))
            ch.step(dve.tensor_tensor(pos[:, :, :], pos[:, :, :], pad[:, :].unsqueeze(1).to_broadcast([P, NT, EX]), ALU.add))
            for q in range(2):
                ch.step(dve.tensor_tensor(sel[:, :, :], pos[:, :, :], K.hot[:, :, q, :], ALU.mult))
                ch.step(dve.tensor_reduce(two[:, q, :], sel[:, :, :], AX.X, ALU.add))
            ch.step(dve.tensor_copy(K.pos[:, :, :], two[:, :, :]))
            dve.sem_inc(ps_r, 1)
            dve.wait_ge(tj_r, 1)
            ch.step(dve.tensor_copy(tj[:, :], tj_i[:, :]))
            ch.step(dve.tensor_tensor(te[:, :, :], tj[:, :].unsqueeze(2).to_broadcast([P, MT, EX]),
                                      offi[:, :].unsqueeze(1).to_broadcast([P, MT, EX]), ALU.is_ge))
            ch.step(dve.tensor_reduce(ti[:, :], te[:, :, :], AX.X, ALU.add))
            ch.step(dve.tensor_scalar(ti[:, :], ti[:, :], float(EX - 1), float(P), ALU.min, ALU.mult))
            ch.step(dve.tensor_scalar(ti[:, :], ti[:, :], K.node[:, 0:1], None, ALU.add))
            ch.step(dve.tensor_copy(K.wrow[:, :], ti[:, :]))
            ch.restart()


def experts(nc, A, K):
    KC, FC = D // P, FF // P
    HALVES = EXT // P
    SLOTS, TURN = 4, 4
    assert MT % TURN == 0 and TURN % SLOTS == 0 and TURN % 2 == 0
    with ExitStack() as ctx:
        ph = Phase(nc, "exp", ctx)
        ids = ph.sb("ids", [P, SLOTS], I32)
        xt = ph.sb("xt", [P, SLOTS, HALVES, D])
        w1 = ph.sb("w1", [P, SLOTS, KC * FF])
        w2 = ph.sb("w2", [P, SLOTS, FC * D])
        b1 = ph.sb("b1", [P, SLOTS, FC])
        xT = ph.sb("xT", [P, 2, KC, EXT])
        hT = ph.sb("hT", [P, 2, FC, EXT])
        yo = ph.sb("yo", [P, 2, HALVES, D])
        tr = ph.ps("tr", [P, 2, KC, EXT])
        hp = ph.ps("hp", [P, 2, FC, EXT])
        op = ph.ps("op", [P, 2, HALVES, D])
        xl, wg_, yw = ph.sems("xl0 xl1 xl2 xl3"), ph.sems("wg0 wg1 wg2 wg3"), ph.sems("yw0 yw1")
        x_f, w_f, tr_r, xT_r, hp_r, hT_r, op_r, dch, ach, pch = ph.sems("x_f w_f tr_r xT_r hp_r hT_r op_r dch ach pch")
        block = ph.block()
        w1_rows = A["w1"].rearrange("e (p k) f -> (e p) (k f)", k=KC)
        w2_rows = A["w2"].rearrange("e (p k) d -> (e p) (k d)", k=FC)
        b1_rows = A["b1"].rearrange("e (p k) -> (e p) k", k=FC)

        def tile(ap, i, t):
            return rows(ap)[:, bass.ds((i * TURN + t) * HALVES, HALVES), :]

        @block.sync
        def _(sp):
            c = Counted(sp)
            with sp.Fori(0, MT // TURN) as i:
                for t in range(TURN):
                    c.wait(x_f)
                    sp.dma_start(xt[:, t % SLOTS, :, :], tile(A["disp_d"], i, t)).then_inc(xl[t % SLOTS], 16)
                c.turn()

        @block.gpsimd
        def _(pool):
            c = Counted(pool)
            ch = Chain(pool, pch)
            pool.sem_inc(w_f, SLOTS)
            with pool.Fori(0, MT // TURN) as i:
                for t in range(TURN):
                    s = t % SLOTS
                    c.wait(w_f)
                    ch.step(pool.tensor_copy(ids[:, s:s + 1], K.wrow[:, bass.ds(i * TURN + t, 1)]))
                    for buf, w in ((w1, w1_rows), (b1, b1_rows), (w2, w2_rows)):
                        pool.indirect_dma_start(buf[:, s, :], None, w, bass.IndirectOffsetOnAxis(ids[:, s:s + 1], 0)).then_inc(wg_[s], 16)
                ch.restart()
                c.turn()

        @block.tensor
        def _(pe):
            c = Counted(pe)
            pe.sem_inc(x_f, SLOTS)
            with pe.Fori(0, MT // TURN) as i:
                def turned(t):
                    s = t % SLOTS
                    c.wait(xl[s], 16)
                    for k in range(KC):
                        for a in range(HALVES):
                            tt = pe.transpose(tr[:, t % 2, k, a * P:(a + 1) * P], xt[:, s, a, :].rearrange("p (q k) -> p k q", k=KC)[:, k, :], K.ident[:, :])
                    tt.then_inc(tr_r, 1)

                def up(t):
                    s = t % SLOTS
                    pe.wait_ge(wg_[s], i * (48 * TURN // SLOTS) + 48 * (t // SLOTS + 1))
                    c.wait(xT_r)
                    w = w1[:, s, :].rearrange("p (k q m) -> p k m q", k=KC, m=FC)
                    for m in range(FC):
                        for k in range(KC):
                            mm = pe.matmul(hp[:, t % 2, m, :], w[:, k, m, :], xT[:, t % 2, k, :], start=(k == 0), stop=(k == KC - 1))
                    mm.then_inc(hp_r, 1)

                def down(t):
                    c.wait(hT_r)
                    for a in range(HALVES):
                        for m in range(FC):
                            mm = pe.matmul(op[:, t % 2, a, :], hT[:, t % 2, m, a * P:(a + 1) * P], w2[:, t % SLOTS, m * D:(m + 1) * D], start=(m == 0), stop=(m == FC - 1))
                    mm.then_inc(op_r, 1)

                turned(0)
                for t in range(TURN):
                    if t + 1 < TURN:
                        turned(t + 1)
                    up(t)
                    if t:
                        down(t - 1)
                down(TURN - 1)
                c.turn()

        @block.scalar
        def _(act):
            c = Counted(act)
            ch = Chain(act, ach)
            for q in range(2):
                act.sem_inc(yw[q], 16)
            with act.Fori(0, MT // TURN) as i:
                def relu(t):
                    c.wait(hp_r)
                    for m in range(FC):
                        ch.mark(act.activation(hT[:, t % 2, m, :], hp[:, t % 2, m, :], ACT.Relu, bias=b1[:, t % SLOTS, m:m + 1]))
                    ch.wait()
                    act.sem_inc(hT_r, 1)

                def leave(t):
                    c.wait(op_r)
                    act.sem_inc(w_f, 1)
                    c.wait(yw[t % 2], 16)
                    ch.step(act.activation(yo[:, t % 2, :, :], op[:, t % 2, :, :], ACT.Copy))
                    act.dma_start(tile(A["eout_d"], i, t), yo[:, t % 2, :, :]).then_inc(yw[t % 2], 16)

                for t in range(TURN):
                    relu(t)
                    if t:
                        leave(t - 1)
                leave(TURN - 1)
                ch.restart()
                c.turn()
            for q in range(2):
                act.wait_ge(yw[q], 16)

        @block.vector
        def _(dve):
            c = Counted(dve)
            ch = Chain(dve, dch)
            with dve.Fori(0, MT // TURN) as i:
                for t in range(TURN):
                    c.wait(tr_r)
                    ch.step(dve.tensor_copy(xT[:, t % 2, :, :], tr[:, t % 2, :, :]))
                    dve.sem_inc(xT_r, 1)
                    dve.sem_inc(x_f, 1)
                ch.restart()
                c.turn()


def finish(nc, A, K):
    with ExitStack() as ctx:
        ph = Phase(nc, "fin", ctx)
        ids = ph.sb("ids", [P, 2, 2, GRP], I32)
        e = ph.sb("e", [P, 2, 2, GRP, D])
        xm = ph.sb("xm", [P, 2, GRP, D])
        x1 = ph.sb("x1", [P, 2, GRP, D])
        g = ph.sb("g", [P, NT, EX])
        g1 = ph.sb("g1", [P, NT, EX])
        gs = ph.sb("gs", [P, GRP, EX])
        gT = ph.sb("gT", [EX, 2, P])
        b2 = ph.sb("b2", [EX, D])
        vec = ph.sb("vec", [P, 2, D])
        y = ph.sb("y", [P, 2, GRP, D])
        st = ph.sb("st", [P, GRP, 6])
        mv = ph.sb("mv", [P, GRP, 2])
        rs = ph.sb("rs", [P, GRP])
        tp = ph.ps("tp", [EX, 2, 512])
        bp = ph.ps("bp", [P, 2, 512])
        cl, in_f, e_f = ph.sems("cl in_f e_f")
        eg, xm_l, x1_l, y_w = (ph.sems(f"{n}0 {n}1") for n in ("eg", "xm_l", "x1_l", "y_w"))
        g_r, gs_r, tp_r, gT_r, bp_r, bp_f, st_r, rs_r, y_r, dch, pch = ph.sems("g_r gs_r tp_r gT_r bp_r bp_f st_r rs_r y_r dch pch")
        block = ph.block()
        tiles = range(GRP)

        def groups(eng, body, turn):
            with eng.Fori(0, NG // 2) as j:
                body(j * 2, 0, False)
                body(j * 2 + 1, 1, False)
                turn()
            body(NG - 1, 0, True)
            turn()

        @block.sync
        def _(sp):
            c = Counted(sp)
            sp.dma_start(b2[:, :], A["b2"]).then_inc(cl, 16)
            for j, v in enumerate((A["gamma"], A["beta"])):
                sp.dma_start(vec[:, j, :], spread(v, D)).then_inc(cl, 16)

            def load(i, p):
                sp.dma_start(xm[:, p, :, :], rows(A["xm_d"])[:, bass.ds(i * GRP, GRP), :]).then_inc(xm_l[p], 16)
                sp.dma_start(x1[:, p, :, :], rows(A["x1_d"])[:, bass.ds(i * GRP, GRP), :]).then_inc(x1_l[p], 16)

            load(0, 0)

            def body(i, p, last):
                if not last:
                    c.wait(in_f)
                    load(i + 1, 1 - p)
                c.wait(y_r)
                if not last:
                    sp.dma_start(rows(A["out"][0:(NT - 1) * P, :])[:, bass.ds(i * GRP, GRP), :], y[:, p, :, :]).then_inc(y_w[p], 16)

            groups(sp, body, c.turn)
            t0 = (NG - 1) * GRP
            sp.dma_start(rows(A["out"][t0 * P:(NT - 1) * P, :]), y[:, 0, 0:GRP - 1, :]).then_inc(y_w[0], 16)
            sp.dma_start(A["out"][(NT - 1) * P:N, :], y[0:NLAST, 0, GRP - 1, :]).then_inc(y_w[0], 16)

        @block.gpsimd
        def _(pool):
            c = Counted(pool)
            ch = Chain(pool, pch)

            def gather(p, q):
                for k in tiles:
                    pool.indirect_dma_start(e[:, p, q, k, :], None, A["eout_d"],
                                            bass.IndirectOffsetOnAxis(ids[:, p, q, k:k + 1], 0)).then_inc(eg[p], 16)

            def turn():
                ch.restart()
                c.turn()

            ch.mark(pool.tensor_copy(ids[:, 0, :, :], K.pos[:, :, 0:GRP]))
            ch.restart()
            gather(0, 0)
            gather(0, 1)

            def body(i, p, last):
                if not last:
                    c.wait(e_f)
                    ch.step(pool.tensor_copy(ids[:, 1 - p, :, :], K.pos[:, :, bass.ds((i + 1) * GRP, GRP)]))
                    gather(1 - p, 0)
                c.wait(st_r)
                inverse_deviation(pool, ch, K, rs[:, :], mv[:, :, 1])
                pool.sem_inc(rs_r, 1)
                if not last:
                    gather(1 - p, 1)

            groups(pool, body, turn)

        @block.tensor
        def _(pe):
            c = Counted(pe)
            pe.wait_ge(cl, 48)
            pe.sem_inc(bp_f, 2)

            def body(i, p, last):
                c.wait(gs_r)

                def turned(k):
                    pe.transpose(tp[:, k % 2, 0:P], gs[:, k, :], K.ident[:, :]).then_inc(tp_r, 1)

                turned(0)
                for k in tiles:
                    if k + 1 < GRP:
                        turned(k + 1)
                    c.wait(gT_r)
                    if k != 1:
                        c.wait(bp_f, 2 if k == 0 else 1)
                    pe.matmul(bp[:, k % 2, 0:D], gT[:, k % 2, :], b2[:, :], start=True, stop=True).then_inc(bp_r, 1)

            groups(pe, body, c.turn)

        @block.scalar
        def _(act):
            c = Counted(act)
            act.wait_ge(g_r, 1)

            def body(i, p, last):
                act.activation(gs[:, :, :], g[:, bass.ds(i * GRP, GRP), :], ACT.Copy).then_inc(gs_r, 1)
                for k in tiles:
                    c.wait(tp_r)
                    act.activation(gT[:, k % 2, :], tp[:, k % 2, 0:P], ACT.Copy).then_inc(gT_r, 1)

            groups(act, body, c.turn)

        @block.vector
        def _(dve):
            c = Counted(dve)
            ch = Chain(dve, dch)
            for q, t in ((0, g), (1, g1)):
                ch.mark(dve.tensor_tensor(t[:, :, :], K.hot[:, :, q, :], K.wts[:, q, :].unsqueeze(2).to_broadcast([P, NT, EX]), ALU.mult))
            ch.wait()
            ch.step(dve.tensor_tensor(g[:, :, :], g[:, :, :], g1[:, :, :], ALU.add))
            dve.sem_inc(g_r, 1)
            ch.restart()
            dve.wait_ge(cl, 48)
            dve.sem_inc(in_f, 1)
            dve.sem_inc(e_f, 1)
            for p in range(2):
                dve.sem_inc(y_w[p], 16)

            def turn():
                ch.restart()
                c.turn()

            def body(i, p, last):
                yp = y[:, p, :, :]
                c.wait(y_w[p], 16)
                c.wait(xm_l[p], 16)
                for k in tiles:
                    c.wait(bp_r)
                    ch.step(dve.tensor_tensor(y[:, p, k, :], bp[:, k % 2, 0:D], xm[:, p, k, :], ALU.add))
                    dve.sem_inc(bp_f, 1)
                dve.wait_ge(eg[p], (i - p) * (16 * GRP) + 2 * 16 * GRP)
                for q in range(2):
                    for k in tiles:
                        ch.mark(dve.scalar_tensor_tensor(out=y[:, p, k, :], in0=e[:, p, q, k, :], scalar=K.wts[:, q, bass.ds(i * GRP + k, 1)],
                                                         in1=y[:, p, k, :], op0=ALU.mult, op1=ALU.add))
                    ch.wait()
                dve.sem_inc(e_f, 1)
                for k in tiles:
                    ch.mark(dve.bn_stats(st[:, k, :], y[:, p, k, :]))
                ch.wait()
                for k in tiles:
                    ch.mark(dve.bn_aggr(mv[:, k, :], st[:, k, :]))
                ch.wait()
                dve.sem_inc(st_r, 1)
                c.wait(rs_r)
                for k in tiles:
                    ch.mark(dve.tensor_scalar(y[:, p, k, :], y[:, p, k, :], mv[:, k, 0:1], rs[:, k:k + 1], ALU.subtract, ALU.mult))
                ch.wait()
                for j, op in ((0, ALU.mult), (1, ALU.add)):
                    ch.step(dve.tensor_tensor(yp, yp, vec[:, j, :].unsqueeze(1).to_broadcast([P, GRP, D]), op))
                c.wait(x1_l[p], 16)
                ch.step(dve.tensor_tensor(yp, yp, x1[:, p, :, :], ALU.add))
                dve.sem_inc(y_r, 1)
                dve.sem_inc(in_f, 1)

            groups(dve, body, turn)
            dve.wait_ge(y_w[0], 32)
            dve.wait_ge(y_w[1], 16)


_INS = {
    "x": ((NP, D), F32), "src": ((EP,), I32), "dst": ((EP,), I32), "dprev": ((EP,), I32), "srcT": ((P, ET), I32), "dstT": ((P, ET), I32), "noise": ((P, NT), F32),
    "gat_w": ((D, D), F32), "gat_wT": ((D, D), F32), "a_src": ((HEADS, FOUT), F32), "a_tgt": ((HEADS, FOUT), F32),
    "gat_b": ((D,), F32), "lnl_g": ((D,), F32), "lnl_b": ((D,), F32), "lng_g": ((D,), F32), "lng_b": ((D,), F32),
    "ln2_g": ((D,), F32), "ln2_b": ((D,), F32), "in_wT": ((D, 2 * D), F32), "conv_w": ((D, 4), F32),
    "conv_b": ((D,), F32), "xp_wT": ((D, 48), F32), "dt_wT": ((NR, D), F32), "dt_b": ((D,), F32),
    "A_log": ((D, NS), F32), "Dp": ((D,), F32), "out_wT": ((D, D), F32), "wlT": ((D, D), F32), "wgT": ((D, D), F32),
    "ff1_wT": ((D, 2 * D), F32), "ff1_b": ((2 * D,), F32), "ff2_wT": ((2 * D, D), F32), "ff2_b": ((D,), F32),
    "gate_w": ((D, EX), F32), "gate_b": ((EX,), F32), "w1": ((EX, D, FF), F32), "b1": ((EX, FF), F32),
    "w2": ((EX, FF, D), F32), "b2": ((EX, D), F32), "gamma": ((D,), F32), "beta": ((D,), F32),
}

_SCRATCH = {
    "xn_d": ((NP, D), F32), "table": ((NP, ROW), F32), "stgt_d": ((NP, HEADS), F32),
    "keys_d": ((2, NP), F32), "rank_d": ((NP,), I32), "first_d": ((ET,), I32), "v_d": ((EP, HEADS), F32),
    "tc_d": ((EP, 2 * HEADS), F32), "xs_d": ((NP, D), F32), "dbs_d": ((96, NP + TC), BF16),
    "dtu_d": ((P, NCH + 1, 4, TC), F32), "szq_d": ((P, NCH, 4, TC), F32), "agg_d": ((EP, ROW), F32),
    "spill_d": ((ET + 1, ROW), F32), "ym_d": ((NP, D), F32), "x1_d": ((NP, D), F32), "xm_d": ((NP, D), F32),
    "disp_d": ((MT * EXT, D), F32), "eout_d": ((MT * EXT, D), F32),
}


class Shared:
    pass


def gnn_ffn_kernel(nc, ins, out, debug=(), upto=99):
    Phase.used = []
    scratch = {}
    for name, (shape, dt) in _SCRATCH.items():
        kind = "ExternalOutput" if name in debug else "Internal"
        scratch[name] = nc.dram_tensor(name, shape, dt, kind=kind).ap()
    A = dict(ins, out=out, **scratch)
    with ExitStack() as ctx:
        def keep(name, shape, dt=F32):
            return ctx.enter_context(nc.sbuf_tensor("k_" + name, shape, dt))

        K = Shared()
        K.ident = keep("ident", [P, P])
        K.upper = keep("upper", [P, P])
        K.ones = keep("ones", [P, P])
        K.iota = keep("iota", [P, P])
        K.nhalf = keep("nhalf", [P, 16])
        K.iota_i = keep("iota_i", [P, P], I32)
        K.node = keep("node", [P, NT])
        K.node_i = keep("node_i", [P, NT], I32)
        K.s_all = keep("s_all", [P, NT, 2 * HEADS])
        K.rank = keep("rank", [P, NT], I32)
        K.start = keep("start", [P, NT], I32)
        K.some = keep("some", [P, NT])
        K.below = keep("below", [P, NT])
        K.same = keep("same", [P, NT])
        K.deg = keep("deg", [P, NT])
        K.spill = keep("spill", [P, NT], I32)
        K.top_src = keep("top_src", [P, HEADS])
        K.top_e = keep("top_e", [P, 1])
        K.gap = keep("gap", [P, NT])
        K.hot = keep("hot", [P, NT, 2, EX])
        K.wts = keep("wts", [P, 2, NT])
        K.pos = keep("pos", [P, 2, NT], I32)
        K.wrow = keep("wrow", [P, MT], I32)
        phases = [constants, project, order, spread_scores, mamba_in, edges_and_scan,
                  combine_nodes, dispatch, experts, finish]
        for n, phase in enumerate(phases):
            if n <= upto:
                phase(nc, A, K)
                if phase in (order, edges_and_scan):
                    clear_semaphores(nc)


def kernel(**inputs):
    import numpy as np
    import concourse.bacc as _bacc
    from concourse.bass_utils import run_bass_kernel_spmd as _run

    nc = _bacc.Bacc("TRN2", target_bir_lowering=False, num_devices=1)
    arrays = layout(inputs)
    ins = {n: nc.dram_tensor("in_" + n, s, t, kind="ExternalInput").ap() for n, (s, t) in _INS.items()}
    out = nc.dram_tensor("out", (N, D), F32, kind="ExternalOutput").ap()
    gnn_ffn_kernel(nc, ins, out)
    r = _run(nc, [arrays], core_ids=[0])
    return np.asarray(r.results[0]["out"])


def layout(inputs):
    import numpy as np

    v = {k.replace("L0_gnn_", "").replace("L0_ffn_", ""): np.asarray(a) for k, a in inputs.items()}
    tail = np.full(EP - E, NP - 1, np.int32)
    noise = np.concatenate([v["node_vec"], np.zeros(NP - N, np.float32)])
    dst = np.concatenate([v["dst"], tail])
    a = {
        "srcT": np.concatenate([v["src"], tail]).reshape(ET, P).T, "dstT": dst.reshape(ET, P).T,
        "x": np.concatenate([v["x"], np.zeros((NP - N, D), np.float32)]),
        "src": np.concatenate([v["src"], tail]),
        "dst": dst, "dprev": np.concatenate([np.full(1, -1, np.int32), v["dst"], tail])[:EP],
        "noise": noise.reshape(NT, P).T, "gat_w": v["gat_w"], "gat_wT": v["gat_w"].T,
        "a_src": v["gat_a_src"], "a_tgt": v["gat_a_tgt"], "gat_b": v["gat_b"],
        "lnl_g": v["ln_local_g"], "lnl_b": v["ln_local_b"], "lng_g": v["ln_global_g"], "lng_b": v["ln_global_b"],
        "ln2_g": v["ln2_g"], "ln2_b": v["ln2_b"], "in_wT": v["in_proj_w"].T, "conv_w": v["conv_w"],
        "conv_b": v["conv_b"], "xp_wT": v["x_proj_w"].T, "dt_wT": v["dt_proj_w"].T, "dt_b": v["dt_proj_b"],
        "A_log": v["A_log"], "Dp": v["D_param"], "out_wT": v["out_proj_w"].T, "wlT": v["wl"].T, "wgT": v["wg"].T,
        "ff1_wT": v["ff1_w"].T, "ff1_b": v["ff1_b"], "ff2_wT": v["ff2_w"].T, "ff2_b": v["ff2_b"],
        "gate_w": v["gate_w"], "gate_b": v["gate_b"], "w1": v["w1"], "b1": v["b1"], "w2": v["w2"], "b2": v["b2"],
        "gamma": v["gamma"], "beta": v["beta"],
    }
    return {"in_" + n: np.ascontiguousarray(x) for n, x in a.items()}
```
